# Optimizing a Trainium2 kernel written in Bass

```python
import numpy as np
import jax
import jax.numpy as jnp

def _softmax(x, axis=-1):
    return jax.nn.softmax(x, axis=axis)

def _gelu(x):
    return jax.nn.gelu(x, approximate=True)

def _silu(x):
    return jax.nn.silu(x)

def _sigmoid(x):
    return jax.nn.sigmoid(x)

def _layernorm(x, axis=-1, eps=1e-05):
    m = jnp.mean(x, axis=axis, keepdims=True)
    v = jnp.var(x, axis=axis, keepdims=True)
    return (x - m) / jnp.sqrt(v + eps)

def _scatter_add(tgt, idx, src, axis=0):
    return tgt.at[idx].add(src)

def _segment_sum(src, seg, n):
    return jax.ops.segment_sum(src, seg, n)
kernel_name = 'mk_cond_seq_d4_seqx_r4_68aaa9'

def setup_inputs(seed: int=0):
    np.random.seed(seed)
    _w = jnp.asarray

    def _rec_inputs():
        import jax
        import jax.numpy as jnp
        _rk = jax.random.key(seed)
        x = -0.000125 + 0.9999 * jax.random.normal(jax.random.fold_in(_rk, 1), (16, 256, 256), jnp.float32)
        _lenS = 256 - jax.random.randint(jax.random.fold_in(_rk, 7), (16,), 0, max(1, 256 // 4) + 1, jnp.int32)
        _lenS2 = 256 - jax.random.randint(jax.random.fold_in(_rk, 8), (16,), 0, max(1, 256 // 4) + 1, jnp.int32)
        cond_256 = 0.0061147 + 1.02565 * jax.random.normal(jax.random.fold_in(_rk, 11), (16, 64), jnp.float32)
        fside_BxS_0 = -0.00265932 + 1.00408 * jax.random.normal(jax.random.fold_in(_rk, 12), (16, 256), jnp.float32)
        return (x, cond_256, fside_BxS_0)
    x, cond_256, fside_BxS_0 = _rec_inputs()

    def _L0_cond_setup():
        import jax, jax.numpy as jnp
        import numpy as np
        DIM = 256
        BN = 128
        H = 64
        DELTA_SCALE = 0.1
        key = jax.random.key(seed)
        ks = jax.random.split(key, 10)
        B, L = (16, 512)

        def init(k, shape, fan_in):
            bound = 1.0 / np.sqrt(fan_in)
            return jax.random.uniform(k, shape, jnp.float32, -bound, bound)
        return {'x': jax.random.normal(ks[0], (B, L, DIM), jnp.float32), 'h_lang': jax.random.normal(ks[1], (B, H), jnp.float32), 'Wd': init(ks[2], (BN, DIM), DIM), 'bd': init(ks[3], (BN,), DIM), 'Wu': init(ks[4], (DIM, BN), BN), 'bu': init(ks[5], (DIM,), BN), 'Wdd': init(ks[6], (BN * DIM, H), H), 'bdd': init(ks[7], (BN * DIM,), H), 'Wdu': init(ks[8], (DIM * BN, H), H), 'bdu': init(ks[9], (DIM * BN,), H)}
    _L0_cond_all = _L0_cond_setup()
    _L0_cond_in = {k: v for k, v in _L0_cond_all.items() if k in ('Wd', 'bd', 'Wu', 'bu', 'Wdd', 'bdd', 'Wdu', 'bdu')}
    del _L0_cond_all

    def _L1_cond_setup():
        import jax, jax.numpy as jnp
        import numpy as np
        EPS = 1e-05
        key = jax.random.key(seed)
        k1, k2, k3, k4 = jax.random.split(key, 4)
        b, t, d, num_con = (8, 1024, 256, 64)
        return {'input': jax.random.normal(k1, (b, t, d), dtype=jnp.float32), 'convInfo': jax.random.normal(k2, (b, num_con), dtype=jnp.float32), 'weight': jnp.ones((d,), dtype=jnp.float32), 'bias': jnp.zeros((d,), dtype=jnp.float32), 'lin_w': jax.random.normal(k3, (d, num_con), dtype=jnp.float32) * (1.0 / np.sqrt(num_con)), 'lin_b': jax.random.normal(k4, (d,), dtype=jnp.float32) * 0.01}
    _L1_cond_all = _L1_cond_setup()
    _L1_cond_in = {k: v for k, v in _L1_cond_all.items() if k in ('weight', 'bias', 'lin_w', 'lin_b')}
    del _L1_cond_all

    def _L2_cond_setup():
        import jax, jax.numpy as jnp
        import numpy as np
        import math
        H = 256
        NH = 16
        DH = H // NH
        EPS = 1e-05

        def _layernorm(x):
            m = jnp.mean(x, axis=-1, keepdims=True)
            v = jnp.mean((x - m) ** 2, axis=-1, keepdims=True)
            return (x - m) / jnp.sqrt(v + EPS)

        def _gelu_tanh(x):
            c = math.sqrt(2.0 / math.pi)
            return 0.5 * x * (1.0 + jnp.tanh(c * (x + 0.044715 * x ** 3)))
        key = jax.random.key(seed)
        ks = jax.random.split(key, 12)
        B, P = (16, 256)
        s = 0.02
        inp = {'x': jax.random.normal(ks[0], (B, P, H), jnp.float32), 't_embd': jax.random.normal(ks[1], (B, 64), jnp.float32), 'c_embd': jax.random.normal(ks[2], (B, H), jnp.float32), 'W_t1': jax.random.normal(ks[3], (H, 64), jnp.float32) * s, 'b_t1': jnp.zeros((H,), jnp.float32), 'W_t2': jax.random.normal(ks[4], (H, H), jnp.float32) * s, 'b_t2': jnp.zeros((H,), jnp.float32), 'W_c': jax.random.normal(ks[5], (6 * H, H), jnp.float32) * s, 'b_c': jnp.zeros((6 * H,), jnp.float32), 'W_qkv': jax.random.normal(ks[6], (3 * H, H), jnp.float32) * s, 'b_qkv': jnp.zeros((3 * H,), jnp.float32), 'W_o': jax.random.normal(ks[7], (H, H), jnp.float32) * s, 'b_o': jnp.zeros((H,), jnp.float32), 'W_f1': jax.random.normal(ks[8], (4 * H, H), jnp.float32) * s, 'b_f1': jnp.zeros((4 * H,), jnp.float32), 'W_f2': jax.random.normal(ks[9], (H, 4 * H), jnp.float32) * s, 'b_f2': jnp.zeros((H,), jnp.float32)}
        return inp
    _L2_cond_all = _L2_cond_setup()
    _L2_cond_in = {k: v for k, v in _L2_cond_all.items() if k in ('W_t1', 'b_t1', 'W_t2', 'b_t2', 'W_c', 'b_c', 'W_qkv', 'b_qkv', 'W_o', 'b_o', 'W_f1', 'b_f1', 'W_f2', 'b_f2')}
    del _L2_cond_all

    def _L3_cond_setup():
        import jax, jax.numpy as jnp
        import numpy as np
        EPS = 1e-06

        def act_quant(x):
            scale = 127.0 / jnp.clip(jnp.max(jnp.abs(x), axis=-1, keepdims=True), 1e-05, None)
            return jnp.clip(jnp.round(x * scale), -128.0, 127.0) / scale

        def weight_quant(w):
            scale = 1.0 / jnp.clip(jnp.mean(jnp.abs(w)), 1e-05, None)
            return jnp.clip(jnp.round(w * scale), -1.0, 1.0) / scale
        key = jax.random.key(seed)
        k0, k1, k2, k3, k4 = jax.random.split(key, 5)
        B, S, D, FF, C = (4, 1024, 256, 1024, 64)
        return {'x': jax.random.normal(k0, (B, S, D), jnp.float32), 'cond': jax.random.normal(k1, (B, C), jnp.float32), 'norm_w': jax.random.normal(k2, (D, C), jnp.float32) * 0.02, 'up_w': jax.random.normal(k3, (2 * FF, D), jnp.float32) * 0.02, 'down_w': jax.random.normal(k4, (D, FF), jnp.float32) * 0.02}
    _L3_cond_all = _L3_cond_setup()
    _L3_cond_in = {k: v for k, v in _L3_cond_all.items() if k in ('norm_w', 'up_w', 'down_w')}
    del _L3_cond_all
    return {'x': x, 'cond_256': cond_256, 'fside_BxS_0': fside_BxS_0, 'L0_cond_Wd': _L0_cond_in['Wd'], 'L0_cond_bd': _L0_cond_in['bd'], 'L0_cond_Wu': _L0_cond_in['Wu'], 'L0_cond_bu': _L0_cond_in['bu'], 'L0_cond_Wdd': _L0_cond_in['Wdd'], 'L0_cond_bdd': _L0_cond_in['bdd'], 'L0_cond_Wdu': _L0_cond_in['Wdu'], 'L0_cond_bdu': _L0_cond_in['bdu'], 'L1_cond_weight': _L1_cond_in['weight'], 'L1_cond_bias': _L1_cond_in['bias'], 'L1_cond_lin_w': _L1_cond_in['lin_w'], 'L1_cond_lin_b': _L1_cond_in['lin_b'], 'L2_cond_W_t1': _L2_cond_in['W_t1'], 'L2_cond_b_t1': _L2_cond_in['b_t1'], 'L2_cond_W_t2': _L2_cond_in['W_t2'], 'L2_cond_b_t2': _L2_cond_in['b_t2'], 'L2_cond_W_c': _L2_cond_in['W_c'], 'L2_cond_b_c': _L2_cond_in['b_c'], 'L2_cond_W_qkv': _L2_cond_in['W_qkv'], 'L2_cond_b_qkv': _L2_cond_in['b_qkv'], 'L2_cond_W_o': _L2_cond_in['W_o'], 'L2_cond_b_o': _L2_cond_in['b_o'], 'L2_cond_W_f1': _L2_cond_in['W_f1'], 'L2_cond_b_f1': _L2_cond_in['b_f1'], 'L2_cond_W_f2': _L2_cond_in['W_f2'], 'L2_cond_b_f2': _L2_cond_in['b_f2'], 'L3_cond_norm_w': _L3_cond_in['norm_w'], 'L3_cond_up_w': _L3_cond_in['up_w'], 'L3_cond_down_w': _L3_cond_in['down_w']}

def reference(x, cond_256, fside_BxS_0, L0_cond_Wd, L0_cond_bd, L0_cond_Wu, L0_cond_bu, L0_cond_Wdd, L0_cond_bdd, L0_cond_Wdu, L0_cond_bdu, L1_cond_weight, L1_cond_bias, L1_cond_lin_w, L1_cond_lin_b, L2_cond_W_t1, L2_cond_b_t1, L2_cond_W_t2, L2_cond_b_t2, L2_cond_W_c, L2_cond_b_c, L2_cond_W_qkv, L2_cond_b_qkv, L2_cond_W_o, L2_cond_b_o, L2_cond_W_f1, L2_cond_b_f1, L2_cond_W_f2, L2_cond_b_f2, L3_cond_norm_w, L3_cond_up_w, L3_cond_down_w):
    import jax
    import jax.numpy as jnp

    def _L0_cond_ref(x, h_lang, Wd, bd, Wu, bu, Wdd, bdd, Wdu, bdu):
        import jax, jax.numpy as jnp
        import numpy as np
        DIM = 256
        BN = 128
        H = 64
        DELTA_SCALE = 0.1
        B, L, D = x.shape
        dWd = ((h_lang @ Wdd.T + bdd) * DELTA_SCALE).reshape(B, BN, D)
        dWu = ((h_lang @ Wdu.T + bdu) * DELTA_SCALE).reshape(B, D, BN)
        Wd_b = Wd + dWd
        Wu_b = Wu + dWu
        down = jax.nn.relu(jnp.einsum('bld,bnd->bln', x, Wd_b) + bd)
        up = jnp.einsum('bln,bdn->bld', down, Wu_b) + bu
        return x + up

    def _L1_cond_ref(input, convInfo, weight, bias, lin_w, lin_b):
        import jax, jax.numpy as jnp
        import numpy as np
        EPS = 1e-05
        mean = jnp.mean(input, axis=-1, keepdims=True)
        var = jnp.mean(jnp.square(input - mean), axis=-1, keepdims=True)
        out = (input - mean) * jax.lax.rsqrt(var + EPS) * weight + bias
        tar_bias = jnp.tanh(convInfo @ lin_w.T + lin_b)[:, None, :]
        out = out + tar_bias
        return out * weight + bias

    def _L2_cond_ref(x, t_embd, c_embd, W_t1, b_t1, W_t2, b_t2, W_c, b_c, W_qkv, b_qkv, W_o, b_o, W_f1, b_f1, W_f2, b_f2):
        import jax, jax.numpy as jnp
        import numpy as np
        import math
        H = 256
        NH = 16
        DH = H // NH
        EPS = 1e-05

        def _layernorm(x):
            m = jnp.mean(x, axis=-1, keepdims=True)
            v = jnp.mean((x - m) ** 2, axis=-1, keepdims=True)
            return (x - m) / jnp.sqrt(v + EPS)

        def _gelu_tanh(x):
            c = math.sqrt(2.0 / math.pi)
            return 0.5 * x * (1.0 + jnp.tanh(c * (x + 0.044715 * x ** 3)))
        B, P, _ = x.shape
        t = jax.nn.silu(t_embd @ W_t1.T + b_t1) @ W_t2.T + b_t2
        cond = jax.nn.silu(t + c_embd) @ W_c.T + b_c
        g1, b1, g2, b2, a1, a2 = jnp.split(cond, 6, axis=-1)
        res1 = x
        h = _layernorm(x) * g1[:, None, :] + b1[:, None, :]
        qkv = h @ W_qkv.T + b_qkv
        q, k, v = jnp.split(qkv, 3, axis=-1)
        q = q.reshape(B, P, NH, DH).transpose(0, 2, 1, 3)
        k = k.reshape(B, P, NH, DH).transpose(0, 2, 1, 3)
        v = v.reshape(B, P, NH, DH).transpose(0, 2, 1, 3)
        scores = jnp.einsum('bhqd,bhkd->bhqk', q, k) / math.sqrt(DH)
        attn = jax.nn.softmax(scores, axis=-1)
        o = jnp.einsum('bhqk,bhkd->bhqd', attn, v)
        o = o.transpose(0, 2, 1, 3).reshape(B, P, H)
        o = o @ W_o.T + b_o
        x = res1 + o * a1[:, None, :]
        res2 = x
        h = _layernorm(x) * g2[:, None, :] + b2[:, None, :]
        h = _gelu_tanh(h @ W_f1.T + b_f1) @ W_f2.T + b_f2
        x = res2 + h * a2[:, None, :]
        return x

    def _L3_cond_ref(x, cond, norm_w, up_w, down_w):
        import jax, jax.numpy as jnp
        import numpy as np
        EPS = 1e-06

        def act_quant(x):
            scale = 127.0 / jnp.clip(jnp.max(jnp.abs(x), axis=-1, keepdims=True), 1e-05, None)
            return jnp.clip(jnp.round(x * scale), -128.0, 127.0) / scale

        def weight_quant(w):
            scale = 1.0 / jnp.clip(jnp.mean(jnp.abs(w)), 1e-05, None)
            return jnp.clip(jnp.round(w * scale), -1.0, 1.0) / scale
        scale = cond @ norm_w.T + 1.0
        ms = jnp.mean(x * x, axis=-1, keepdims=True)
        h = x * (scale[:, None, :] * jax.lax.rsqrt(ms + EPS))
        u = h @ up_w.T
        val, gate = jnp.split(u, 2, axis=-1)
        h = val * jax.nn.gelu(gate, approximate=False)
        hq = h + jax.lax.stop_gradient(act_quant(h) - h)
        wq = down_w + jax.lax.stop_gradient(weight_quant(down_w) - down_w)
        y = hq @ wq.T
        return y + x
    x = _L0_cond_ref(x, cond_256, L0_cond_Wd, L0_cond_bd, L0_cond_Wu, L0_cond_bu, L0_cond_Wdd, L0_cond_bdd, L0_cond_Wdu, L0_cond_bdu)
    x = _L1_cond_ref(x, cond_256, L1_cond_weight, L1_cond_bias, L1_cond_lin_w, L1_cond_lin_b)
    x = _L2_cond_ref(x, cond_256, fside_BxS_0, L2_cond_W_t1, L2_cond_b_t1, L2_cond_W_t2, L2_cond_b_t2, L2_cond_W_c, L2_cond_b_c, L2_cond_W_qkv, L2_cond_b_qkv, L2_cond_W_o, L2_cond_b_o, L2_cond_W_f1, L2_cond_b_f1, L2_cond_W_f2, L2_cond_b_f2)
    x = _L3_cond_ref(x, cond_256, L3_cond_norm_w, L3_cond_up_w, L3_cond_down_w)
    return x

_drawn_inputs = setup_inputs


def setup_inputs(seed=0):
    import zlib

    import numpy as np

    out = dict(_drawn_inputs(seed))
    spreads = {'L1_cond_weight': (1.0, 0.2),
     'L1_cond_bias': (0.0, 0.1),
     'L2_cond_b_t1': (0.0, 0.8),
     'L2_cond_b_t2': (0.0, 0.8),
     'L2_cond_b_c': (0.0, 0.641),
     'L2_cond_b_qkv': (0.0, 0.8),
     'L2_cond_b_o': (0.0, 0.492),
     'L2_cond_b_f1': (0.0, 0.8),
     'L2_cond_b_f2': (0.0, 1.483)}
    factors = {'fside_BxS_0': 2.813,
     'L0_cond_bd': 3.622,
     'L1_cond_lin_b': 8.0,
     'L2_cond_W_t1': 8.0,
     'L2_cond_W_t2': 8.0,
     'L2_cond_W_qkv': 8.0,
     'L2_cond_W_o': 8.0,
     'L2_cond_W_f1': 8.0,
     'L2_cond_W_f2': 7.526,
     'L3_cond_norm_w': 8.0,
     'L3_cond_up_w': 3.286,
     'L3_cond_down_w': 3.304}
    for name, (base, spread) in spreads.items():
        noise = np.random.default_rng([zlib.crc32(name.encode()), seed]).standard_normal(out[name].shape)
        drawn = base * np.exp(spread * noise) if base else spread * noise
        out[name] = jnp.asarray(drawn.astype(out[name].dtype))
    for name, factor in factors.items():
        out[name] = (out[name] * factor).astype(out[name].dtype)
    return out
```

```python
from contextlib import ExitStack

import concourse.bass as bass
from concourse import mybir

F32 = mybir.dt.float32
F32R = mybir.dt.float32r
BF16 = mybir.dt.bfloat16
ALU = mybir.AluOpType
ACT = mybir.ActivationFunctionType
AX = mybir.AxisListType

P = 128
NB = 16
L = 256
D = 256
BN = 128
HC = 64
NH = 16
DH = D // NH
FF = 1024
RT = L // P
KT = D // P
FT = FF // P
NCH = 16
CHC = BN * D // NCH
HALF = 512
DELTA = 0.1
EPS_LN = 1e-5
EPS_RMS = 1e-6
Q_MIN = 1e-5
ROUND = 1.5 * 2.0 ** 23
KQ = 3 * DH
KM = KQ + 2

PE_A = ["down", "up", "ht", "q", "k", "v"]
PE_S = [f"s{u}" for u in range(NH)]
PE_M = [f"m{g}" for g in range(4)]
PE_T = [f"t{h}" for h in range(NH)]
PE_O = [f"o{h}" for h in range(NH)]
PE_C = ["ot", "proj", "ht", "f0", "f1", "f2", "f3", "y"]
PE_D = ["xt", "g0", "v0", "g1", "v1", "g2", "v2", "g3", "v3", "qt0", "y0", "qt1", "y1"]
ACT_A = ["relu", "hi", "qhi0", "qhi1", "khi0", "khi1", "v"]
ACT_T = [f"exp{h}" for h in range(NH)]
ACT_C = ["ot", "hi"] + [f"gelu{m}" for m in range(FT)]
ACT_D = ["sq0", "sq1", "hi", "gelu0", "gelu1", "gelu2", "gelu3", "qt0", "qt1"]
DVE_A = ["x0", "st0", "st1", "ag0", "ag1", "n0", "n1", "st2", "st3", "ag2", "ag3", "n2", "n3",
         "ev0", "ev1", "lo", "qlo0", "qlo1", "klo0", "klo1"]
DVE_S = [f"max{u}" for u in range(NH)]
DVE_M = [f"{part}{g}" for g in range(4) for part in ("hi", "lo")]
DVE_O = ["rec0", "norm0", "rec1", "norm1"]
DVE_C = ["gate1", "st0", "st1", "ag0", "ag1", "n0", "n1", "ev0", "ev1", "lo", "gate2"]
DVE_D = ["ev0", "ev1", "lo", "h0", "h1", "amax0", "step0", "inv0", "back0", "ra0", "rb0",
         "h2", "h3", "amax1", "step1", "inv1", "back1", "ra1", "rb1", "y0", "y1"]
POOL_A = ["xbu", "ve0", "rs0", "w2", "x1", "xr", "ve1", "rs1"]
POOL_C = ["x2", "xr", "ve", "rs", "x3"]
POOL_D = ["ve", "rs"]


def at(steps, name, b):
    return b * len(steps) + (steps.index(name) + 1)


def order(a, bb, c, d):
    S = lambda u: ("B", "s", u)
    M = lambda g: ("B", "m", g)
    U = lambda u: ("D", "u", u)
    F = lambda k: ("C", "f", k)
    T = lambda h: ("B", "t", h)
    O = lambda h: ("B", "o", h)
    G = lambda j: ("C", "g", j)
    one = [S(0), ("A", "down", 0), S(1), ("D", "xt", 0), S(2), ("C", "ot", 0), S(3), ("C", "proj", 0), ("A", "up", 0), M(0),
           U(0), S(4), ("C", "ln", 0), S(5), ("A", "n0", 0), U(1), S(6), ("C", "n1", 0), S(7), ("D", "quant", 0), M(1),
           ("C", "ht", 0), U(2), S(8), ("A", "ln", 0), S(9), U(3), ("A", "n1", 0), S(10), S(11), M(2), ("D", "quant", 1)]
    two = [F(0), S(12), S(13), F(1), S(14), S(15), F(2), ("A", "ht", 0), M(3), ("A", "load", 0), F(3)]
    fill = {0: [("A", "k", 0)], 1: [("A", "v", 0)], 2: [G(0)], 3: [G(1)], 4: [G(2)], 5: [G(3)], 6: [("D", "qt", 0)],
            7: [("D", "y", 0)], 8: [("D", "qt", 1)], 9: [("D", "y", 1)]}
    three = [("A", "q", 0)]
    for h in range(NH):
        three.append(T(h))
        if h:
            three.append(O(h - 1))
        three += fill.get(h, [])
    three.append(O(NH - 1))
    on = {"A": a, "B": bb, "C": c, "D": d}
    return [s for s in one + two + three if on[s[0]]]


def cond_seq_kernel(nc, xT, x, hyper, base, cols, k64, rows, w_qkv, w_o, w_f1, w_f2, w_up, w_down, out,
                    rows_scratch, cur_scratch, qk_scratch):
    ctx = ExitStack()
    with ctx:
        def sb(name, shape, dt):
            return ctx.enter_context(nc.sbuf_tensor(name, shape, dt))

        def sem(name):
            return ctx.enter_context(nc.semaphore(name))

        wqkv_hi = sb("wqkv_hi", [P, KT, 3 * D], F32R)
        wqkv_lo = sb("wqkv_lo", [P, KT, 3 * D], F32R)
        wf1_hi = sb("wf1_hi", [P, KT, FF], F32R)
        wf1_lo = sb("wf1_lo", [P, KT, FF], F32R)
        wup_hi = sb("wup_hi", [P, KT, 2 * FF], F32R)
        wup_lo_at = nc.sbuf_base
        wup_lo = sb("wup_lo", [P, KT, 2 * FF], F32R)
        wo = sb("wo", [P, KT, D], F32)
        wf2 = sb("wf2", [P, FT, D], F32)
        wq3 = sb("wq3", [P, FT, D], BF16)
        small = sb("small", [P, 192], F32)
        ident = small[:, 0:128]
        bt1, bt2, bc_t = small[:, 128:130], small[:, 130:132], small[:, 132:144]
        bd, bq, bk, bv, bf1 = small[:, 144:145], small[:, 145:147], small[:, 147:149], small[:, 149:151], small[:, 151:159]
        identb = sb("identb", [P, P], BF16)
        bu_t = sb("bu_t", [P, D], F32)
        w2_t = sb("w2_t", [P, D], F32)
        mod = sb("mod", [P, 8, NB], F32)
        scale3 = sb("scale3", [P, KT, NB], F32)
        wmean = sb("wmean", [P, 2], F32)
        half_neg = sb("half_neg", [P, RT], F32)
        eps_ln = sb("eps_ln", [P, RT], F32)
        eps_rms = sb("eps_rms", [P, RT], F32)
        Kp = sb("Kp", [P, 2, NH // 2, L], F32R)
        Va = sb("Va", [P, 2, RT, NH, DH + 1], F32)
        xT_t = sb("xT_t", [P, KT, L], F32)
        x_t = sb("x_t", [P, RT, D], F32)
        cur = sb("cur", [P, 2 * D], F32)
        tA = sb("tA", [P, 2, D], F32)
        stage_at = nc.sbuf_base
        Qp = sb("Qp", [P, 2, NH // 2, L], F32R)
        tC = sb("tC", [P, 3, D], F32)
        dn = sb("dn", [P, L], F32)
        x0 = sb("x0", [P, RT, D], F32)
        xr = sb("xr", [P, 2, RT, D], F32)
        hA = sb("hA", [P, KT, L], F32)
        hA_hi = sb("hA_hi", [P, KT, L], F32R)
        hA_lo = sb("hA_lo", [P, KT, L], F32R)
        q_hi = sb("q_hi", [P, 2, L], F32R)
        q_lo = sb("q_lo", [P, 2, L], F32R)
        k_hi = sb("k_hi", [P, 2, L], F32R)
        k_lo = sb("k_lo", [P, 2, L], F32R)
        stA = sb("stA", [P, RT, 6], F32)
        mvA = sb("mvA", [P, RT, 2], F32)
        rsA = sb("rsA", [P, 2, RT], F32)
        nmax = sb("nmax", [P, 2, 8], F32)
        m_hi = sb("m_hi", [8, 2, P], F32R)
        m_lo = sb("m_lo", [8, 2, P], F32R)
        Pr = sb("Pr", [P, 3, 2 * L], F32)
        rec = sb("rec", [P, RT, 8], F32)
        o_t = sb("o_t", [P, RT, D], F32)
        oT = sb("oT", [P, KT, L], F32)
        xc = sb("xc", [P, RT, D], F32)
        xcr = sb("xcr", [P, RT, D], F32)
        stC = sb("stC", [P, RT, 6], F32)
        mvC = sb("mvC", [P, RT, 2], F32)
        rsC = sb("rsC", [P, 2, RT], F32)
        hC = sb("hC", [P, KT, L], F32)
        hC_hi = sb("hC_hi", [P, KT, L], F32R)
        hC_lo = sb("hC_lo", [P, KT, L], F32R)
        G = sb("G", [P, FT, L], F32)
        x3 = sb("x3", [P, 2, RT, D], F32)
        hD = sb("hD", [P, KT, L], F32)
        hD_hi = sb("hD_hi", [P, KT, L], F32R)
        hD_lo = sb("hD_lo", [P, KT, L], F32R)
        sq = sb("sq", [P, D], F32)
        ssD = sb("ssD", [P, RT], F32)
        rsD = sb("rsD", [P, 2, RT], F32)
        gl = sb("gl", [P, 2, HALF], F32)
        hd = sb("hd", [P, FF], F32)
        am = sb("am", [P, RT, 4], F32)
        qi = sb("qi", [P, RT, FF], BF16)
        qT = sb("qT", [P, FT, P], BF16)
        ys = sb("ys", [P, RT, D], F32)

        def staged(name, shape, dt, words):
            nonlocal stage_at
            t = nc.alloc_sbuf_tensor_at(name, shape, dt, offset=stage_at)
            stage_at += 4 * words
            return t

        hyp = staged("hyp", [P, 4, CHC], F32, 4 * CHC)
        raw = staged("raw", [P, 2 * P, 2 * NB], F32, 64 * P)
        stg = staged("stg", [P, 2, 2048], F32, 4096)
        base_t = staged("base_t", [P, 2, 2, D], F32, 4 * D)
        condbd = staged("condbd", [P, 2 * NB], F32, 2 * NB)
        c64 = staged("c64", [HC, NB + 3 * D], F32, NB + 3 * D)
        wt2 = staged("wt2", [P, KT, D], F32, KT * D)
        side = staged("side", [P, KT, NB], F32, KT * NB)
        zb = staged("zb", [P, 4, KT, NB], F32, 4 * KT * NB)
        s1 = staged("s1", [P, KT, NB], F32, KT * NB)
        s2 = staged("s2", [P, KT, NB], F32, KT * NB)
        ones = staged("ones", [P, P], F32, P)
        wsum = staged("wsum", [P, 4], F32, 4)
        assert stage_at <= nc.sbuf_base, (stage_at, nc.sbuf_base)
        row_t = nc.alloc_sbuf_tensor_at("row_t", [P, 8 * D], F32, offset=wup_lo_at)
        tb = nc.alloc_sbuf_tensor_at("tb", [NB, 8, D], F32, offset=wup_lo_at + 32 * D)
        raw_flat = raw[:, :, :].rearrange("p j n -> p (j n)")
        curall = hyp[:, :, :].rearrange("p s c -> p (s c)").rearrange("p (b n) -> p b n", b=NB)

        bank = [ctx.enter_context(nc.psum_tensor(f"bank{i}", [P, HALF], F32)) for i in range(8)]
        F_BANK = [bank[5], bank[1], bank[2], bank[3]]

        pe_a, pe_s, pe_m, pe_t, pe_o, pe_c, pe_d = (sem(f"pe_{s}") for s in "asmtocd")
        act_a, act_t, act_c, act_d = (sem(f"act_{s}") for s in "atcd")
        dve_a, dve_s, dve_m, dve_o, dve_c, dve_d = (sem(f"dve_{s}") for s in "asmocd")
        pool_a, pool_c, pool_d = (sem(f"pool_{s}") for s in "acd")
        xT_in, x_in, cur_in, tA_in, tC_in = (sem(f"{s}_in") for s in ("xT", "x", "cur", "tA", "tC"))
        qh_out, ql_out, kh_out, kl_out = (sem(f"{s}_out") for s in ("qh", "ql", "kh", "kl"))
        qp_in, kp_in = sem("qp_in"), sem("kp_in")
        mx_in = [sem(f"mx_in{g}") for g in range(4)]
        y_out = [sem(f"y_out{r}") for r in range(RT)]
        hyp_in = [sem(f"hyp_in{i}") for i in range(4)]
        hyp_mm, raw_act, raw_dve = sem("hyp_mm"), sem("raw_act"), sem("raw_dve")
        small_in, k64_in, side_in, row_in, wt2_in, wc_in, cond_in, base_in = (
            sem(f"{s}_in") for s in ("small", "k64", "side", "row", "wt2", "wc", "cond", "base"))
        w_in = [sem("w_in0"), sem("w_in1")]
        wo_in, wf2_in = sem("wo_in"), sem("wf2_in")
        split, prep, zero, cur_done, rows_done = sem("split"), sem("prep"), sem("zero"), sem("cur_done"), sem("rows_done")
        pre_pe, pre_act, ones_set = sem("pre_pe"), sem("pre_act"), sem("ones_set")
        rows_out, cur_out, cond_clear = sem("rows_out"), sem("cur_out"), sem("cond_clear")

        block = ctx.enter_context(nc.Block())

        PREP = ["z1", "d1", "r1", "s1", "z2a", "z2", "d2", "r2", "s2", "mod", "scale3", "tbl", "a12", "co",
                "tb1", "tb2", "c", "a1co", "a2bf", "bu", "w2", "base", "identb"]
        PRE_PE = ["t1", "t2", "mod", "s3", "tb", "a12", "co", "wsum"]
        SPLIT = ["qkv_hi", "qkv_lo", "f1_hi", "f1_lo", "up0_hi", "up0_lo", "up1_hi", "up1_lo",
                 "wabs", "mean", "inv", "wround", "wclip", "wq"]
        WPARTS = [("qkv", w_qkv, wqkv_hi, wqkv_lo, 0, KT * 3 * D), ("f1", w_f1, wf1_hi, wf1_lo, 0, KT * FF),
                  ("up0", w_up, wup_hi, wup_lo, 0, 2048), ("up1", w_up, wup_hi, wup_lo, 2048, 2048)]

        def turns(eng, body):
            def alone(t):
                body(t, t % 2, order(t < NB, 1 <= t <= NB, 2 <= t <= NB + 1, t >= 3))

            for t in range(4):
                alone(t)
            with eng.Fori(4, NB - 2, 2) as t:
                body(t, 0, order(True, True, True, True))
                body(t + 1, 1, order(True, True, True, True))
            for t in range(NB - 2, NB + 3):
                alone(t)

        def past(eng, sem_, steps, name, b, back):
            if not isinstance(b, int) or b >= back:
                eng.wait_ge(sem_, at(steps, name, b - back))

        @block.sync
        def _(sp):
            sp.dma_start(c64[:, :], k64).then_inc(k64_in, 16)
            sp.wait_ge(cond_clear, 1)
            sp.dma_start(condbd[0:HC, 0:NB], k64[:, 0:NB]).then_inc(cond_in, 16)
            sp.dma_start(condbd[HC:P, NB:2 * NB], k64[:, 0:NB]).then_inc(cond_in, 16)
            sp.dma_start(small[:, 0:192], cols[:, 0:192]).then_inc(small_in, 16)
            sp.dma_start(side[:, :, :].rearrange("p a b -> p (a b)"), cols[:, 192:224]).then_inc(side_in, 16)
            sp.dma_start(wt2[:, :, :].rearrange("p a b -> p (a b)"), cols[:, 224:736]).then_inc(wt2_in, 16)
            sp.dma_start(base_t[:, :, :, :].rearrange("p a b c -> p (a b c)"), base).then_inc(base_in, 16)
            for s in range(4):
                sp.dma_start(hyp[:, s, :], hyper[:, s * CHC:(s + 1) * CHC]).then_inc(hyp_in[s], 16)
            with sp.Fori(1, NCH // 4) as i:
                for s in range(4):
                    sp.wait_ge(hyp_mm, i * 4 + (s - 3))
                    sp.dma_start(hyp[:, s, :], hyper[:, bass.ds(i * (4 * CHC) + s * CHC, CHC)]).then_inc(hyp_in[s], 16)
            sp.wait_ge(cur_done, 2 * NB)
            sp.dma_start(cur_scratch.rearrange("b p n -> p b n"), curall).then_inc(cur_out, 16)
            sp.wait_ge(prep, PREP.index("a2bf") + 1)
            sp.dma_start(rows_scratch, tb[:, 0:5, :]).then_inc(rows_out, 16)
            sp.wait_ge(cur_out, 16)
            sp.wait_ge(rows_out, 16)

            def load_a(b):
                sp.dma_start(xT_t[:, :, :], xT[bass.ds(b, 1)].rearrange("o p a b -> (o p) a b")).then_inc(xT_in, 16)
                sp.dma_start(x_t[:, :, :], x[bass.ds(b, 1)].rearrange("o p a b -> (o p) a b")).then_inc(x_in, 16)
                sp.dma_start(cur[:, :], cur_scratch[bass.ds(b, 1)].rearrange("o p n -> (o p) n")).then_inc(cur_in, 16)
                sp.dma_start(tA[:, :, :].rearrange("p a b -> p (a b)"),
                             rows_scratch[bass.ds(b, 1), 0:2, :].rearrange("o a b -> o (a b)").to_broadcast([P, 2 * D])).then_inc(tA_in, 16)

            load_a(0)
            sp.wait_ge(split, len(SPLIT))

            def turn(t, par, slices):
                a, b, c = t, t - 1, t - 2
                for stage, what, n in slices:
                    if (stage, what) == ("A", "k"):
                        for parts, ready_hi, ready_lo, outs, w in (
                                ((q_hi, q_lo), "qhi1", "qlo1", (qh_out, ql_out), 0),
                                ((k_hi, k_lo), "khi1", "klo1", (kh_out, kl_out), 2)):
                            sp.wait_ge(act_a, at(ACT_A, ready_hi, a))
                            sp.dma_start(qk_scratch[w], parts[0][:, :, :].rearrange("p a b -> p (a b)").bitcast(F32)).then_inc(outs[0], 16)
                            sp.wait_ge(dve_a, at(DVE_A, ready_lo, a))
                            sp.dma_start(qk_scratch[w + 1], parts[1][:, :, :].rearrange("p a b -> p (a b)").bitcast(F32)).then_inc(outs[1], 16)
                        for outs, dst, srcs, arrived in (((qh_out, ql_out), Qp, (0, 0, 1), qp_in), ((kh_out, kl_out), Kp, (2, 3, 2), kp_in)):
                            sp.wait_ge(outs[0], 16 * a + 16)
                            sp.wait_ge(outs[1], 16 * a + 16)
                            if not isinstance(a, int) or a >= 2:
                                sp.wait_ge(pe_t, at(PE_T, "t15", a - 2))
                            for half in range(2):
                                for r, w in enumerate(srcs):
                                    sp.dma_start(
                                        dst[64 * half + DH * r:64 * half + DH * (r + 1), par, :, :].rearrange("d (j c) n -> d j (c n)", j=4).bitcast(F32),
                                        qk_scratch[w, 64 * half:64 * half + 64, :].rearrange("(j d) n -> d j n", j=4)).then_inc(arrived, 16)
                    elif (stage, what) == ("B", "m"):
                        sp.wait_ge(dve_m, at(DVE_M, f"lo{n}", b))
                        for half in range(2):
                            for row, part in ((KQ, m_hi), (KQ + 1, m_lo)):
                                src = part[4 * half:4 * half + 4, n % 2, :]
                                sp.dma_start(Qp[64 * half + row:64 * half + row + 1, 1 - par, 2 * n:2 * n + 2, :].bitcast(F32),
                                             src.bitcast(F32)).then_inc(mx_in[n], 16)
                    elif (stage, what) == ("A", "load"):
                        if not isinstance(t, int) or t + 1 < NB:
                            sp.wait_ge(pe_a, at(PE_A, "up", a))
                            sp.wait_ge(pool_a, at(POOL_A, "xr", a))
                            sp.wait_ge(dve_a, at(DVE_A, "x0", a))
                            load_a(a + 1)
                    elif (stage, what) == ("C", "ot"):
                        past(sp, dve_c, DVE_C, "gate2", c, 1)
                        past(sp, pool_c, POOL_C, "xr", c, 1)
                        sp.dma_start(tC[:, :, :].rearrange("p a b -> p (a b)"),
                                     rows_scratch[bass.ds(c, 1), 2:5, :].rearrange("o a b -> o (a b)").to_broadcast([P, 3 * D])).then_inc(tC_in, 16)
                    elif (stage, what) == ("D", "y"):
                        sp.wait_ge(dve_d, at(DVE_D, f"y{n}", t - 3))
                        sp.dma_start(out[bass.ds(t - 3, 1), n * P:(n + 1) * P, :].rearrange("o p n -> (o p) n"), ys[:, n, :]).then_inc(y_out[n], 16)

            turns(sp, turn)
            for r in range(RT):
                sp.wait_ge(y_out[r], 16 * NB)

        @block.tensor
        def _(pe):
            def three(dst, lhs, rhs, first, last):
                for i, (l, r) in enumerate(((lhs[0], rhs[0]), (lhs[1], rhs[0]), (lhs[0], rhs[1]))):
                    mm = pe.matmul(dst, l, r, start=first and i == 0, stop=last and i == 2)
                return mm

            pe.wait_ge(k64_in, 16)
            for m in range(KT):
                mm = pe.matmul(bank[4][:, m * NB:(m + 1) * NB], c64[:, NB + m * P:NB + (m + 1) * P], c64[:, 0:NB], start=True, stop=True)
            mm.then_inc(pre_pe, 1)
            pe.wait_ge(wt2_in, 16)
            pe.wait_ge(prep, PREP.index("s1") + 1)
            for m in range(KT):
                for k in range(KT):
                    mm = pe.matmul(bank[5][:, m * NB:(m + 1) * NB], wt2[:, k, m * P:(m + 1) * P], s1[:, k, :], start=k == 0, stop=k == KT - 1)
            mm.then_inc(pre_pe, 1)
            pe.wait_ge(w_in[0], 16)
            pe.wait_ge(w_in[1], 16)
            pe.wait_ge(prep, PREP.index("s2") + 1)
            wc = stg[:, :, 0:6 * D]
            for m in range(8):
                for k in range(KT):
                    mm = pe.matmul(bank[6][:, m * NB:(m + 1) * NB], wc[:, k, m * P:(m + 1) * P], s2[:, k, :], start=k == 0, stop=k == KT - 1)
            mm.then_inc(pre_pe, 1)
            for m in range(KT):
                mm = pe.matmul(bank[7][:, m * NB:(m + 1) * NB], c64[:, NB + 2 * D + m * P:NB + 2 * D + (m + 1) * P], c64[:, 0:NB], start=True, stop=True)
            mm.then_inc(pre_pe, 1)
            pe.wait_ge(prep, PREP.index("z1") + 1)
            pe.matmul(bank[4][0:NB, 0:D], c64[:, 0:NB], c64[:, NB + D:NB + 2 * D], start=True, stop=True).then_inc(pre_pe, 1)
            pe.wait_ge(prep, PREP.index("z2a") + 1)
            for k in range(KT):
                mm = pe.matmul(bank[5][0:NB, 0:2 * D], s2[:, k, :], wc[:, k, 4 * D:6 * D], start=k == 0, stop=k == KT - 1)
            mm.then_inc(pre_pe, 1)
            pe.wait_ge(wo_in, 16)
            pe.wait_ge(small_in, 16)
            pe.wait_ge(prep, PREP.index("mod") + 1)
            for k in range(KT):
                mm = pe.matmul(bank[6][0:NB, 0:D], bv[:, k:k + 1].to_broadcast([P, NB]), wo[:, k, :], start=k == 0, stop=k == KT - 1)
            mm.then_inc(pre_pe, 1)
            pe.wait_ge(cond_in, 32)

            def generate(i):
                for s in range(4):
                    pe.wait_ge(hyp_in[s], i * 16 + 16)
                    if not isinstance(i, int):
                        pe.wait_ge(raw_act if s % 2 == 0 else raw_dve, i * 2 + (s // 2 - 1))
                    for j in range(CHC // P):
                        mm = pe.matmul(bank[s][:, j * 2 * NB:(j + 1) * 2 * NB], hyp[:, s, j * P:(j + 1) * P], condbd[:, :], start=True, stop=True)
                    mm.then_inc(hyp_mm, 1)

            generate(0)
            with pe.Fori(1, NCH // 4) as i:
                generate(i)
            pe.wait_ge(split, at(SPLIT, "wabs", 0))
            pe.wait_ge(ones_set, 1)
            pe.wait_ge(prep, PREP.index("scale3") + 1)
            pe.matmul(bank[7][:, 0:1], ones[:, :], wsum[:, 0:1], start=True, stop=True).then_inc(pre_pe, 1)
            pe.wait_ge(prep, len(PREP))
            pe.wait_ge(split, len(SPLIT))

            def turn(t, par, slices):
                a, b, c, d = t, t - 1, t - 2, t - 3
                with_c = any(s[0] == "C" for s in slices)
                with_b = any(s[0] == "B" for s in slices)

                def a_down():
                    pe.wait_ge(xT_in, 16 * a + 16)
                    pe.wait_ge(cur_in, 16 * a + 16)
                    past(pe, act_a, ACT_A, "v", a, 1)
                    for k in range(KT):
                        mm = pe.matmul(bank[4][:, 0:L], cur[:, k * BN:(k + 1) * BN], xT_t[:, k, :], start=k == 0, stop=k == KT - 1)
                    mm.then_inc(pe_a, 1)

                def a_up():
                    pe.wait_ge(act_a, at(ACT_A, "relu", a))
                    for r in range(RT):
                        mm = pe.matmul(bank[4][:, r * D:(r + 1) * D], dn[:, r * P:(r + 1) * P], cur[:, D:2 * D], start=True, stop=True)
                    mm.then_inc(pe_a, 1)

                def a_ht():
                    pe.wait_ge(dve_a, at(DVE_A, "n3", a))
                    for k in range(KT):
                        for r in range(RT):
                            mm = pe.transpose(bank[4][:, k * L + r * P:k * L + (r + 1) * P], x0[:, r, k * P:(k + 1) * P], ident)
                    mm.then_inc(pe_a, 1)

                def a_q():
                    pe.wait_ge(dve_a, at(DVE_A, "lo", a))
                    for m in range(2):
                        for k in range(KT):
                            mm = three(bank[4][:, m * L:(m + 1) * L], (wqkv_hi[:, k, m * P:(m + 1) * P], wqkv_lo[:, k, m * P:(m + 1) * P]),
                                       (hA_hi[:, k, :], hA_lo[:, k, :]), k == 0, k == KT - 1)
                    mm.then_inc(pe_a, 1)

                def a_k():
                    if with_c:
                        pe.wait_ge(act_c, at(ACT_C, "gelu1", c))
                    else:
                        past(pe, dve_a, DVE_A, "klo1", a, 1)
                    for m in range(2):
                        for k in range(KT):
                            mm = three(bank[5][:, m * L:(m + 1) * L], (wqkv_hi[:, k, D + m * P:D + (m + 1) * P], wqkv_lo[:, k, D + m * P:D + (m + 1) * P]),
                                       (hA_hi[:, k, :], hA_lo[:, k, :]), k == 0, k == KT - 1)
                    mm.then_inc(pe_a, 1)

                def a_v():
                    pe.wait_ge(dve_a, at(DVE_A, "qlo1", a))
                    for r in range(RT):
                        for k in range(KT):
                            mm = three(bank[4][:, r * D:(r + 1) * D], (hA_hi[:, k, r * P:(r + 1) * P], hA_lo[:, k, r * P:(r + 1) * P]),
                                       (wqkv_hi[:, k, 2 * D:3 * D], wqkv_lo[:, k, 2 * D:3 * D]), k == 0, k == KT - 1)
                    mm.then_inc(pe_a, 1)

                def b_s(u):
                    lo, g = 64 * (u % 2), u // 2
                    if u == 0:
                        pe.wait_ge(qp_in, 96 * b + 96)
                        pe.wait_ge(kp_in, 96 * b + 96)
                        past(pe, dve_m, DVE_M, "lo3", b, 1)
                    elif u % 4 == 0:
                        pe.wait_ge(dve_m, at(DVE_M, f"lo{u // 4 - 1}", b))
                    else:
                        pe.wait_ge(dve_s, at(DVE_S, f"max{u - 1}", b))
                    for r in range(RT):
                        mm = pe.matmul(bank[0][:, r * L:(r + 1) * L], Qp[lo:lo + KQ, 1 - par, g, r * P:(r + 1) * P],
                                       Kp[lo:lo + KQ, 1 - par, g, :], start=True, stop=True)
                    mm.then_inc(pe_s, 1)

                def b_m(g):
                    pe.wait_ge(dve_s, at(DVE_S, f"max{4 * g + 3}", b))
                    pe.transpose(bank[0][0:8, 0:P], nmax[:, g % 2, :], ident).then_inc(pe_m, 1)

                def b_t(h):
                    lo, g = 64 * (h % 2), h // 2
                    dst = bank[1 + h % 2]
                    if h % 4 == 0:
                        pe.wait_ge(mx_in[h // 4], 64 * b + 64)
                    if h >= 2:
                        pe.wait_ge(act_t, at(ACT_T, f"exp{h - 2}", b))
                    elif with_c:
                        pe.wait_ge(act_c, at(ACT_C, f"gelu{3 + 2 * h}", c))
                    else:
                        past(pe, act_t, ACT_T, f"exp{h + 14}", b, 1)
                    for k in range(RT):
                        mm = pe.matmul(dst[:, k * L:(k + 1) * L], Kp[lo:lo + KM, 1 - par, g, k * P:(k + 1) * P],
                                       Qp[lo:lo + KM, 1 - par, g, :], start=True, stop=True)
                    mm.then_inc(pe_t, 1)

                def b_o(h):
                    if h == 0:
                        pe.wait_ge(act_a, at(ACT_A, "v", b))
                        if with_c:
                            pe.wait_ge(act_c, at(ACT_C, "gelu7", c))
                        past(pe, dve_o, DVE_O, "norm1", b, 1)
                    if h == 8:
                        pe.wait_ge(dve_o, at(DVE_O, "norm0", b))
                    pe.wait_ge(act_t, at(ACT_T, f"exp{h}", b))
                    for r in range(RT):
                        for k in range(RT):
                            col = (r * 8 + h % 8) * (DH + 1)
                            mm = pe.matmul(bank[3][:, col:col + DH + 1], Pr[:, h % 3, k * L + r * P:k * L + (r + 1) * P],
                                           Va[:, 1 - par, k, h, :], start=k == 0, stop=k == RT - 1)
                    mm.then_inc(pe_o, 1)

                def c_ot():
                    pe.wait_ge(dve_o, at(DVE_O, "norm1", c))
                    past(pe, dve_c, DVE_C, "gate2", c, 1)
                    if isinstance(c, int) and c == 0:
                        pe.wait_ge(dve_a, at(DVE_A, "klo1", a - 1))
                    for k in range(KT):
                        for r in range(RT):
                            mm = pe.transpose(bank[5][:, k * L + r * P:k * L + (r + 1) * P], o_t[:, r, k * P:(k + 1) * P], ident)
                    mm.then_inc(pe_c, 1)

                def c_proj():
                    pe.wait_ge(act_c, at(ACT_C, "ot", c))
                    for r in range(RT):
                        for k in range(KT):
                            mm = pe.matmul(bank[5][:, r * D:(r + 1) * D], oT[:, k, r * P:(r + 1) * P], wo[:, k, :], start=k == 0, stop=k == KT - 1)
                    mm.then_inc(pe_c, 1)

                def c_ht():
                    pe.wait_ge(dve_c, at(DVE_C, "n1", c))
                    for k in range(KT):
                        for r in range(RT):
                            mm = pe.transpose(bank[5][:, k * L + r * P:k * L + (r + 1) * P], xc[:, r, k * P:(k + 1) * P], ident)
                    mm.then_inc(pe_c, 1)

                def c_f(n):
                    if n == 0:
                        pe.wait_ge(dve_c, at(DVE_C, "lo", c))
                    for m in (2 * n, 2 * n + 1):
                        for k in range(KT):
                            mm = three(F_BANK[n][:, (m % 2) * L:(m % 2 + 1) * L], (wf1_hi[:, k, m * P:(m + 1) * P], wf1_lo[:, k, m * P:(m + 1) * P]),
                                       (hC_hi[:, k, :], hC_lo[:, k, :]), k == 0, k == KT - 1)
                    mm.then_inc(pe_c, 1)

                def c_g(n):
                    r = n // 2
                    if n == 0:
                        pe.wait_ge(act_c, at(ACT_C, "gelu7", c))
                        if not isinstance(a, int) or a < NB:
                            pe.wait_ge(dve_a, at(DVE_A, "klo1", a))
                    for k in range(4 * (n % 2), 4 * (n % 2) + 4):
                        mm = pe.matmul(bank[5][:, r * D:(r + 1) * D], G[:, k, r * P:(r + 1) * P], wf2[:, k, :], start=k == 0, stop=k == FT - 1)
                    if n == 3:
                        mm.then_inc(pe_c, 1)

                def d_xt():
                    pe.wait_ge(pool_c, at(POOL_C, "x3", d))
                    past(pe, dve_d, DVE_D, "y1", d, 1)
                    for k in range(KT):
                        for r in range(RT):
                            mm = pe.transpose(bank[6][:, k * L + r * P:k * L + (r + 1) * P], x3[:, 1 - par, r, k * P:(k + 1) * P], ident)
                    mm.then_inc(pe_d, 1)

                def d_u(n):
                    r, col = n // 2, (n % 2) * HALF
                    if n == 0:
                        pe.wait_ge(dve_d, at(DVE_D, "lo", d))
                    else:
                        pe.wait_ge(act_d, at(ACT_D, f"gelu{n - 1}", d))
                    lhs = [(hD_hi[:, k, r * P:(r + 1) * P], hD_lo[:, k, r * P:(r + 1) * P]) for k in range(KT)]
                    for k in range(KT):
                        c0 = FF + col
                        mm = three(bank[6][:, :], lhs[k], (wup_hi[:, k, c0:c0 + HALF], wup_lo[:, k, c0:c0 + HALF]), k == 0, k == KT - 1)
                    mm.then_inc(pe_d, 1)
                    if n == 0:
                        past(pe, act_d, ACT_D, "qt1", d, 1)
                    else:
                        pe.wait_ge(dve_d, at(DVE_D, f"h{n - 1}", d))
                    for k in range(KT):
                        mm = three(bank[7][:, :], lhs[k], (wup_hi[:, k, col:col + HALF], wup_lo[:, k, col:col + HALF]), k == 0, k == KT - 1)
                    mm.then_inc(pe_d, 1)

                def d_qt(r):
                    pe.wait_ge(dve_d, at(DVE_D, "h3" if r == 0 else "rb1", d))
                    if r == 1:
                        pe.wait_ge(act_d, at(ACT_D, "qt0", d))
                    for k in range(FT):
                        mm = pe.transpose(bank[7][:, :].bitcast(BF16)[:, k * P:(k + 1) * P], qi[:, r, k * P:(k + 1) * P], identb[:, :])
                    mm.then_inc(pe_d, 1)

                def d_y(r):
                    pe.wait_ge(act_d, at(ACT_D, f"qt{r}", d))
                    if r == 1:
                        pe.wait_ge(dve_d, at(DVE_D, "y0", d))
                    for k in range(FT):
                        mm = pe.matmul(bank[6][:, 0:D], qT[:, k, :], wq3[:, k, :], start=k == 0, stop=k == FT - 1)
                    mm.then_inc(pe_d, 1)

                for stage, what, n in slices:
                    if stage == "A" and what in ("down", "up", "ht", "q", "k", "v"):
                        {"down": a_down, "up": a_up, "ht": a_ht, "q": a_q, "k": a_k, "v": a_v}[what]()
                    elif stage == "B":
                        {"s": b_s, "m": b_m, "t": b_t, "o": b_o}[what](n)
                    elif stage == "C" and what in ("ot", "proj", "ht"):
                        {"ot": c_ot, "proj": c_proj, "ht": c_ht}[what]()
                    elif stage == "C" and what in ("f", "g"):
                        {"f": c_f, "g": c_g}[what](n)
                    elif stage == "D" and what == "xt":
                        d_xt()
                    elif stage == "D" and what in ("u", "qt", "y"):
                        {"u": d_u, "qt": d_qt, "y": d_y}[what](n)

            turns(pe, turn)

        @block.scalar
        def _(act):
            act.wait_ge(prep, PREP.index("z1") + 1)
            act.activation(zb[:, 1], zb[:, 0], ACT.Exp, scale=-1.0).then_inc(pre_act, 1)
            act.wait_ge(prep, PREP.index("z2") + 1)
            act.activation(zb[:, 3], zb[:, 2], ACT.Exp, scale=-1.0).then_inc(pre_act, 1)
            act.wait_ge(prep, PREP.index("tbl") + 1)
            act.activation(tb[:, 6, :], tb[:, 5, :], ACT.Tanh).then_inc(pre_act, 1)
            with act.Fori(0, NCH // 4) as i:
                for s in (0, 2):
                    act.wait_ge(hyp_mm, i * 4 + (s + 1))
                    act.activation(raw_flat[:, bass.ds(i * (4 * HALF) + s * HALF, HALF)], bank[s][:, :], ACT.Copy).then_inc(raw_act, 1)
            act.wait_ge(split, len(SPLIT))
            act.wait_ge(cur_out, 16)
            act.wait_ge(rows_out, 16)
            act.wait_ge(pre_pe, len(PRE_PE))

            def turn(t, par, slices):
                a, b, c, d = t, t - 1, t - 2, t - 3

                def a_down():
                    act.wait_ge(pe_a, at(PE_A, "down", a))
                    past(act, pe_a, PE_A, "up", a, 1)
                    act.activation(dn[:, :], bank[4][:, 0:L], ACT.Relu, bias=bd).then_inc(act_a, 1)

                def a_ht():
                    act.wait_ge(dve_a, at(DVE_A, "ev1", a))
                    past(act, pe_a, PE_A, "v", a, 1)
                    act.activation(hA_hi[:, :, :], hA[:, :, :], ACT.Copy).then_inc(act_a, 1)

                def a_parts(what, src, dst, bias, outs):
                    act.wait_ge(pe_a, at(PE_A, what, a))
                    if not isinstance(a, int) or a >= 1:
                        act.wait_ge(outs, 16 * a)
                    for m in range(2):
                        act.activation(dst[:, m, :], src[:, m * L:(m + 1) * L], ACT.Identity, bias=bias[:, m:m + 1]).then_inc(act_a, 1)

                def a_v():
                    act.wait_ge(pe_a, at(PE_A, "v", a))
                    past(act, pe_o, PE_O, "o15", a, 2)
                    act.activation(Va[:, par, :, :, 0:DH], bank[4][:, :].rearrange("p (r h e) -> p r h e", r=RT, h=NH),
                                   ACT.Copy).then_inc(act_a, 1)

                def b_t(h):
                    act.wait_ge(pe_t, at(PE_T, f"t{h}", b))
                    if h >= 3:
                        act.wait_ge(pe_o, at(PE_O, f"o{h - 3}", b))
                    else:
                        past(act, pe_o, PE_O, "o15", b, 1)
                    act.activation(Pr[:, h % 3, :], bank[1 + h % 2][:, :], ACT.Exp, scale=DH ** -0.5).then_inc(act_t, 1)

                def c_ot():
                    act.wait_ge(pe_c, at(PE_C, "ot", c))
                    past(act, pe_c, PE_C, "proj", c, 1)
                    act.activation(oT[:, :, :].rearrange("p k n -> p (k n)"), bank[5][:, :], ACT.Copy).then_inc(act_c, 1)

                def c_ht():
                    act.wait_ge(dve_c, at(DVE_C, "ev1", c))
                    past(act, pe_c, PE_C, "f3", c, 1)
                    act.activation(hC_hi[:, :, :], hC[:, :, :], ACT.Copy).then_inc(act_c, 1)

                def c_f(n):
                    act.wait_ge(pe_c, at(PE_C, f"f{n}", c))
                    past(act, pe_c, PE_C, "y", c, 1)
                    for m in (2 * n, 2 * n + 1):
                        act.activation(G[:, m, :], F_BANK[n][:, (m % 2) * L:(m % 2 + 1) * L], ACT.Gelu_apprx_tanh,
                                       bias=bf1[:, m:m + 1]).then_inc(act_c, 1)

                def d_xt():
                    act.wait_ge(pool_c, at(POOL_C, "x3", d))
                    for r in range(RT):
                        past(act, pool_d, POOL_D, "ve", d, 1)
                        if r:
                            act.wait_ge(act_d, at(ACT_D, "sq0", d))
                        else:
                            past(act, act_d, ACT_D, "sq1", d, 1)
                        act.activation(sq[:, :], x3[:, 1 - par, r, :], ACT.Square, scale=D ** -0.5, accum_out=ssD[:, r:r + 1]).then_inc(act_d, 1)
                    act.wait_ge(dve_d, at(DVE_D, "ev1", d))
                    past(act, pe_d, PE_D, "v3", d, 1)
                    act.activation(hD_hi[:, :, :], hD[:, :, :], ACT.Copy).then_inc(act_d, 1)

                def d_u(n):
                    act.wait_ge(pe_d, at(PE_D, f"g{n}", d))
                    if n == 0:
                        act.wait_ge(pool_d, at(POOL_D, "rs", d))
                    if n >= 2:
                        act.wait_ge(dve_d, at(DVE_D, f"h{n - 2}", d))
                    else:
                        past(act, dve_d, DVE_D, f"h{n + 2}", d, 1)
                    act.activation(gl[:, n % 2, :], bank[6][:, :], ACT.Gelu, scale=rsD[:, 1, n // 2:n // 2 + 1]).then_inc(act_d, 1)

                def d_qt(r):
                    act.wait_ge(pe_d, at(PE_D, f"qt{r}", d))
                    if r:
                        act.wait_ge(pe_d, at(PE_D, "y0", d))
                    else:
                        past(act, pe_d, PE_D, "y1", d, 1)
                    act.activation(qT[:, :, :].rearrange("p k n -> p (k n)"), bank[7][:, :].bitcast(BF16), ACT.Copy).then_inc(act_d, 1)

                for stage, what, n in slices:
                    if stage == "A":
                        if what == "down":
                            a_down()
                        elif what == "ht":
                            a_ht()
                        elif what == "q":
                            a_parts("q", bank[4], q_hi, bq, qh_out)
                        elif what == "k":
                            a_parts("k", bank[5], k_hi, bk, kh_out)
                        elif what == "v":
                            a_v()
                    elif stage == "B" and what == "t":
                        b_t(n)
                    elif stage == "C":
                        if what == "ot":
                            c_ot()
                        elif what == "ht":
                            c_ht()
                        elif what == "f":
                            c_f(n)
                    elif stage == "D":
                        if what == "xt":
                            d_xt()
                        elif what == "u":
                            d_u(n)
                        elif what == "qt":
                            d_qt(n)

            turns(act, turn)

        @block.vector
        def _(dve):
            def bcast(col, n):
                return col.unsqueeze(2).to_broadcast([P, col.shape[1], n])

            def z(i):
                return zb[:, i]

            done = [0]

            def step(ins):
                ins.then_inc(prep, 1)
                done[0] += 1

            def after_last():
                dve.wait_ge(prep, done[0])

            mm4 = bank[4][:, 0:KT * NB].rearrange("p (k n) -> p k n", k=KT)
            mm5 = bank[5][:, 0:KT * NB].rearrange("p (k n) -> p k n", k=KT)
            dve.wait_ge(small_in, 16)
            dve.wait_ge(pre_pe, 1)
            step(dve.tensor_tensor(z(0), mm4, bcast(bt1, NB), ALU.add))
            dve.wait_ge(pre_act, 1)
            step(dve.tensor_scalar(z(1), z(1), 1.0, None, ALU.add))
            after_last()
            step(dve.reciprocal(z(1), z(1)))
            after_last()
            step(dve.tensor_tensor(s1[:, :, :], z(0), z(1), ALU.mult))
            dve.wait_ge(pre_pe, 2)
            step(dve.tensor_tensor(z(2), mm5, bcast(bt2, NB), ALU.add))
            dve.wait_ge(side_in, 16)
            after_last()
            step(dve.tensor_tensor(z(2), z(2), side[:, :, :], ALU.add))
            dve.wait_ge(pre_act, 2)
            step(dve.tensor_scalar(z(3), z(3), 1.0, None, ALU.add))
            after_last()
            step(dve.reciprocal(z(3), z(3)))
            after_last()
            step(dve.tensor_tensor(s2[:, :, :], z(2), z(3), ALU.mult))
            dve.wait_ge(pre_pe, 3)
            step(dve.tensor_tensor(mod[:, :, :], bank[6][:, 0:8 * NB].rearrange("p (k n) -> p k n", k=8), bcast(bc_t[:, 0:8], NB), ALU.add))
            dve.wait_ge(pre_pe, 4)
            step(dve.tensor_scalar(scale3[:, :, :].rearrange("p k n -> p (k n)"), bank[7][:, 0:KT * NB], 1.0, None, ALU.add))
            lin_b, w, bias, b_o, b_f2 = (row_t[0:NB, i * D:(i + 1) * D] for i in range(5))
            dve.wait_ge(row_in, 16)
            dve.wait_ge(pre_pe, 5)
            step(dve.tensor_tensor(tb[:, 5, :], bank[4][0:NB, 0:D], lin_b, ALU.add))
            dve.wait_ge(pre_pe, 6)
            step(dve.tensor_tensor(tb[:, 2:4, :].rearrange("p a b -> p (a b)"), bank[5][0:NB, :], row_t[0:NB, 5 * D:7 * D], ALU.add))
            dve.wait_ge(pre_pe, 7)
            step(dve.tensor_tensor(tb[:, 7, :], bank[6][0:NB, 0:D], b_o, ALU.add))
            dve.wait_ge(pre_act, 3)
            step(dve.tensor_tensor(tb[:, 5, :], tb[:, 6, :], bias, ALU.add))
            after_last()
            step(dve.tensor_tensor(tb[:, 5, :], tb[:, 5, :], w, ALU.mult))
            after_last()
            step(dve.tensor_tensor(tb[:, 0, :], tb[:, 5, :], bias, ALU.add))
            step(dve.tensor_tensor(tb[:, 1, :], tb[:, 7, :], tb[:, 2, :], ALU.mult))
            step(dve.tensor_tensor(tb[:, 4, :], tb[:, 3, :], b_f2, ALU.mult))
            step(dve.tensor_copy(bu_t[:, :], row_t[:, 7 * D:8 * D]))
            step(dve.tensor_tensor(w2_t[:, :], row_t[:, D:2 * D], row_t[:, D:2 * D], ALU.mult))
            dve.wait_ge(base_in, 16)
            step(dve.scalar_tensor_tensor(base_t[:, 0], base_t[:, 1], DELTA, base_t[:, 0], ALU.mult, ALU.add))
            step(dve.tensor_copy(identb[:, :], ident))
            assert done[0] == len(PREP)

            def split_weight(n):
                name, _, hi, lo, first, width = WPARTS[n]
                src = stg[:, n % 2, 0:width]
                hi_f, lo_f = (w_[:, :, :].rearrange("p k n -> p (k n)")[:, first:first + width] for w_ in (hi, lo))
                dve.wait_ge(w_in[n % 2], 16 * (n // 2 + 2))
                if name == "up0":
                    dve.wait_ge(rows_out, 16)
                dve.tensor_copy(hi_f, src).then_inc(split, 1)
                dve.wait_ge(split, 2 * n + 1)
                dve.tensor_tensor(lo_f, src, hi_f.bitcast(F32), ALU.subtract).then_inc(split, 1)

            with dve.Fori(0, NCH // 4) as i:
                for s in (1, 3):
                    dve.wait_ge(hyp_mm, i * 4 + (s + 1))
                    dve.tensor_copy(raw_flat[:, bass.ds(i * (4 * HALF) + s * HALF, HALF)], bank[s][:, :]).then_inc(raw_dve, 1)
            dve.wait_ge(raw_act, NCH // 2)
            dve.wait_ge(raw_dve, NCH // 2)
            dve.wait_ge(prep, len(PREP))
            with dve.Fori(0, NB) as b:
                dve.scalar_tensor_tensor(
                    curall[:, bass.ds(b, 1), 0:D].rearrange("p o (t n) -> p n (o t)", t=KT),
                    raw[:, :, bass.ds(b, 1)].rearrange("p (n t) o -> p n (t o)", t=KT), DELTA,
                    base_t[:, 0, 0, :].rearrange("p (n t) -> p n t", t=KT), ALU.mult, ALU.add).then_inc(cur_done, 1)
                dve.scalar_tensor_tensor(
                    curall[:, bass.ds(b, 1), D:2 * D].rearrange("p o n -> p (o n)"),
                    raw[:, :, bass.ds(b + NB, 1)].rearrange("p n o -> p (n o)"), DELTA, base_t[:, 0, 1, :],
                    ALU.mult, ALU.add).then_inc(cur_done, 1)
            for n in range(len(WPARTS)):
                split_weight(n)
            dwn = stg[:, 0, :]
            dve.wait_ge(w_in[0], 16 * 4)
            dve.tensor_reduce(wsum[:, 0:1], dwn, AX.X, ALU.add, apply_absolute_value=True).then_inc(split, 1)
            dve.wait_ge(pre_pe, len(PRE_PE))
            dve.tensor_scalar(wmean[:, 0:1], bank[7][:, 0:1], 1.0 / (D * FF), Q_MIN, ALU.mult, ALU.max).then_inc(split, 1)
            dve.wait_ge(split, at(SPLIT, "mean", 0))
            dve.reciprocal(wmean[:, 1:2], wmean[:, 0:1]).then_inc(split, 1)
            dve.wait_ge(split, at(SPLIT, "inv", 0))
            dve.tensor_scalar(dwn, dwn, wmean[:, 1:2], ROUND, ALU.mult, ALU.add).then_inc(split, 1)
            dve.wait_ge(split, at(SPLIT, "wround", 0))
            dve.tensor_scalar(dwn, dwn, -ROUND, 1.0, ALU.add, ALU.min).then_inc(split, 1)
            dve.wait_ge(split, at(SPLIT, "wclip", 0))
            dve.tensor_scalar(wq3[:, :, :].rearrange("p k n -> p (k n)"), dwn, -1.0, None, ALU.max).then_inc(split, 1)
            dve.wait_ge(cur_out, 16)
            dve.wait_ge(rows_out, 16)

            def turn(t, par, slices):
                a, b, c, d = t, t - 1, t - 2, t - 3

                def stats(src, st, mv, sem_, steps, names, batch):
                    values = [at(steps, names[r], batch) for r in range(RT)]
                    values = [v if isinstance(v, int) else dve.to_reg(v) for v in values]
                    for r in range(RT):
                        dve.bn_stats(st[:, r, :], src[:, r, :]).then_inc(sem_, 1)
                    for r in range(RT):
                        dve.wait_ge(prep, len(PREP))
                        dve.wait_ge(sem_, values[r])
                        dve.bn_aggr(mv[:, r, :], st[:, r, :]).then_inc(sem_, 1)

                def normalise(buf, mv, rs, sem_):
                    for r in range(RT):
                        dve.tensor_scalar(buf[:, r, :], buf[:, r, :], mv[:, r, 0:1], rs[:, 1, r:r + 1],
                                          ALU.subtract, ALU.mult).then_inc(sem_, 1)

                def a_up():
                    dve.wait_ge(pe_a, at(PE_A, "up", a))
                    dve.wait_ge(pool_a, at(POOL_A, "xbu", a))
                    past(dve, pe_a, PE_A, "ht", a, 1)
                    past(dve, pool_a, POOL_A, "rs1", a, 1)
                    dve.tensor_tensor(x0[:, :, :].rearrange("p r n -> p (r n)"), bank[4][:, :],
                                      x_t[:, :, :].rearrange("p r n -> p (r n)"), ALU.add).then_inc(dve_a, 1)
                    dve.wait_ge(dve_a, at(DVE_A, "x0", a))
                    stats(x0, stA, mvA, dve_a, DVE_A, ("st0", "st1"), a)

                def a_n0():
                    dve.wait_ge(pool_a, at(POOL_A, "rs0", a))
                    normalise(x0, mvA, rsA, dve_a)

                def a_ln():
                    dve.wait_ge(pool_a, at(POOL_A, "x1", a))
                    stats(x0, stA, mvA, dve_a, DVE_A, ("st2", "st3"), a)

                def a_n1():
                    dve.wait_ge(pool_a, at(POOL_A, "rs1", a))
                    normalise(x0, mvA, rsA, dve_a)

                def a_ht():
                    dve.wait_ge(pe_a, at(PE_A, "ht", a))
                    past(dve, act_a, ACT_A, "hi", a, 1)
                    past(dve, dve_a, DVE_A, "lo", a, 1)
                    for k in range(KT):
                        dve.tensor_scalar(hA[:, k, :], bank[4][:, k * L:(k + 1) * L], mod[:, k, bass.ds(a, 1)],
                                          mod[:, 2 + k, bass.ds(a, 1)], ALU.mult, ALU.add).then_inc(dve_a, 1)
                    dve.wait_ge(act_a, at(ACT_A, "hi", a))
                    past(dve, pe_a, PE_A, "v", a, 1)
                    dve.tensor_tensor(hA_lo[:, :, :], hA[:, :, :], hA_hi[:, :, :].bitcast(F32), ALU.subtract).then_inc(dve_a, 1)

                def a_parts(what, src, hi, lo, bias, outs):
                    dve.wait_ge(act_a, at(ACT_A, f"{what}hi1", a))
                    if not isinstance(a, int) or a >= 1:
                        dve.wait_ge(outs, 16 * a)
                    for m in range(2):
                        dve.scalar_tensor_tensor(lo[:, m, :], src[:, m * L:(m + 1) * L], bias[:, m:m + 1], hi[:, m, :].bitcast(F32),
                                                 ALU.add, ALU.subtract).then_inc(dve_a, 1)

                def b_s(u):
                    col = 4 * (u % 2) + 2 * ((u % 4) // 2)
                    dve.wait_ge(pe_s, at(PE_S, f"s{u}", b))
                    if u % 4 == 0:
                        if u >= 8:
                            dve.wait_ge(pe_m, at(PE_M, f"m{u // 4 - 2}", b))
                        else:
                            past(dve, pe_m, PE_M, f"m{u // 4 + 2}", b, 1)
                    dve.tensor_reduce(nmax[:, (u // 4) % 2, col:col + 2], bank[0][:, :].rearrange("p (r n) -> p r n", r=RT),
                                      AX.X, ALU.max, negate=True).then_inc(dve_s, 1)

                def b_m(g):
                    dve.wait_ge(pe_m, at(PE_M, f"m{g}", b))
                    if g >= 2:
                        dve.wait_ge(mx_in[g - 2], 64 * b + 64)
                    elif not isinstance(b, int) or b >= 1:
                        dve.wait_ge(mx_in[g + 2], 64 * b)
                    dve.tensor_copy(m_hi[:, g % 2, :], bank[0][0:8, 0:P]).then_inc(dve_m, 1)
                    dve.wait_ge(dve_m, at(DVE_M, f"hi{g}", b))
                    dve.tensor_tensor(m_lo[:, g % 2, :], bank[0][0:8, 0:P], m_hi[:, g % 2, :].bitcast(F32), ALU.subtract).then_inc(dve_m, 1)

                def b_o(h):
                    if h % 8 != 7:
                        return
                    n = h // 8
                    dve.wait_ge(pe_o, at(PE_O, f"o{h}", b))
                    if n:
                        dve.wait_ge(dve_o, at(DVE_O, "norm0", b))
                    else:
                        past(dve, dve_o, DVE_O, "norm1", b, 1)
                        past(dve, pe_c, PE_C, "ot", b, 1)
                    acc = bank[3][:, 0:RT * 8 * (DH + 1)].rearrange("p (h e) -> p h e", e=DH + 1)
                    dve.reciprocal(rec[:, :, :].rearrange("p r h -> p (r h)").unsqueeze(2), acc[:, :, DH:DH + 1]).then_inc(dve_o, 1)
                    dve.wait_ge(dve_o, at(DVE_O, f"rec{n}", b))
                    dve.tensor_tensor(o_t[:, :, n * P:(n + 1) * P].rearrange("p r (h e) -> p r h e", e=DH),
                                      acc[:, :, 0:DH].rearrange("p (r h) e -> p r h e", r=RT),
                                      rec[:, :, :].unsqueeze(3).to_broadcast([P, RT, 8, DH]), ALU.mult).then_inc(dve_o, 1)

                def over_rows(row):
                    return row.unsqueeze(1).to_broadcast([P, RT, D])

                def c_proj():
                    dve.wait_ge(pe_c, at(PE_C, "proj", c))
                    dve.wait_ge(tC_in, 16 * c + 16)
                    past(dve, pe_c, PE_C, "ht", c, 1)
                    past(dve, pool_c, POOL_C, "rs", c, 1)
                    dve.tensor_tensor(xc[:, :, :], bank[5][:, :].rearrange("p (r n) -> p r n", r=RT), over_rows(tC[:, 0, :]),
                                      ALU.mult).then_inc(dve_c, 1)

                def c_ln():
                    dve.wait_ge(pool_c, at(POOL_C, "x2", c))
                    stats(xc, stC, mvC, dve_c, DVE_C, ("st0", "st1"), c)

                def c_n1():
                    dve.wait_ge(pool_c, at(POOL_C, "rs", c))
                    dve.wait_ge(pool_c, at(POOL_C, "xr", c))
                    normalise(xc, mvC, rsC, dve_c)

                def c_ht():
                    dve.wait_ge(pe_c, at(PE_C, "ht", c))
                    past(dve, act_c, ACT_C, "hi", c, 1)
                    past(dve, dve_c, DVE_C, "lo", c, 1)
                    for k in range(KT):
                        dve.tensor_scalar(hC[:, k, :], bank[5][:, k * L:(k + 1) * L], mod[:, 4 + k, bass.ds(c, 1)],
                                          mod[:, 6 + k, bass.ds(c, 1)], ALU.mult, ALU.add).then_inc(dve_c, 1)
                    dve.wait_ge(act_c, at(ACT_C, "hi", c))
                    past(dve, pe_c, PE_C, "f3", c, 1)
                    dve.tensor_tensor(hC_lo[:, :, :], hC[:, :, :], hC_hi[:, :, :].bitcast(F32), ALU.subtract).then_inc(dve_c, 1)

                def c_g(n):
                    if n != 3:
                        return
                    dve.wait_ge(pe_c, at(PE_C, "y", c))
                    past(dve, dve_d, DVE_D, "y1", c, 2)
                    dve.tensor_tensor(x3[:, par, :, :], bank[5][:, :].rearrange("p (r n) -> p r n", r=RT), over_rows(tC[:, 1, :]),
                                      ALU.mult).then_inc(dve_c, 1)

                def d_xt():
                    dve.wait_ge(pe_d, at(PE_D, "xt", d))
                    past(dve, act_d, ACT_D, "hi", d, 1)
                    past(dve, dve_d, DVE_D, "lo", d, 1)
                    for k in range(KT):
                        dve.tensor_scalar(hD[:, k, :], bank[6][:, k * L:(k + 1) * L], scale3[:, k, bass.ds(d, 1)], None,
                                          ALU.mult).then_inc(dve_d, 1)
                    dve.wait_ge(act_d, at(ACT_D, "hi", d))
                    past(dve, pe_d, PE_D, "v3", d, 1)
                    dve.tensor_tensor(hD_lo[:, :, :], hD[:, :, :], hD_hi[:, :, :].bitcast(F32), ALU.subtract).then_inc(dve_d, 1)

                def d_u(n):
                    dve.wait_ge(pe_d, at(PE_D, f"v{n}", d))
                    dve.wait_ge(act_d, at(ACT_D, f"gelu{n}", d))
                    if n == 2:
                        dve.wait_ge(dve_d, at(DVE_D, "rb0", d))
                    elif n == 0:
                        past(dve, dve_d, DVE_D, "rb1", d, 1)
                    dve.scalar_tensor_tensor(hd[:, (n % 2) * HALF:(n % 2 + 1) * HALF], bank[7][:, :], rsD[:, 1, n // 2:n // 2 + 1],
                                             gl[:, n % 2, :], ALU.mult, ALU.mult).then_inc(dve_d, 1)

                def d_quant(r):
                    top, size, inv, back = (am[:, r, i:i + 1] for i in range(4))
                    dve.wait_ge(dve_d, at(DVE_D, f"h{2 * r + 1}", d))
                    dve.tensor_reduce(top, hd[:, :], AX.X, ALU.max, apply_absolute_value=True).then_inc(dve_d, 1)
                    dve.wait_ge(dve_d, at(DVE_D, f"amax{r}", d))
                    dve.tensor_scalar(size, top, Q_MIN, 1.0 / 127.0, ALU.max, ALU.mult).then_inc(dve_d, 1)
                    dve.wait_ge(dve_d, at(DVE_D, f"step{r}", d))
                    dve.reciprocal(inv, size).then_inc(dve_d, 1)
                    dve.tensor_tensor(back, size, wmean[:, 0:1], ALU.mult).then_inc(dve_d, 1)
                    dve.wait_ge(dve_d, at(DVE_D, f"inv{r}", d))
                    dve.tensor_scalar(hd[:, :], hd[:, :], inv, ROUND, ALU.mult, ALU.add).then_inc(dve_d, 1)
                    dve.wait_ge(dve_d, at(DVE_D, f"ra{r}", d))
                    past(dve, pe_d, PE_D, f"qt{r}", d, 1)
                    dve.tensor_scalar(qi[:, r, :], hd[:, :], -ROUND, 127.0, ALU.add, ALU.min).then_inc(dve_d, 1)

                def d_y(r):
                    dve.wait_ge(pe_d, at(PE_D, f"y{r}", d))
                    dve.wait_ge(dve_d, at(DVE_D, f"back{r}", d))
                    if not isinstance(d, int) or d >= 1:
                        dve.wait_ge(y_out[r], 16 * d)
                    dve.scalar_tensor_tensor(ys[:, r, :], bank[6][:, 0:D], am[:, r, 3:4], x3[:, 1 - par, r, :], ALU.mult, ALU.add).then_inc(dve_d, 1)

                for stage, what, n in slices:
                    if stage == "A":
                        if what == "up":
                            a_up()
                        elif what == "n0":
                            a_n0()
                        elif what == "ln":
                            a_ln()
                        elif what == "n1":
                            a_n1()
                        elif what == "ht":
                            a_ht()
                        elif what == "q":
                            a_parts("q", bank[4], q_hi, q_lo, bq, ql_out)
                        elif what == "k":
                            a_parts("k", bank[5], k_hi, k_lo, bk, kl_out)
                    elif stage == "B":
                        if what == "s":
                            b_s(n)
                        elif what == "m":
                            b_m(n)
                        elif what == "o":
                            b_o(n)
                    elif stage == "C":
                        if what == "proj":
                            c_proj()
                        elif what == "ln":
                            c_ln()
                        elif what == "n1":
                            c_n1()
                        elif what == "ht":
                            c_ht()
                        elif what == "g":
                            c_g(n)
                    else:
                        if what == "xt":
                            d_xt()
                        elif what == "u":
                            d_u(n)
                        elif what == "quant":
                            d_quant(n)
                        elif what == "y":
                            d_y(n)

            turns(dve, turn)

        @block.gpsimd
        def _(pool):
            pool.memset(condbd[:, :], 0.0).then_inc(cond_clear, 1)
            pool.dma_start(row_t[:, :], rows.to_broadcast([P, 8 * D])).then_inc(row_in, 16)
            pool.dma_start(wo[:, :, :].rearrange("p k n -> p (k n)"), w_o).then_inc(wo_in, 16)
            for k in range(KT):
                pool.dma_start(stg[:, k, 0:6 * D], cols[:, 736 + k * 6 * D:736 + (k + 1) * 6 * D]).then_inc(w_in[k], 16)
            pool.dma_start(wf2[:, :, :].rearrange("p k n -> p (k n)"), w_f2).then_inc(wf2_in, 16)
            pool.memset(ones[:, :], 1.0).then_inc(ones_set, 1)
            pool.memset(half_neg[:, :], -0.5).then_inc(zero, 1)
            pool.memset(eps_ln[:, :], EPS_LN).then_inc(zero, 1)
            pool.memset(eps_rms[:, :], EPS_RMS).then_inc(zero, 1)
            for n, lo in enumerate((32, 96)):
                pool.wait_ge(zero, 3 + n)
                pool.memset(Kp[lo:lo + 32, :, :, :].bitcast(F32), 1.0).then_inc(zero, 1)
            pool.wait_ge(zero, 5)
            pool.memset(Va[:, :, :, :, DH:DH + 1], 1.0).then_inc(zero, 1)
            for n, (_, src, _, _, first, width) in enumerate(WPARTS):
                if n < 2:
                    pool.wait_ge(pre_pe, PRE_PE.index("a12") + 1)
                else:
                    pool.wait_ge(split, 2 * (n - 1))
                pool.dma_start(stg[:, n % 2, 0:width], src[:, first:first + width]).then_inc(w_in[n % 2], 16)
            pool.wait_ge(split, at(SPLIT, "up0_lo", 0))
            pool.dma_start(stg[:, 0, :], w_down).then_inc(w_in[0], 16)
            pool.wait_ge(split, len(SPLIT))
            pool.wait_ge(cur_out, 16)
            pool.wait_ge(rows_out, 16)
            pool.wait_ge(pre_pe, len(PRE_PE))
            pool.wait_ge(zero, 6)

            def turn(t, par, slices):
                a, b, c, d = t, t - 1, t - 2, t - 3

                def rstd(src, rs, eps, sem_, steps, names, batch):
                    pool.tensor_tensor(rs[:, 0, :], src, eps[:, :], ALU.add).then_inc(sem_, 1)
                    pool.wait_ge(sem_, at(steps, names, batch))
                    pool.tensor_tensor(rs[:, 1, :], rs[:, 0, :], half_neg[:, :], ALU.pow).then_inc(sem_, 1)

                def over_rows(row):
                    return row.unsqueeze(1).to_broadcast([P, RT, D])

                def a_down():
                    pool.wait_ge(x_in, 16 * a + 16)
                    pool.tensor_tensor(x_t[:, :, :], x_t[:, :, :], over_rows(bu_t[:, :]), ALU.add).then_inc(pool_a, 1)

                def a_up():
                    pool.wait_ge(dve_a, at(DVE_A, "ag1", a))
                    past(pool, dve_a, DVE_A, "n3", a, 1)
                    rstd(mvA[:, :, 1], rsA, eps_ln, pool_a, POOL_A, "ve0", a)

                def a_n0():
                    pool.wait_ge(dve_a, at(DVE_A, "n1", a))
                    pool.tensor_tensor(x0[:, :, :], x0[:, :, :], over_rows(w2_t[:, :]), ALU.mult).then_inc(pool_a, 1)
                    pool.wait_ge(pool_a, at(POOL_A, "w2", a))
                    pool.wait_ge(tA_in, 16 * a + 16)
                    pool.tensor_tensor(x0[:, :, :], x0[:, :, :], over_rows(tA[:, 0, :]), ALU.add).then_inc(pool_a, 1)
                    pool.wait_ge(pool_a, at(POOL_A, "x1", a))
                    past(pool, pool_c, POOL_C, "x2", a, 2)
                    pool.tensor_tensor(xr[:, par, :, :], x0[:, :, :], over_rows(tA[:, 1, :]), ALU.add).then_inc(pool_a, 1)

                def a_ln():
                    pool.wait_ge(dve_a, at(DVE_A, "ag3", a))
                    rstd(mvA[:, :, 1], rsA, eps_ln, pool_a, POOL_A, "ve1", a)

                def c_proj():
                    pool.wait_ge(dve_c, at(DVE_C, "gate1", c))
                    pool.tensor_tensor(xc[:, :, :], xc[:, :, :], xr[:, par, :, :], ALU.add).then_inc(pool_c, 1)
                    pool.wait_ge(pool_c, at(POOL_C, "x2", c))
                    pool.wait_ge(tC_in, 16 * c + 16)
                    past(pool, pool_c, POOL_C, "x3", c, 1)
                    pool.tensor_tensor(xcr[:, :, :], xc[:, :, :], over_rows(tC[:, 2, :]), ALU.add).then_inc(pool_c, 1)

                def c_ln():
                    pool.wait_ge(dve_c, at(DVE_C, "ag1", c))
                    past(pool, dve_c, DVE_C, "n1", c, 1)
                    rstd(mvC[:, :, 1], rsC, eps_ln, pool_c, POOL_C, "ve", c)

                def c_g(n):
                    if n == 3:
                        pool.wait_ge(dve_c, at(DVE_C, "gate2", c))
                        pool.tensor_tensor(x3[:, par, :, :], x3[:, par, :, :], xcr[:, :, :], ALU.add).then_inc(pool_c, 1)

                def d_xt():
                    pool.wait_ge(act_d, at(ACT_D, "sq1", d))
                    past(pool, act_d, ACT_D, "gelu3", d, 1)
                    past(pool, dve_d, DVE_D, "h3", d, 1)
                    rstd(ssD[:, :], rsD, eps_rms, pool_d, POOL_D, "ve", d)

                for stage, what, n in slices:
                    if stage == "A":
                        if what == "down":
                            a_down()
                        elif what == "up":
                            a_up()
                        elif what == "n0":
                            a_n0()
                        elif what == "ln":
                            a_ln()
                    elif stage == "C":
                        if what == "proj":
                            c_proj()
                        elif what == "ln":
                            c_ln()
                        elif what == "g":
                            c_g(n)
                    elif stage == "D" and what == "xt":
                        d_xt()

            turns(pool, turn)


def kernel(x, cond_256, fside_BxS_0, L0_cond_Wd, L0_cond_bd, L0_cond_Wu, L0_cond_bu, L0_cond_Wdd, L0_cond_bdd, L0_cond_Wdu,
           L0_cond_bdu, L1_cond_weight, L1_cond_bias, L1_cond_lin_w, L1_cond_lin_b, L2_cond_W_t1, L2_cond_b_t1, L2_cond_W_t2,
           L2_cond_b_t2, L2_cond_W_c, L2_cond_b_c, L2_cond_W_qkv, L2_cond_b_qkv, L2_cond_W_o, L2_cond_b_o, L2_cond_W_f1,
           L2_cond_b_f1, L2_cond_W_f2, L2_cond_b_f2, L3_cond_norm_w, L3_cond_up_w, L3_cond_down_w):
    import numpy as np
    import concourse.bacc as bacc
    from concourse.bass_utils import run_bass_kernel_spmd

    c = np.ascontiguousarray
    arr = np.asarray
    x = arr(x)

    def tiles(w):
        return c(w.reshape(-1, P, w.shape[1]).transpose(1, 0, 2).reshape(P, -1))

    def col(v):
        return v.reshape(-1, P).T

    heads = np.arange(D).reshape(4, 2, 2, DH).transpose(1, 2, 0, 3).reshape(-1)
    wqkv = arr(L2_cond_W_qkv).T
    bqkv = arr(L2_cond_b_qkv)
    wqkv = np.concatenate([wqkv[:, 0:D][:, heads], wqkv[:, D:2 * D][:, heads], wqkv[:, 2 * D:]], 1)
    wd, bdd = arr(L0_cond_Wd), arr(L0_cond_bdd).reshape(BN, D)
    wu, bdu = arr(L0_cond_Wu), arr(L0_cond_bdu).reshape(D, BN)

    def by_part(w):
        return w.reshape(BN, KT, P).transpose(2, 0, 1).reshape(P, -1)

    arrays = {
        "xT": c(x.reshape(NB, L, KT, P).transpose(0, 3, 2, 1)),
        "x": c(x.reshape(NB, RT, P, D).transpose(0, 2, 1, 3)),
        "hyper": c(np.concatenate([arr(L0_cond_Wdd).T, arr(L0_cond_Wdu).T], 0)),
        "base": c(np.concatenate([by_part(wd), wu.T, by_part(bdd), bdu.T], 1)),
        "cols": c(np.concatenate([
            np.eye(P, dtype=np.float32), col(arr(L2_cond_b_t1)), col(arr(L2_cond_b_t2)), col(arr(L2_cond_b_c)),
            col(arr(L0_cond_bd)), col(bqkv[0:D][heads]), col(bqkv[D:2 * D][heads]), col(bqkv[2 * D:]), col(arr(L2_cond_b_f1)),
            np.zeros((P, 192 - 159), np.float32), tiles(arr(fside_BxS_0).T), tiles(arr(L2_cond_W_t2).T),
            tiles(arr(L2_cond_W_c).T)], 1)),
        "k64": c(np.concatenate([arr(cond_256).T, arr(L2_cond_W_t1).T, arr(L1_cond_lin_w).T, arr(L3_cond_norm_w).T], 1)),
        "rows": c(np.concatenate([arr(v).reshape(-1) for v in (
            L1_cond_lin_b, L1_cond_weight, L1_cond_bias, L2_cond_b_o, L2_cond_b_f2, arr(L2_cond_b_c)[4 * D:], L0_cond_bu)])[None, :]),
        "w_qkv": tiles(wqkv),
        "w_o": tiles(arr(L2_cond_W_o).T),
        "w_f1": tiles(arr(L2_cond_W_f1).T),
        "w_f2": tiles(arr(L2_cond_W_f2).T),
        "w_up": tiles(arr(L3_cond_up_w).T),
        "w_down": tiles(arr(L3_cond_down_w).T),
    }
    nc = bacc.Bacc("TRN2", target_bir_lowering=False, num_devices=1)
    ins = [nc.dram_tensor(f"in_{n}", a.shape, mybir.dt.from_np(a.dtype), kind="ExternalInput").ap() for n, a in arrays.items()]
    out = nc.dram_tensor("out_y", (NB, L, D), F32, kind="ExternalOutput").ap()
    rows_scratch = nc.dram_tensor("rows_scratch", (NB, 5, D), F32, kind="Internal").ap()
    cur_scratch = nc.dram_tensor("cur_scratch", (NB, P, 2 * D), F32, kind="Internal").ap()
    qk_scratch = nc.dram_tensor("qk_scratch", (4, P, 2 * L), F32, kind="Internal").ap()
    cond_seq_kernel(nc, *ins, out, rows_scratch, cur_scratch, qk_scratch)
    r = run_bass_kernel_spmd(nc, [{f"in_{n}": a for n, a in arrays.items()}], core_ids=[0])
    return r.results[0]["out_y"]
```

```python
from contextlib import ExitStack

import concourse.bass as bass
from concourse import mybir

F32 = mybir.dt.float32
F32R = mybir.dt.float32r
BF16 = mybir.dt.bfloat16
ALU = mybir.AluOpType
ACT = mybir.ActivationFunctionType
AX = mybir.AxisListType

P = 128
NB = 16
L = 256
D = 256
BN = 128
HC = 64
NH = 16
DH = D // NH
FF = 1024
RT = L // P
KT = D // P
FT = FF // P
NCH = 16
CHC = BN * D // NCH
HALF = 512
DELTA = 0.1
EPS_LN = 1e-5
EPS_RMS = 1e-6
Q_MIN = 1e-5
ROUND = 1.5 * 2.0 ** 23
KQ = 3 * DH
KM = KQ + 2

PE_A = ["down", "up", "ht", "q", "k", "v"]
PE_S = [f"s{u}" for u in range(NH)]
PE_M = [f"m{g}" for g in range(4)]
PE_T = [f"t{h}" for h in range(NH)]
PE_O = [f"o{h}" for h in range(NH)]
PE_C = ["ot", "proj", "ht", "f0", "f1", "f2", "f3", "y"]
PE_D = ["xt", "g0", "v0", "g1", "v1", "g2", "v2", "g3", "v3", "qt0", "y0", "qt1", "y1"]
ACT_A = ["relu", "ev0", "ev1", "hi", "qhi0", "qhi1", "khi0", "khi1", "v"]
ACT_T = [f"exp{h}" for h in range(NH)]
ACT_C = ["ot", "ev0", "ev1", "hi"] + [f"gelu{m}" for m in range(FT)]
ACT_D = ["sq0", "sq1", "ev0", "ev1", "hi", "gelu0", "gelu1", "gelu2", "gelu3", "qt0", "qt1"]
DVE_A = ["x0", "st0", "st1", "ag0", "ag1", "n0", "n1", "st2", "st3", "ag2", "ag3", "n2", "n3",
         "qlo0", "qlo1", "klo0", "klo1"]
DVE_S = [f"max{u}" for u in range(NH)]
DVE_M = [f"{part}{g}" for g in range(4) for part in ("hi", "lo")]
DVE_O = ["rec0", "norm0", "rec1", "norm1"]
DVE_C = ["gate1", "st0", "st1", "ag0", "ag1", "n0", "n1", "gate2"]
DVE_D = ["h0", "h1", "amax0", "step0", "inv0", "back0", "ra0", "rb0",
         "h2", "h3", "amax1", "step1", "inv1", "back1", "ra1", "rb1", "y0", "y1"]
POOL_A = ["xbu", "ve0", "rs0", "w2", "x1", "xr", "ve1", "rs1", "lo"]
POOL_C = ["x2", "xr", "ve", "rs", "lo", "x3"]
POOL_D = ["ve", "rs", "lo"]


def at(steps, name, b):
    return b * len(steps) + (steps.index(name) + 1)


SP_ORDER = """
    C.ot B.m0 B.m1 B.m2 A.k D.y0 D.y1 B.m3 A.load
""".split()
PE_ORDER = """
    B.s0 A.down C.ot A.up C.proj B.s1 D.u0 B.s2 B.s3 D.u1 C.ht B.m0 D.u2 B.s4 B.s5 A.ht C.f0 C.f1 C.f2 B.s6 A.q B.s7 C.f3
    B.t0 B.m1 D.u3 B.s8 B.t1 B.o0 B.t2 B.s9 B.t3 B.o1 B.s10 A.k B.s11 B.t4 B.o2 A.v B.m2 B.o3 B.o4 B.t5 B.s12 B.t6 C.g0 B.o5
    B.s13 D.qt0 C.g1 D.y0 B.t7 B.o6 B.s14 B.o7 B.t8 D.qt1 B.s15 B.t9 C.g2 B.t10 B.m3 D.y1 C.g3 B.o8 B.t11 B.o9 B.o10 B.o11
    B.t12 C.xt B.t13 B.o12 B.t14 B.t15 B.o13 B.o14 B.o15
""".split()
ACT_ORDER = """
    A.down C.ot D.u0 D.u1 C.ht D.u2 A.ht C.f0 C.f1 C.f2 C.f3 B.t0 B.t1 A.q B.t2 B.t3 D.u3 B.t4 A.k B.t5 D.qt0 B.t6 B.t7
    D.qt1 B.t8 B.t9 B.t10 B.t11 B.t12 B.t13 A.v B.t14 B.t15 C.xt
""".split()
DVE_ORDER = """
    B.s0 A.up C.proj B.s1 A.lna C.ln B.s2 D.u0 B.s3 C.lnb D.u1 A.ln B.m0 A.lnb D.quant0 B.s4 B.s5 D.u2 B.s6 B.s7 B.m1 B.s8
    B.s9 B.s10 A.q B.s11 B.m2 A.k D.u3 B.s12 B.s13 D.quant1 B.s14 D.y0 B.o7 B.s15 D.y1 B.m3 C.g3 B.o15
""".split()
POOL_ORDER = """
    A.down A.up C.proj C.ln A.lna A.ln C.ht A.ht C.g3 C.xt
""".split()


def order(slices, a, b, c, d):
    on = {"A": a, "B": b, "C": c, "D": d}
    out = []
    for name in slices:
        what = name[2:].rstrip("0123456789")
        if on[name[0]]:
            out.append((name[0], what, int(name[2 + len(what):] or 0)))
    return out


def cond_seq_kernel(nc, xT, x, hyper, base, cols, k64, rows, w_qkv, w_o, w_f1, w_f2, w_up, w_down, out,
                    rows_scratch, cur_scratch, qk_scratch):
    ctx = ExitStack()
    with ctx:
        def sb(name, shape, dt):
            return ctx.enter_context(nc.sbuf_tensor(name, shape, dt))

        def sem(name):
            return ctx.enter_context(nc.semaphore(name))

        wqkv_hi = sb("wqkv_hi", [P, KT, 3 * D], F32R)
        wqkv_lo = sb("wqkv_lo", [P, KT, 3 * D], F32R)
        wf1_hi = sb("wf1_hi", [P, KT, FF], F32R)
        wf1_lo = sb("wf1_lo", [P, KT, FF], F32R)
        wup_hi = sb("wup_hi", [P, KT, 2 * FF], F32R)
        wup_lo_at = nc.sbuf_base
        wup_lo = sb("wup_lo", [P, KT, 2 * FF], F32R)
        wo = sb("wo", [P, KT, D], F32)
        wf2 = sb("wf2", [P, FT, D], F32)
        wq3 = sb("wq3", [P, FT, D], BF16)
        small = sb("small", [P, 192], F32)
        ident = small[:, 0:128]
        bt1, bt2, bc_t = small[:, 128:130], small[:, 130:132], small[:, 132:144]
        bd, bq, bk, bv, bf1 = small[:, 144:145], small[:, 145:147], small[:, 147:149], small[:, 149:151], small[:, 151:159]
        identb = sb("identb", [P, P], BF16)
        bu_t = sb("bu_t", [P, D], F32)
        w2_t = sb("w2_t", [P, D], F32)
        mod = sb("mod", [P, 8, NB], F32)
        scale3 = sb("scale3", [P, KT, NB], F32)
        wmean = sb("wmean", [P, 2], F32)
        half_neg = sb("half_neg", [P, RT], F32)
        eps_ln = sb("eps_ln", [P, RT], F32)
        eps_rms = sb("eps_rms", [P, RT], F32)
        Kp = sb("Kp", [P, 2, NH // 2, L], F32R)
        Va = sb("Va", [P, 2, RT, NH, DH + 1], F32)
        xT_t = sb("xT_t", [P, KT, L], F32)
        x_t = sb("x_t", [P, RT, D], F32)
        cur = sb("cur", [P, 2 * D], F32)
        tA = sb("tA", [P, 2, D], F32)
        stage_at = nc.sbuf_base
        Qp = sb("Qp", [P, 2, NH // 2, L], F32R)
        tC = sb("tC", [P, 3, D], F32)
        dn = sb("dn", [P, L], F32)
        x0 = sb("x0", [P, RT, D], F32)
        xr = sb("xr", [P, 2, RT, D], F32)
        hA = sb("hA", [P, KT, L], F32)
        hA_hi = sb("hA_hi", [P, KT, L], F32R)
        hA_lo = sb("hA_lo", [P, KT, L], F32R)
        q_hi = sb("q_hi", [P, 2, L], F32R)
        q_lo = sb("q_lo", [P, 2, L], F32R)
        k_hi = sb("k_hi", [P, 2, L], F32R)
        k_lo = sb("k_lo", [P, 2, L], F32R)
        stA = sb("stA", [P, RT, 6], F32)
        mvA = sb("mvA", [P, RT, 2], F32)
        rsA = sb("rsA", [P, 2, RT], F32)
        nmax = sb("nmax", [P, 2, 8], F32)
        m_hi = sb("m_hi", [8, 2, P], F32R)
        m_lo = sb("m_lo", [8, 2, P], F32R)
        Pr = sb("Pr", [P, 3, 2 * L], F32)
        rec = sb("rec", [P, RT, 8], F32)
        o_t = sb("o_t", [P, RT, D], F32)
        oT = sb("oT", [P, KT, L], F32)
        xc = sb("xc", [P, RT, D], F32)
        xcr = sb("xcr", [P, RT, D], F32)
        stC = sb("stC", [P, RT, 6], F32)
        mvC = sb("mvC", [P, RT, 2], F32)
        rsC = sb("rsC", [P, 2, RT], F32)
        hC = sb("hC", [P, KT, L], F32)
        hC_hi = sb("hC_hi", [P, KT, L], F32R)
        hC_lo = sb("hC_lo", [P, KT, L], F32R)
        G = sb("G", [P, FT, L], F32)
        x3 = sb("x3", [P, 2, RT, D], F32)
        hD = sb("hD", [P, KT, L], F32)
        hD_hi = sb("hD_hi", [P, KT, L], F32R)
        hD_lo = sb("hD_lo", [P, KT, L], F32R)
        sq = sb("sq", [P, D], F32)
        ssD = sb("ssD", [P, RT], F32)
        rsD = sb("rsD", [P, 2, RT], F32)
        gl = sb("gl", [P, 2, HALF], F32)
        hd = sb("hd", [P, FF], F32)
        am = sb("am", [P, RT, 4], F32)
        qi = sb("qi", [P, RT, FF], BF16)
        qT = sb("qT", [P, FT, P], BF16)
        ys = sb("ys", [P, RT, D], F32)

        def staged(name, shape, dt, words):
            nonlocal stage_at
            t = nc.alloc_sbuf_tensor_at(name, shape, dt, offset=stage_at)
            stage_at += 4 * words
            return t

        hyp = staged("hyp", [P, 4, CHC], F32, 4 * CHC)
        raw = staged("raw", [P, 2 * P, 2 * NB], F32, 64 * P)
        stg = staged("stg", [P, 2, 2048], F32, 4096)
        base_t = staged("base_t", [P, 2, 2, D], F32, 4 * D)
        condbd = staged("condbd", [P, 2 * NB], F32, 2 * NB)
        c64 = staged("c64", [HC, NB + 3 * D], F32, NB + 3 * D)
        wt2 = staged("wt2", [P, KT, D], F32, KT * D)
        side = staged("side", [P, KT, NB], F32, KT * NB)
        zb = staged("zb", [P, 4, KT, NB], F32, 4 * KT * NB)
        s1 = staged("s1", [P, KT, NB], F32, KT * NB)
        s2 = staged("s2", [P, KT, NB], F32, KT * NB)
        ones = staged("ones", [P, P], F32, P)
        wsum = staged("wsum", [P, 4], F32, 4)
        assert stage_at <= nc.sbuf_base, (stage_at, nc.sbuf_base)
        row_t = nc.alloc_sbuf_tensor_at("row_t", [P, 8 * D], F32, offset=wup_lo_at)
        tb = nc.alloc_sbuf_tensor_at("tb", [NB, 8, D], F32, offset=wup_lo_at + 32 * D)
        raw_flat = raw[:, :, :].rearrange("p j n -> p (j n)")
        curall = hyp[:, :, :].rearrange("p s c -> p (s c)").rearrange("p (b n) -> p b n", b=NB)

        bank = [ctx.enter_context(nc.psum_tensor(f"bank{i}", [P, HALF], F32)) for i in range(8)]
        F_BANK = [bank[5], bank[1], bank[2], bank[5]]
        S_BANK = [bank[3 * (u % 2)] if u < 8 else bank[0] for u in range(NH)]

        pe_a, pe_s, pe_m, pe_t, pe_o, pe_c, pe_d = (sem(f"pe_{s}") for s in "asmtocd")
        act_a, act_t, act_c, act_d = (sem(f"act_{s}") for s in "atcd")
        dve_a, dve_s, dve_m, dve_o, dve_c, dve_d = (sem(f"dve_{s}") for s in "asmocd")
        pool_a, pool_c, pool_d = (sem(f"pool_{s}") for s in "acd")
        xT_in, x_in, cur_in, tA_in, tC_in = (sem(f"{s}_in") for s in ("xT", "x", "cur", "tA", "tC"))
        qh_out, ql_out, kh_out, kl_out = (sem(f"{s}_out") for s in ("qh", "ql", "kh", "kl"))
        qp_in, kp_in = sem("qp_in"), sem("kp_in")
        mx_in = [sem(f"mx_in{g}") for g in range(4)]
        y_out = [sem(f"y_out{r}") for r in range(RT)]
        hyp_in = [sem(f"hyp_in{i}") for i in range(4)]
        hyp_mm, raw_act, raw_dve = sem("hyp_mm"), sem("raw_act"), sem("raw_dve")
        small_in, k64_in, side_in, row_in, wt2_in, wc_in, cond_in, base_in = (
            sem(f"{s}_in") for s in ("small", "k64", "side", "row", "wt2", "wc", "cond", "base"))
        w_in = [sem("w_in0"), sem("w_in1")]
        wo_in, wf2_in = sem("wo_in"), sem("wf2_in")
        split, prep, zero, cur_done, rows_done = sem("split"), sem("prep"), sem("zero"), sem("cur_done"), sem("rows_done")
        pre_pe, pre_act, ones_set = sem("pre_pe"), sem("pre_act"), sem("ones_set")
        rows_out, cur_out, cond_clear = sem("rows_out"), sem("cur_out"), sem("cond_clear")

        block = ctx.enter_context(nc.Block())

        PREP = ["z1", "d1", "r1", "s1", "z2a", "z2", "d2", "r2", "s2", "mod", "scale3", "tbl", "a12", "co",
                "tb1", "tb2", "c", "a1co", "a2bf", "bu", "w2", "base", "identb"]
        PRE_PE = ["t1", "t2", "mod", "s3", "tb", "a12", "co", "wsum"]
        SPLIT = ["qkv_hi", "qkv_lo", "f1_hi", "f1_lo", "up0_hi", "up0_lo", "up1_hi", "up1_lo",
                 "wabs", "mean", "inv", "wround", "wclip", "wq"]
        WPARTS = [("qkv", w_qkv, wqkv_hi, wqkv_lo, 0, KT * 3 * D), ("f1", w_f1, wf1_hi, wf1_lo, 0, KT * FF),
                  ("up0", w_up, wup_hi, wup_lo, 0, 2048), ("up1", w_up, wup_hi, wup_lo, 2048, 2048)]

        def turns(eng, body, slices):
            def alone(t):
                body(t, t % 2, order(slices, t < NB, 1 <= t <= NB, 2 <= t <= NB + 1, t >= 3))

            for t in range(4):
                alone(t)
            with eng.Fori(4, NB - 2, 2) as t:
                body(t, 0, order(slices, True, True, True, True))
                body(t + 1, 1, order(slices, True, True, True, True))
            for t in range(NB - 2, NB + 3):
                alone(t)

        def past(eng, sem_, steps, name, b, back):
            if not isinstance(b, int) or b >= back:
                eng.wait_ge(sem_, at(steps, name, b - back))

        @block.sync
        def _(sp):
            sp.dma_start(c64[:, :], k64).then_inc(k64_in, 16)
            sp.wait_ge(cond_clear, 1)
            sp.dma_start(condbd[0:HC, 0:NB], k64[:, 0:NB]).then_inc(cond_in, 16)
            sp.dma_start(condbd[HC:P, NB:2 * NB], k64[:, 0:NB]).then_inc(cond_in, 16)
            sp.dma_start(small[:, 0:192], cols[:, 0:192]).then_inc(small_in, 16)
            sp.dma_start(side[:, :, :].rearrange("p a b -> p (a b)"), cols[:, 192:224]).then_inc(side_in, 16)
            sp.dma_start(wt2[:, :, :].rearrange("p a b -> p (a b)"), cols[:, 224:736]).then_inc(wt2_in, 16)
            sp.dma_start(base_t[:, :, :, :].rearrange("p a b c -> p (a b c)"), base).then_inc(base_in, 16)
            for s in range(4):
                sp.dma_start(hyp[:, s, :], hyper[:, s * CHC:(s + 1) * CHC]).then_inc(hyp_in[s], 16)
            with sp.Fori(1, NCH // 4) as i:
                for s in range(4):
                    sp.wait_ge(hyp_mm, i * 4 + (s - 3))
                    sp.dma_start(hyp[:, s, :], hyper[:, bass.ds(i * (4 * CHC) + s * CHC, CHC)]).then_inc(hyp_in[s], 16)
            sp.wait_ge(cur_done, 2 * NB)
            sp.dma_start(cur_scratch.rearrange("b p n -> p b n"), curall).then_inc(cur_out, 16)
            sp.wait_ge(prep, PREP.index("a2bf") + 1)
            sp.dma_start(rows_scratch, tb[:, 0:5, :]).then_inc(rows_out, 16)
            sp.wait_ge(cur_out, 16)
            sp.wait_ge(rows_out, 16)

            def load_a(b):
                sp.dma_start(xT_t[:, :, :], xT[bass.ds(b, 1)].rearrange("o p a b -> (o p) a b")).then_inc(xT_in, 16)
                sp.dma_start(x_t[:, :, :], x[bass.ds(b, 1)].rearrange("o p a b -> (o p) a b")).then_inc(x_in, 16)
                sp.dma_start(cur[:, :], cur_scratch[bass.ds(b, 1)].rearrange("o p n -> (o p) n")).then_inc(cur_in, 16)
                sp.dma_start(tA[:, :, :].rearrange("p a b -> p (a b)"),
                             rows_scratch[bass.ds(b, 1), 0:2, :].rearrange("o a b -> o (a b)").to_broadcast([P, 2 * D])).then_inc(tA_in, 16)

            load_a(0)
            sp.wait_ge(split, len(SPLIT))

            def turn(t, par, slices):
                a, b, c = t, t - 1, t - 2
                index = lambda v: v if isinstance(v, int) else sp.snap(v)
                upcoming, gated, stored = index(t + 1), index(t - 2), index(t - 3)
                value = lambda v: v if isinstance(v, int) else sp.to_reg(v)
                xT_used, x_read, x_used = value(at(PE_A, "up", a)), value(at(POOL_A, "xr", a)), value(at(DVE_A, "x0", a))
                for stage, what, n in slices:
                    if (stage, what) == ("A", "k"):
                        for parts, ready_hi, ready_lo, outs, w in (
                                ((q_hi, q_lo), "qhi1", "qlo1", (qh_out, ql_out), 0),
                                ((k_hi, k_lo), "khi1", "klo1", (kh_out, kl_out), 2)):
                            sp.wait_ge(act_a, at(ACT_A, ready_hi, a))
                            sp.dma_start(qk_scratch[w], parts[0][:, :, :].rearrange("p a b -> p (a b)").bitcast(F32)).then_inc(outs[0], 16)
                            sp.wait_ge(dve_a, at(DVE_A, ready_lo, a))
                            sp.dma_start(qk_scratch[w + 1], parts[1][:, :, :].rearrange("p a b -> p (a b)").bitcast(F32)).then_inc(outs[1], 16)
                        for outs, dst, srcs, arrived in (((qh_out, ql_out), Qp, (0, 0, 1), qp_in), ((kh_out, kl_out), Kp, (2, 3, 2), kp_in)):
                            sp.wait_ge(outs[0], 16 * a + 16)
                            sp.wait_ge(outs[1], 16 * a + 16)
                            if not isinstance(a, int) or a >= 2:
                                sp.wait_ge(pe_t, at(PE_T, "t15", a - 2))
                            for half in range(2):
                                for r, w in enumerate(srcs):
                                    sp.dma_start(
                                        dst[64 * half + DH * r:64 * half + DH * (r + 1), par, :, :].rearrange("d (j c) n -> d j (c n)", j=4).bitcast(F32),
                                        qk_scratch[w, 64 * half:64 * half + 64, :].rearrange("(j d) n -> d j n", j=4)).then_inc(arrived, 16)
                    elif (stage, what) == ("B", "m"):
                        sp.wait_ge(dve_m, at(DVE_M, f"lo{n}", b))
                        for half in range(2):
                            for row, part in ((KQ, m_hi), (KQ + 1, m_lo)):
                                src = part[4 * half:4 * half + 4, n % 2, :]
                                sp.dma_start(Qp[64 * half + row:64 * half + row + 1, 1 - par, 2 * n:2 * n + 2, :].bitcast(F32),
                                             src.bitcast(F32)).then_inc(mx_in[n], 16)
                    elif (stage, what) == ("A", "load"):
                        if not isinstance(t, int) or t + 1 < NB:
                            sp.wait_ge(pe_a, xT_used)
                            sp.wait_ge(pool_a, x_read)
                            sp.wait_ge(dve_a, x_used)
                            load_a(upcoming)
                    elif (stage, what) == ("C", "ot"):
                        past(sp, dve_c, DVE_C, "gate2", c, 1)
                        past(sp, pool_c, POOL_C, "xr", c, 1)
                        sp.dma_start(tC[:, :, :].rearrange("p a b -> p (a b)"),
                                     rows_scratch[bass.ds(gated, 1), 2:5, :].rearrange("o a b -> o (a b)").to_broadcast([P, 3 * D])).then_inc(tC_in, 16)
                    elif (stage, what) == ("D", "y"):
                        sp.wait_ge(dve_d, at(DVE_D, f"y{n}", t - 3))
                        sp.dma_start(out[bass.ds(stored, 1), n * P:(n + 1) * P, :].rearrange("o p n -> (o p) n"), ys[:, n, :]).then_inc(y_out[n], 16)

            turns(sp, turn, SP_ORDER)
            for r in range(RT):
                sp.wait_ge(y_out[r], 16 * NB)

        @block.tensor
        def _(pe):
            def three(dst, lhs, rhs, first, last):
                for i, (l, r) in enumerate(((lhs[0], rhs[0]), (lhs[1], rhs[0]), (lhs[0], rhs[1]))):
                    mm = pe.matmul(dst, l, r, start=first and i == 0, stop=last and i == 2)
                return mm

            pe.wait_ge(k64_in, 16)
            for m in range(KT):
                mm = pe.matmul(bank[4][:, m * NB:(m + 1) * NB], c64[:, NB + m * P:NB + (m + 1) * P], c64[:, 0:NB], start=True, stop=True)
            mm.then_inc(pre_pe, 1)
            pe.wait_ge(wt2_in, 16)
            pe.wait_ge(prep, PREP.index("s1") + 1)
            for m in range(KT):
                for k in range(KT):
                    mm = pe.matmul(bank[5][:, m * NB:(m + 1) * NB], wt2[:, k, m * P:(m + 1) * P], s1[:, k, :], start=k == 0, stop=k == KT - 1)
            mm.then_inc(pre_pe, 1)
            pe.wait_ge(w_in[0], 16)
            pe.wait_ge(w_in[1], 16)
            pe.wait_ge(prep, PREP.index("s2") + 1)
            wc = stg[:, :, 0:6 * D]
            for m in range(8):
                for k in range(KT):
                    mm = pe.matmul(bank[6][:, m * NB:(m + 1) * NB], wc[:, k, m * P:(m + 1) * P], s2[:, k, :], start=k == 0, stop=k == KT - 1)
            mm.then_inc(pre_pe, 1)
            for m in range(KT):
                mm = pe.matmul(bank[7][:, m * NB:(m + 1) * NB], c64[:, NB + 2 * D + m * P:NB + 2 * D + (m + 1) * P], c64[:, 0:NB], start=True, stop=True)
            mm.then_inc(pre_pe, 1)
            pe.wait_ge(prep, PREP.index("z1") + 1)
            pe.matmul(bank[4][0:NB, 0:D], c64[:, 0:NB], c64[:, NB + D:NB + 2 * D], start=True, stop=True).then_inc(pre_pe, 1)
            pe.wait_ge(prep, PREP.index("z2a") + 1)
            for k in range(KT):
                mm = pe.matmul(bank[5][0:NB, 0:2 * D], s2[:, k, :], wc[:, k, 4 * D:6 * D], start=k == 0, stop=k == KT - 1)
            mm.then_inc(pre_pe, 1)
            pe.wait_ge(wo_in, 16)
            pe.wait_ge(small_in, 16)
            pe.wait_ge(prep, PREP.index("mod") + 1)
            for k in range(KT):
                mm = pe.matmul(bank[6][0:NB, 0:D], bv[:, k:k + 1].to_broadcast([P, NB]), wo[:, k, :], start=k == 0, stop=k == KT - 1)
            mm.then_inc(pre_pe, 1)
            pe.wait_ge(cond_in, 32)

            def generate(i):
                for s in range(4):
                    pe.wait_ge(hyp_in[s], i * 16 + 16)
                    if not isinstance(i, int):
                        pe.wait_ge(raw_act if s % 2 == 0 else raw_dve, i * 2 + (s // 2 - 1))
                    for j in range(CHC // P):
                        mm = pe.matmul(bank[s][:, j * 2 * NB:(j + 1) * 2 * NB], hyp[:, s, j * P:(j + 1) * P], condbd[:, :], start=True, stop=True)
                    mm.then_inc(hyp_mm, 1)

            generate(0)
            with pe.Fori(1, NCH // 4) as i:
                generate(i)
            pe.wait_ge(split, at(SPLIT, "wabs", 0))
            pe.wait_ge(ones_set, 1)
            pe.wait_ge(prep, PREP.index("scale3") + 1)
            pe.matmul(bank[7][:, 0:1], ones[:, :], wsum[:, 0:1], start=True, stop=True).then_inc(pre_pe, 1)
            pe.wait_ge(prep, len(PREP))
            pe.wait_ge(split, len(SPLIT))

            def turn(t, par, slices):
                a, b, c, d = t, t - 1, t - 2, t - 3
                with_c = any(s[0] == "C" for s in slices)
                with_b = any(s[0] == "B" for s in slices)

                def a_down():
                    pe.wait_ge(xT_in, 16 * a + 16)
                    pe.wait_ge(cur_in, 16 * a + 16)
                    past(pe, act_a, ACT_A, "v", a, 1)
                    for k in range(KT):
                        mm = pe.matmul(bank[4][:, 0:L], cur[:, k * BN:(k + 1) * BN], xT_t[:, k, :], start=k == 0, stop=k == KT - 1)
                    mm.then_inc(pe_a, 1)

                def a_up():
                    pe.wait_ge(act_a, at(ACT_A, "relu", a))
                    for r in range(RT):
                        mm = pe.matmul(bank[4][:, r * D:(r + 1) * D], dn[:, r * P:(r + 1) * P], cur[:, D:2 * D], start=True, stop=True)
                    mm.then_inc(pe_a, 1)

                def a_ht():
                    pe.wait_ge(dve_a, at(DVE_A, "n3", a))
                    for k in range(KT):
                        for r in range(RT):
                            mm = pe.transpose(bank[4][:, k * L + r * P:k * L + (r + 1) * P], x0[:, r, k * P:(k + 1) * P], ident)
                    mm.then_inc(pe_a, 1)

                def a_q():
                    pe.wait_ge(pool_a, at(POOL_A, "lo", a))
                    for m in range(2):
                        for k in range(KT):
                            mm = three(bank[4][:, m * L:(m + 1) * L], (wqkv_hi[:, k, m * P:(m + 1) * P], wqkv_lo[:, k, m * P:(m + 1) * P]),
                                       (hA_hi[:, k, :], hA_lo[:, k, :]), k == 0, k == KT - 1)
                    mm.then_inc(pe_a, 1)

                def a_k():
                    if with_c:
                        pe.wait_ge(act_c, at(ACT_C, "gelu7", c))
                    else:
                        past(pe, dve_a, DVE_A, "klo1", a, 1)
                    for m in range(2):
                        for k in range(KT):
                            mm = three(bank[5][:, m * L:(m + 1) * L], (wqkv_hi[:, k, D + m * P:D + (m + 1) * P], wqkv_lo[:, k, D + m * P:D + (m + 1) * P]),
                                       (hA_hi[:, k, :], hA_lo[:, k, :]), k == 0, k == KT - 1)
                    mm.then_inc(pe_a, 1)

                def a_v():
                    pe.wait_ge(dve_a, at(DVE_A, "qlo1", a))
                    for r in range(RT):
                        for k in range(KT):
                            mm = three(bank[4][:, r * D:(r + 1) * D], (hA_hi[:, k, r * P:(r + 1) * P], hA_lo[:, k, r * P:(r + 1) * P]),
                                       (wqkv_hi[:, k, 2 * D:3 * D], wqkv_lo[:, k, 2 * D:3 * D]), k == 0, k == KT - 1)
                    mm.then_inc(pe_a, 1)

                def b_s(u):
                    lo, g = 64 * (u % 2), u // 2
                    if u == 0:
                        pe.wait_ge(qp_in, 96 * b + 96)
                        pe.wait_ge(kp_in, 96 * b + 96)
                        past(pe, dve_m, DVE_M, "lo3", b, 1)
                    elif u == 1:
                        past(pe, dve_o, DVE_O, "norm1", b, 1)
                    elif u % 4 == 0:
                        pe.wait_ge(dve_m, at(DVE_M, f"lo{u // 4 - 1}", b))
                    else:
                        pe.wait_ge(dve_s, at(DVE_S, f"max{u - 2 if u < 8 else u - 1}", b))
                    for r in range(RT):
                        mm = pe.matmul(S_BANK[u][:, r * L:(r + 1) * L], Qp[lo:lo + KQ, 1 - par, g, r * P:(r + 1) * P],
                                       Kp[lo:lo + KQ, 1 - par, g, :], start=True, stop=True)
                    mm.then_inc(pe_s, 1)

                def b_m(g):
                    pe.wait_ge(dve_s, at(DVE_S, f"max{4 * g + 3}", b))
                    pe.transpose(bank[0][0:8, 0:P], nmax[:, g % 2, :], ident).then_inc(pe_m, 1)

                def b_t(h):
                    lo, g = 64 * (h % 2), h // 2
                    dst = bank[1 + h % 2]
                    if h % 4 == 0:
                        pe.wait_ge(mx_in[h // 4], 64 * b + 64)
                    if h >= 2:
                        pe.wait_ge(act_t, at(ACT_T, f"exp{h - 2}", b))
                    elif with_c:
                        pe.wait_ge(act_c, at(ACT_C, f"gelu{3 + 2 * h}", c))
                    else:
                        past(pe, act_t, ACT_T, f"exp{h + 14}", b, 1)
                    for k in range(RT):
                        mm = pe.matmul(dst[:, k * L:(k + 1) * L], Kp[lo:lo + KM, 1 - par, g, k * P:(k + 1) * P],
                                       Qp[lo:lo + KM, 1 - par, g, :], start=True, stop=True)
                    mm.then_inc(pe_t, 1)

                def b_o(h):
                    if h == 0:
                        pe.wait_ge(act_a, at(ACT_A, "v", b))
                        pe.wait_ge(dve_s, at(DVE_S, "max7", b))
                    if h == 8:
                        pe.wait_ge(dve_o, at(DVE_O, "norm0", b))
                    pe.wait_ge(act_t, at(ACT_T, f"exp{h}", b))
                    for r in range(RT):
                        for k in range(RT):
                            col = (r * 8 + h % 8) * (DH + 1)
                            mm = pe.matmul(bank[3][:, col:col + DH + 1], Pr[:, h % 3, k * L + r * P:k * L + (r + 1) * P],
                                           Va[:, 1 - par, k, h, :], start=k == 0, stop=k == RT - 1)
                    mm.then_inc(pe_o, 1)

                def c_ot():
                    pe.wait_ge(dve_o, at(DVE_O, "norm1", c))
                    past(pe, dve_c, DVE_C, "gate2", c, 1)
                    if isinstance(c, int) and c == 0:
                        pe.wait_ge(dve_a, at(DVE_A, "klo1", a - 1))
                    for k in range(KT):
                        for r in range(RT):
                            mm = pe.transpose(bank[5][:, k * L + r * P:k * L + (r + 1) * P], o_t[:, r, k * P:(k + 1) * P], ident)
                    mm.then_inc(pe_c, 1)

                def c_proj():
                    pe.wait_ge(act_c, at(ACT_C, "ot", c))
                    for r in range(RT):
                        for k in range(KT):
                            mm = pe.matmul(bank[5][:, r * D:(r + 1) * D], oT[:, k, r * P:(r + 1) * P], wo[:, k, :], start=k == 0, stop=k == KT - 1)
                    mm.then_inc(pe_c, 1)

                def c_ht():
                    pe.wait_ge(dve_c, at(DVE_C, "n1", c))
                    for k in range(KT):
                        for r in range(RT):
                            mm = pe.transpose(bank[5][:, k * L + r * P:k * L + (r + 1) * P], xc[:, r, k * P:(k + 1) * P], ident)
                    mm.then_inc(pe_c, 1)

                def c_f(n):
                    if n == 0:
                        pe.wait_ge(pool_c, at(POOL_C, "lo", c))
                    if n == 3:
                        pe.wait_ge(act_c, at(ACT_C, "gelu1", c))
                    for m in (2 * n, 2 * n + 1):
                        for k in range(KT):
                            mm = three(F_BANK[n][:, (m % 2) * L:(m % 2 + 1) * L], (wf1_hi[:, k, m * P:(m + 1) * P], wf1_lo[:, k, m * P:(m + 1) * P]),
                                       (hC_hi[:, k, :], hC_lo[:, k, :]), k == 0, k == KT - 1)
                    mm.then_inc(pe_c, 1)

                def c_g(n):
                    r = n // 2
                    if n == 0:
                        pe.wait_ge(act_c, at(ACT_C, "gelu7", c))
                        if not isinstance(a, int) or a < NB:
                            pe.wait_ge(dve_a, at(DVE_A, "klo1", a))
                    for k in range(4 * (n % 2), 4 * (n % 2) + 4):
                        mm = pe.matmul(bank[5][:, r * D:(r + 1) * D], G[:, k, r * P:(r + 1) * P], wf2[:, k, :], start=k == 0, stop=k == FT - 1)
                    if n == 3:
                        mm.then_inc(pe_c, 1)

                def c_xt():
                    pe.wait_ge(pool_c, at(POOL_C, "x3", c))
                    past(pe, dve_d, DVE_D, "y1", c, 1)
                    for k in range(KT):
                        for r in range(RT):
                            mm = pe.transpose(bank[6][:, k * L + r * P:k * L + (r + 1) * P], x3[:, par, r, k * P:(k + 1) * P], ident)
                    mm.then_inc(pe_d, 1)

                def d_u(n):
                    r, col = n // 2, (n % 2) * HALF
                    if n == 0:
                        pe.wait_ge(pool_d, at(POOL_D, "lo", d))
                    else:
                        pe.wait_ge(act_d, at(ACT_D, f"gelu{n - 1}", d))
                    lhs = [(hD_hi[:, k, r * P:(r + 1) * P], hD_lo[:, k, r * P:(r + 1) * P]) for k in range(KT)]
                    for k in range(KT):
                        c0 = FF + col
                        mm = three(bank[6][:, :], lhs[k], (wup_hi[:, k, c0:c0 + HALF], wup_lo[:, k, c0:c0 + HALF]), k == 0, k == KT - 1)
                    mm.then_inc(pe_d, 1)
                    if n == 0:
                        past(pe, act_d, ACT_D, "qt1", d, 1)
                    else:
                        pe.wait_ge(dve_d, at(DVE_D, f"h{n - 1}", d))
                    for k in range(KT):
                        mm = three(bank[7][:, :], lhs[k], (wup_hi[:, k, col:col + HALF], wup_lo[:, k, col:col + HALF]), k == 0, k == KT - 1)
                    mm.then_inc(pe_d, 1)

                def d_qt(r):
                    pe.wait_ge(dve_d, at(DVE_D, "h3" if r == 0 else "rb1", d))
                    if r == 1:
                        pe.wait_ge(act_d, at(ACT_D, "qt0", d))
                    for k in range(FT):
                        mm = pe.transpose(bank[7][:, :].bitcast(BF16)[:, k * P:(k + 1) * P], qi[:, r, k * P:(k + 1) * P], identb[:, :])
                    mm.then_inc(pe_d, 1)

                def d_y(r):
                    pe.wait_ge(act_d, at(ACT_D, f"qt{r}", d))
                    if r == 1:
                        pe.wait_ge(dve_d, at(DVE_D, "y0", d))
                    for k in range(FT):
                        mm = pe.matmul(bank[6][:, 0:D], qT[:, k, :], wq3[:, k, :], start=k == 0, stop=k == FT - 1)
                    mm.then_inc(pe_d, 1)

                for stage, what, n in slices:
                    if stage == "A" and what in ("down", "up", "ht", "q", "k", "v"):
                        {"down": a_down, "up": a_up, "ht": a_ht, "q": a_q, "k": a_k, "v": a_v}[what]()
                    elif stage == "B":
                        {"s": b_s, "m": b_m, "t": b_t, "o": b_o}[what](n)
                    elif stage == "C" and what in ("ot", "proj", "ht", "xt"):
                        {"ot": c_ot, "proj": c_proj, "ht": c_ht, "xt": c_xt}[what]()
                    elif stage == "C" and what in ("f", "g"):
                        {"f": c_f, "g": c_g}[what](n)
                    elif stage == "D" and what in ("u", "qt", "y"):
                        {"u": d_u, "qt": d_qt, "y": d_y}[what](n)

            turns(pe, turn, PE_ORDER)

        @block.scalar
        def _(act):
            act.wait_ge(prep, PREP.index("z1") + 1)
            act.activation(zb[:, 1], zb[:, 0], ACT.Exp, scale=-1.0).then_inc(pre_act, 1)
            act.wait_ge(prep, PREP.index("z2") + 1)
            act.activation(zb[:, 3], zb[:, 2], ACT.Exp, scale=-1.0).then_inc(pre_act, 1)
            act.wait_ge(prep, PREP.index("tbl") + 1)
            act.activation(tb[:, 6, :], tb[:, 5, :], ACT.Tanh).then_inc(pre_act, 1)
            with act.Fori(0, NCH // 4) as i:
                for s in (0, 2):
                    act.wait_ge(hyp_mm, i * 4 + (s + 1))
                    act.activation(raw_flat[:, bass.ds(i * (4 * HALF) + s * HALF, HALF)], bank[s][:, :], ACT.Copy).then_inc(raw_act, 1)
            act.wait_ge(split, len(SPLIT))
            act.wait_ge(cur_out, 16)
            act.wait_ge(rows_out, 16)
            act.wait_ge(pre_pe, len(PRE_PE))

            def turn(t, par, slices):
                a, b, c, d = t, t - 1, t - 2, t - 3

                def a_down():
                    act.wait_ge(pe_a, at(PE_A, "down", a))
                    past(act, pe_a, PE_A, "up", a, 1)
                    act.activation(dn[:, :], bank[4][:, 0:L], ACT.Relu, bias=bd).then_inc(act_a, 1)

                def modulate(dst, src, first, batch, sem_):
                    for k in range(KT):
                        act.activation(dst[:, k, :], src[:, k * L:(k + 1) * L], ACT.Identity, scale=mod[:, first + k, bass.ds(batch, 1)],
                                       bias=mod[:, first + 2 + k, bass.ds(batch, 1)]).then_inc(sem_, 1)

                def a_ht():
                    act.wait_ge(pe_a, at(PE_A, "ht", a))
                    past(act, pool_a, POOL_A, "lo", a, 1)
                    modulate(hA, bank[4], 0, a, act_a)
                    act.wait_ge(act_a, at(ACT_A, "ev1", a))
                    past(act, pe_a, PE_A, "v", a, 1)
                    act.activation(hA_hi[:, :, :], hA[:, :, :], ACT.Copy).then_inc(act_a, 1)

                def a_parts(what, src, dst, bias, outs):
                    act.wait_ge(pe_a, at(PE_A, what, a))
                    if not isinstance(a, int) or a >= 1:
                        act.wait_ge(outs, 16 * a)
                    for m in range(2):
                        act.activation(dst[:, m, :], src[:, m * L:(m + 1) * L], ACT.Identity, bias=bias[:, m:m + 1]).then_inc(act_a, 1)

                def a_v():
                    act.wait_ge(pe_a, at(PE_A, "v", a))
                    past(act, pe_o, PE_O, "o15", a, 2)
                    act.activation(Va[:, par, :, :, 0:DH], bank[4][:, :].rearrange("p (r h e) -> p r h e", r=RT, h=NH),
                                   ACT.Copy).then_inc(act_a, 1)

                def b_t(h):
                    act.wait_ge(pe_t, at(PE_T, f"t{h}", b))
                    if h >= 3:
                        act.wait_ge(pe_o, at(PE_O, f"o{h - 3}", b))
                    else:
                        past(act, pe_o, PE_O, "o15", b, 1)
                    act.activation(Pr[:, h % 3, :], bank[1 + h % 2][:, :], ACT.Exp, scale=DH ** -0.5).then_inc(act_t, 1)

                def c_ot():
                    act.wait_ge(pe_c, at(PE_C, "ot", c))
                    past(act, pe_c, PE_C, "proj", c, 1)
                    act.activation(oT[:, :, :].rearrange("p k n -> p (k n)"), bank[5][:, :], ACT.Copy).then_inc(act_c, 1)

                def c_ht():
                    act.wait_ge(pe_c, at(PE_C, "ht", c))
                    past(act, pool_c, POOL_C, "lo", c, 1)
                    modulate(hC, bank[5], 4, c, act_c)
                    act.wait_ge(act_c, at(ACT_C, "ev1", c))
                    past(act, pe_c, PE_C, "f3", c, 1)
                    act.activation(hC_hi[:, :, :], hC[:, :, :], ACT.Copy).then_inc(act_c, 1)

                def c_f(n):
                    act.wait_ge(pe_c, at(PE_C, f"f{n}", c))
                    past(act, pe_c, PE_C, "y", c, 1)
                    for m in (2 * n, 2 * n + 1):
                        act.activation(G[:, m, :], F_BANK[n][:, (m % 2) * L:(m % 2 + 1) * L], ACT.Gelu_apprx_tanh,
                                       bias=bf1[:, m:m + 1]).then_inc(act_c, 1)

                def c_xt():
                    act.wait_ge(pool_c, at(POOL_C, "x3", c))
                    for r in range(RT):
                        if r:
                            act.wait_ge(act_d, at(ACT_D, "sq0", c))
                        else:
                            past(act, pool_d, POOL_D, "ve", c, 1)
                            past(act, act_d, ACT_D, "sq1", c, 1)
                        act.activation(sq[:, :], x3[:, par, r, :], ACT.Square, scale=D ** -0.5, accum_out=ssD[:, r:r + 1]).then_inc(act_d, 1)
                    act.wait_ge(pe_d, at(PE_D, "xt", c))
                    past(act, pool_d, POOL_D, "lo", c, 1)
                    for k in range(KT):
                        act.activation(hD[:, k, :], bank[6][:, k * L:(k + 1) * L], ACT.Copy, scale=scale3[:, k, bass.ds(c, 1)]).then_inc(act_d, 1)
                    act.wait_ge(act_d, at(ACT_D, "ev1", c))
                    past(act, pe_d, PE_D, "v3", c, 1)
                    act.activation(hD_hi[:, :, :], hD[:, :, :], ACT.Copy).then_inc(act_d, 1)

                def d_u(n):
                    act.wait_ge(pe_d, at(PE_D, f"g{n}", d))
                    if n == 0:
                        act.wait_ge(pool_d, at(POOL_D, "rs", d))
                    if n >= 2:
                        act.wait_ge(dve_d, at(DVE_D, f"h{n - 2}", d))
                    else:
                        past(act, dve_d, DVE_D, f"h{n + 2}", d, 1)
                    act.activation(gl[:, n % 2, :], bank[6][:, :], ACT.Gelu, scale=rsD[:, 1, n // 2:n // 2 + 1]).then_inc(act_d, 1)

                def d_qt(r):
                    act.wait_ge(pe_d, at(PE_D, f"qt{r}", d))
                    if r:
                        act.wait_ge(pe_d, at(PE_D, "y0", d))
                    else:
                        past(act, pe_d, PE_D, "y1", d, 1)
                    act.activation(qT[:, :, :].rearrange("p k n -> p (k n)"), bank[7][:, :].bitcast(BF16), ACT.Copy).then_inc(act_d, 1)

                for stage, what, n in slices:
                    if stage == "A":
                        if what == "down":
                            a_down()
                        elif what == "ht":
                            a_ht()
                        elif what == "q":
                            a_parts("q", bank[4], q_hi, bq, qh_out)
                        elif what == "k":
                            a_parts("k", bank[5], k_hi, bk, kh_out)
                        elif what == "v":
                            a_v()
                    elif stage == "B" and what == "t":
                        b_t(n)
                    elif stage == "C":
                        if what == "ot":
                            c_ot()
                        elif what == "ht":
                            c_ht()
                        elif what == "f":
                            c_f(n)
                        elif what == "xt":
                            c_xt()
                    elif stage == "D":
                        if what == "u":
                            d_u(n)
                        elif what == "qt":
                            d_qt(n)

            turns(act, turn, ACT_ORDER)

        @block.vector
        def _(dve):
            def bcast(col, n):
                return col.unsqueeze(2).to_broadcast([P, col.shape[1], n])

            def z(i):
                return zb[:, i]

            done = [0]

            def step(ins):
                ins.then_inc(prep, 1)
                done[0] += 1

            def after_last():
                dve.wait_ge(prep, done[0])

            mm4 = bank[4][:, 0:KT * NB].rearrange("p (k n) -> p k n", k=KT)
            mm5 = bank[5][:, 0:KT * NB].rearrange("p (k n) -> p k n", k=KT)
            dve.wait_ge(small_in, 16)
            dve.wait_ge(pre_pe, 1)
            step(dve.tensor_tensor(z(0), mm4, bcast(bt1, NB), ALU.add))
            dve.wait_ge(pre_act, 1)
            step(dve.tensor_scalar(z(1), z(1), 1.0, None, ALU.add))
            after_last()
            step(dve.reciprocal(z(1), z(1)))
            after_last()
            step(dve.tensor_tensor(s1[:, :, :], z(0), z(1), ALU.mult))
            dve.wait_ge(pre_pe, 2)
            step(dve.tensor_tensor(z(2), mm5, bcast(bt2, NB), ALU.add))
            dve.wait_ge(side_in, 16)
            after_last()
            step(dve.tensor_tensor(z(2), z(2), side[:, :, :], ALU.add))
            dve.wait_ge(pre_act, 2)
            step(dve.tensor_scalar(z(3), z(3), 1.0, None, ALU.add))
            after_last()
            step(dve.reciprocal(z(3), z(3)))
            after_last()
            step(dve.tensor_tensor(s2[:, :, :], z(2), z(3), ALU.mult))
            dve.wait_ge(pre_pe, 3)
            step(dve.tensor_tensor(mod[:, :, :], bank[6][:, 0:8 * NB].rearrange("p (k n) -> p k n", k=8), bcast(bc_t[:, 0:8], NB), ALU.add))
            dve.wait_ge(pre_pe, 4)
            step(dve.tensor_scalar(scale3[:, :, :].rearrange("p k n -> p (k n)"), bank[7][:, 0:KT * NB], 1.0, None, ALU.add))
            lin_b, w, bias, b_o, b_f2 = (row_t[0:NB, i * D:(i + 1) * D] for i in range(5))
            dve.wait_ge(row_in, 16)
            dve.wait_ge(pre_pe, 5)
            step(dve.tensor_tensor(tb[:, 5, :], bank[4][0:NB, 0:D], lin_b, ALU.add))
            dve.wait_ge(pre_pe, 6)
            step(dve.tensor_tensor(tb[:, 2:4, :].rearrange("p a b -> p (a b)"), bank[5][0:NB, :], row_t[0:NB, 5 * D:7 * D], ALU.add))
            dve.wait_ge(pre_pe, 7)
            step(dve.tensor_tensor(tb[:, 7, :], bank[6][0:NB, 0:D], b_o, ALU.add))
            dve.wait_ge(pre_act, 3)
            step(dve.tensor_tensor(tb[:, 5, :], tb[:, 6, :], bias, ALU.add))
            after_last()
            step(dve.tensor_tensor(tb[:, 5, :], tb[:, 5, :], w, ALU.mult))
            after_last()
            step(dve.tensor_tensor(tb[:, 0, :], tb[:, 5, :], bias, ALU.add))
            step(dve.tensor_tensor(tb[:, 1, :], tb[:, 7, :], tb[:, 2, :], ALU.mult))
            step(dve.tensor_tensor(tb[:, 4, :], tb[:, 3, :], b_f2, ALU.mult))
            step(dve.tensor_copy(bu_t[:, :], row_t[:, 7 * D:8 * D]))
            step(dve.tensor_tensor(w2_t[:, :], row_t[:, D:2 * D], row_t[:, D:2 * D], ALU.mult))
            dve.wait_ge(base_in, 16)
            step(dve.scalar_tensor_tensor(base_t[:, 0], base_t[:, 1], DELTA, base_t[:, 0], ALU.mult, ALU.add))
            step(dve.tensor_copy(identb[:, :], ident))
            assert done[0] == len(PREP)

            def split_weight(n):
                name, _, hi, lo, first, width = WPARTS[n]
                src = stg[:, n % 2, 0:width]
                hi_f, lo_f = (w_[:, :, :].rearrange("p k n -> p (k n)")[:, first:first + width] for w_ in (hi, lo))
                dve.wait_ge(w_in[n % 2], 16 * (n // 2 + 2))
                if name == "up0":
                    dve.wait_ge(rows_out, 16)
                dve.tensor_copy(hi_f, src).then_inc(split, 1)
                dve.wait_ge(split, 2 * n + 1)
                dve.tensor_tensor(lo_f, src, hi_f.bitcast(F32), ALU.subtract).then_inc(split, 1)

            with dve.Fori(0, NCH // 4) as i:
                for s in (1, 3):
                    dve.wait_ge(hyp_mm, i * 4 + (s + 1))
                    dve.tensor_copy(raw_flat[:, bass.ds(i * (4 * HALF) + s * HALF, HALF)], bank[s][:, :]).then_inc(raw_dve, 1)
            dve.wait_ge(raw_act, NCH // 2)
            dve.wait_ge(raw_dve, NCH // 2)
            dve.wait_ge(prep, len(PREP))
            with dve.Fori(0, NB) as b:
                dve.scalar_tensor_tensor(
                    curall[:, bass.ds(b, 1), 0:D].rearrange("p o (t n) -> p n (o t)", t=KT),
                    raw[:, :, bass.ds(b, 1)].rearrange("p (n t) o -> p n (t o)", t=KT), DELTA,
                    base_t[:, 0, 0, :].rearrange("p (n t) -> p n t", t=KT), ALU.mult, ALU.add).then_inc(cur_done, 1)
                dve.scalar_tensor_tensor(
                    curall[:, bass.ds(b, 1), D:2 * D].rearrange("p o n -> p (o n)"),
                    raw[:, :, bass.ds(b + NB, 1)].rearrange("p n o -> p (n o)"), DELTA, base_t[:, 0, 1, :],
                    ALU.mult, ALU.add).then_inc(cur_done, 1)
            for n in range(len(WPARTS)):
                split_weight(n)
            dwn = stg[:, 0, :]
            dve.wait_ge(w_in[0], 16 * 4)
            dve.tensor_reduce(wsum[:, 0:1], dwn, AX.X, ALU.add, apply_absolute_value=True).then_inc(split, 1)
            dve.wait_ge(pre_pe, len(PRE_PE))
            dve.tensor_scalar(wmean[:, 0:1], bank[7][:, 0:1], 1.0 / (D * FF), Q_MIN, ALU.mult, ALU.max).then_inc(split, 1)
            dve.wait_ge(split, at(SPLIT, "mean", 0))
            dve.reciprocal(wmean[:, 1:2], wmean[:, 0:1]).then_inc(split, 1)
            dve.wait_ge(split, at(SPLIT, "inv", 0))
            dve.tensor_scalar(dwn, dwn, wmean[:, 1:2], ROUND, ALU.mult, ALU.add).then_inc(split, 1)
            dve.wait_ge(split, at(SPLIT, "wround", 0))
            dve.tensor_scalar(dwn, dwn, -ROUND, 1.0, ALU.add, ALU.min).then_inc(split, 1)
            dve.wait_ge(split, at(SPLIT, "wclip", 0))
            dve.tensor_scalar(wq3[:, :, :].rearrange("p k n -> p (k n)"), dwn, -1.0, None, ALU.max).then_inc(split, 1)
            dve.wait_ge(cur_out, 16)
            dve.wait_ge(rows_out, 16)

            def turn(t, par, slices):
                a, b, c, d = t, t - 1, t - 2, t - 3

                def stats(src, st, mv, sem_, steps, names, batch):
                    values = [at(steps, names[r], batch) for r in range(RT)]
                    values = [v if isinstance(v, int) else dve.to_reg(v) for v in values]
                    for r in range(RT):
                        dve.bn_stats(st[:, r, :], src[:, r, :]).then_inc(sem_, 1)
                    for r in range(RT):
                        dve.wait_ge(prep, len(PREP))
                        dve.wait_ge(sem_, values[r])
                        dve.bn_aggr(mv[:, r, :], st[:, r, :]).then_inc(sem_, 1)

                def normalise(buf, mv, rs, sem_):
                    for r in range(RT):
                        dve.tensor_scalar(buf[:, r, :], buf[:, r, :], mv[:, r, 0:1], rs[:, 1, r:r + 1],
                                          ALU.subtract, ALU.mult).then_inc(sem_, 1)

                def a_up():
                    dve.wait_ge(pe_a, at(PE_A, "up", a))
                    dve.wait_ge(pool_a, at(POOL_A, "xbu", a))
                    past(dve, pe_a, PE_A, "ht", a, 1)
                    past(dve, pool_a, POOL_A, "rs1", a, 1)
                    dve.tensor_tensor(x0[:, :, :].rearrange("p r n -> p (r n)"), bank[4][:, :],
                                      x_t[:, :, :].rearrange("p r n -> p (r n)"), ALU.add).then_inc(dve_a, 1)
                    dve.wait_ge(dve_a, at(DVE_A, "x0", a))
                    stats(x0, stA, mvA, dve_a, DVE_A, ("st0", "st1"), a)

                def a_n0():
                    dve.wait_ge(pool_a, at(POOL_A, "rs0", a))
                    normalise(x0, mvA, rsA, dve_a)

                def a_ln():
                    dve.wait_ge(pool_a, at(POOL_A, "x1", a))
                    stats(x0, stA, mvA, dve_a, DVE_A, ("st2", "st3"), a)

                def a_n1():
                    dve.wait_ge(pool_a, at(POOL_A, "rs1", a))
                    normalise(x0, mvA, rsA, dve_a)

                def a_parts(what, src, hi, lo, bias, outs):
                    dve.wait_ge(act_a, at(ACT_A, f"{what}hi1", a))
                    if not isinstance(a, int) or a >= 1:
                        dve.wait_ge(outs, 16 * a)
                    for m in range(2):
                        dve.scalar_tensor_tensor(lo[:, m, :], src[:, m * L:(m + 1) * L], bias[:, m:m + 1], hi[:, m, :].bitcast(F32),
                                                 ALU.add, ALU.subtract).then_inc(dve_a, 1)

                def b_s(u):
                    col = 4 * (u % 2) + 2 * ((u % 4) // 2)
                    dve.wait_ge(pe_s, at(PE_S, f"s{u}", b))
                    if u % 4 == 0:
                        if u >= 8:
                            dve.wait_ge(pe_m, at(PE_M, f"m{u // 4 - 2}", b))
                        else:
                            past(dve, pe_m, PE_M, f"m{u // 4 + 2}", b, 1)
                    dve.tensor_reduce(nmax[:, (u // 4) % 2, col:col + 2], S_BANK[u][:, :].rearrange("p (r n) -> p r n", r=RT),
                                      AX.X, ALU.max, negate=True).then_inc(dve_s, 1)

                def b_m(g):
                    dve.wait_ge(pe_m, at(PE_M, f"m{g}", b))
                    if g >= 2:
                        dve.wait_ge(mx_in[g - 2], 64 * b + 64)
                    elif not isinstance(b, int) or b >= 1:
                        dve.wait_ge(mx_in[g + 2], 64 * b)
                    dve.tensor_copy(m_hi[:, g % 2, :], bank[0][0:8, 0:P]).then_inc(dve_m, 1)
                    dve.wait_ge(dve_m, at(DVE_M, f"hi{g}", b))
                    dve.tensor_tensor(m_lo[:, g % 2, :], bank[0][0:8, 0:P], m_hi[:, g % 2, :].bitcast(F32), ALU.subtract).then_inc(dve_m, 1)

                def b_o(h):
                    if h % 8 != 7:
                        return
                    n = h // 8
                    dve.wait_ge(pe_o, at(PE_O, f"o{h}", b))
                    if n:
                        dve.wait_ge(dve_o, at(DVE_O, "norm0", b))
                    else:
                        past(dve, dve_o, DVE_O, "norm1", b, 1)
                        past(dve, pe_c, PE_C, "ot", b, 1)
                    acc = bank[3][:, 0:RT * 8 * (DH + 1)].rearrange("p (h e) -> p h e", e=DH + 1)
                    dve.reciprocal(rec[:, :, :].rearrange("p r h -> p (r h)").unsqueeze(2), acc[:, :, DH:DH + 1]).then_inc(dve_o, 1)
                    dve.wait_ge(dve_o, at(DVE_O, f"rec{n}", b))
                    dve.tensor_tensor(o_t[:, :, n * P:(n + 1) * P].rearrange("p r (h e) -> p r h e", e=DH),
                                      acc[:, :, 0:DH].rearrange("p (r h) e -> p r h e", r=RT),
                                      rec[:, :, :].unsqueeze(3).to_broadcast([P, RT, 8, DH]), ALU.mult).then_inc(dve_o, 1)

                def over_rows(row):
                    return row.unsqueeze(1).to_broadcast([P, RT, D])

                def c_proj():
                    dve.wait_ge(pe_c, at(PE_C, "proj", c))
                    dve.wait_ge(tC_in, 16 * c + 16)
                    past(dve, pe_c, PE_C, "ht", c, 1)
                    past(dve, pool_c, POOL_C, "rs", c, 1)
                    dve.tensor_tensor(xc[:, :, :], bank[5][:, :].rearrange("p (r n) -> p r n", r=RT), over_rows(tC[:, 0, :]),
                                      ALU.mult).then_inc(dve_c, 1)

                def c_ln():
                    dve.wait_ge(pool_c, at(POOL_C, "x2", c))
                    stats(xc, stC, mvC, dve_c, DVE_C, ("st0", "st1"), c)

                def c_n1():
                    dve.wait_ge(pool_c, at(POOL_C, "rs", c))
                    dve.wait_ge(pool_c, at(POOL_C, "xr", c))
                    normalise(xc, mvC, rsC, dve_c)

                def c_g(n):
                    if n != 3:
                        return
                    dve.wait_ge(pe_c, at(PE_C, "y", c))
                    past(dve, dve_d, DVE_D, "y1", c, 2)
                    dve.tensor_tensor(x3[:, par, :, :], bank[5][:, :].rearrange("p (r n) -> p r n", r=RT), over_rows(tC[:, 1, :]),
                                      ALU.mult).then_inc(dve_c, 1)

                def d_u(n):
                    dve.wait_ge(pe_d, at(PE_D, f"v{n}", d))
                    dve.wait_ge(act_d, at(ACT_D, f"gelu{n}", d))
                    if n == 2:
                        dve.wait_ge(dve_d, at(DVE_D, "rb0", d))
                    elif n == 0:
                        past(dve, dve_d, DVE_D, "rb1", d, 1)
                    dve.scalar_tensor_tensor(hd[:, (n % 2) * HALF:(n % 2 + 1) * HALF], bank[7][:, :], rsD[:, 1, n // 2:n // 2 + 1],
                                             gl[:, n % 2, :], ALU.mult, ALU.mult).then_inc(dve_d, 1)

                def d_quant(r):
                    top, size, inv, back = (am[:, r, i:i + 1] for i in range(4))
                    dve.wait_ge(dve_d, at(DVE_D, f"h{2 * r + 1}", d))
                    dve.tensor_reduce(top, hd[:, :], AX.X, ALU.max, apply_absolute_value=True).then_inc(dve_d, 1)
                    dve.wait_ge(dve_d, at(DVE_D, f"amax{r}", d))
                    dve.tensor_scalar(size, top, Q_MIN, 1.0 / 127.0, ALU.max, ALU.mult).then_inc(dve_d, 1)
                    dve.wait_ge(dve_d, at(DVE_D, f"step{r}", d))
                    dve.reciprocal(inv, size).then_inc(dve_d, 1)
                    dve.tensor_tensor(back, size, wmean[:, 0:1], ALU.mult).then_inc(dve_d, 1)
                    dve.wait_ge(dve_d, at(DVE_D, f"inv{r}", d))
                    dve.tensor_scalar(hd[:, :], hd[:, :], inv, ROUND, ALU.mult, ALU.add).then_inc(dve_d, 1)
                    dve.wait_ge(dve_d, at(DVE_D, f"ra{r}", d))
                    past(dve, pe_d, PE_D, f"qt{r}", d, 1)
                    dve.tensor_scalar(qi[:, r, :], hd[:, :], -ROUND, 127.0, ALU.add, ALU.min).then_inc(dve_d, 1)

                def d_y(r):
                    dve.wait_ge(pe_d, at(PE_D, f"y{r}", d))
                    dve.wait_ge(dve_d, at(DVE_D, f"back{r}", d))
                    if not isinstance(d, int) or d >= 1:
                        dve.wait_ge(y_out[r], 16 * d)
                    dve.scalar_tensor_tensor(ys[:, r, :], bank[6][:, 0:D], am[:, r, 3:4], x3[:, 1 - par, r, :], ALU.mult, ALU.add).then_inc(dve_d, 1)

                for stage, what, n in slices:
                    if stage == "A":
                        if what == "up":
                            a_up()
                        elif what == "lna":
                            a_n0()
                        elif what == "ln":
                            a_ln()
                        elif what == "lnb":
                            a_n1()
                        elif what == "q":
                            a_parts("q", bank[4], q_hi, q_lo, bq, ql_out)
                        elif what == "k":
                            a_parts("k", bank[5], k_hi, k_lo, bk, kl_out)
                    elif stage == "B":
                        if what == "s":
                            b_s(n)
                        elif what == "m":
                            b_m(n)
                        elif what == "o":
                            b_o(n)
                    elif stage == "C":
                        if what == "proj":
                            c_proj()
                        elif what == "ln":
                            c_ln()
                        elif what == "lnb":
                            c_n1()
                        elif what == "g":
                            c_g(n)
                    else:
                        if what == "u":
                            d_u(n)
                        elif what == "quant":
                            d_quant(n)
                        elif what == "y":
                            d_y(n)

            turns(dve, turn, DVE_ORDER)

        @block.gpsimd
        def _(pool):
            pool.memset(condbd[:, :], 0.0).then_inc(cond_clear, 1)
            pool.dma_start(row_t[:, :], rows.to_broadcast([P, 8 * D])).then_inc(row_in, 16)
            pool.dma_start(wo[:, :, :].rearrange("p k n -> p (k n)"), w_o).then_inc(wo_in, 16)
            for k in range(KT):
                pool.dma_start(stg[:, k, 0:6 * D], cols[:, 736 + k * 6 * D:736 + (k + 1) * 6 * D]).then_inc(w_in[k], 16)
            pool.dma_start(wf2[:, :, :].rearrange("p k n -> p (k n)"), w_f2).then_inc(wf2_in, 16)
            pool.memset(ones[:, :], 1.0).then_inc(ones_set, 1)
            pool.memset(half_neg[:, :], -0.5).then_inc(zero, 1)
            pool.memset(eps_ln[:, :], EPS_LN).then_inc(zero, 1)
            pool.memset(eps_rms[:, :], EPS_RMS).then_inc(zero, 1)
            for n, lo in enumerate((32, 96)):
                pool.wait_ge(zero, 3 + n)
                pool.memset(Kp[lo:lo + 32, :, :, :].bitcast(F32), 1.0).then_inc(zero, 1)
            pool.wait_ge(zero, 5)
            pool.memset(Va[:, :, :, :, DH:DH + 1], 1.0).then_inc(zero, 1)
            for n, (_, src, _, _, first, width) in enumerate(WPARTS):
                if n < 2:
                    pool.wait_ge(pre_pe, PRE_PE.index("a12") + 1)
                else:
                    pool.wait_ge(split, 2 * (n - 1))
                pool.dma_start(stg[:, n % 2, 0:width], src[:, first:first + width]).then_inc(w_in[n % 2], 16)
            pool.wait_ge(split, at(SPLIT, "up0_lo", 0))
            pool.dma_start(stg[:, 0, :], w_down).then_inc(w_in[0], 16)
            pool.wait_ge(split, len(SPLIT))
            pool.wait_ge(cur_out, 16)
            pool.wait_ge(rows_out, 16)
            pool.wait_ge(pre_pe, len(PRE_PE))
            pool.wait_ge(zero, 6)

            def turn(t, par, slices):
                a, b, c, d = t, t - 1, t - 2, t - 3

                def rstd(src, rs, eps, sem_, steps, names, batch):
                    pool.tensor_tensor(rs[:, 0, :], src, eps[:, :], ALU.add).then_inc(sem_, 1)
                    pool.wait_ge(sem_, at(steps, names, batch))
                    pool.tensor_tensor(rs[:, 1, :], rs[:, 0, :], half_neg[:, :], ALU.pow).then_inc(sem_, 1)

                def over_rows(row):
                    return row.unsqueeze(1).to_broadcast([P, RT, D])

                def a_down():
                    pool.wait_ge(x_in, 16 * a + 16)
                    pool.tensor_tensor(x_t[:, :, :], x_t[:, :, :], over_rows(bu_t[:, :]), ALU.add).then_inc(pool_a, 1)

                def a_up():
                    pool.wait_ge(dve_a, at(DVE_A, "ag1", a))
                    past(pool, dve_a, DVE_A, "n3", a, 1)
                    rstd(mvA[:, :, 1], rsA, eps_ln, pool_a, POOL_A, "ve0", a)

                def a_n0():
                    pool.wait_ge(dve_a, at(DVE_A, "n1", a))
                    pool.tensor_tensor(x0[:, :, :], x0[:, :, :], over_rows(w2_t[:, :]), ALU.mult).then_inc(pool_a, 1)
                    pool.wait_ge(pool_a, at(POOL_A, "w2", a))
                    pool.wait_ge(tA_in, 16 * a + 16)
                    pool.tensor_tensor(x0[:, :, :], x0[:, :, :], over_rows(tA[:, 0, :]), ALU.add).then_inc(pool_a, 1)
                    pool.wait_ge(pool_a, at(POOL_A, "x1", a))
                    past(pool, pool_c, POOL_C, "x2", a, 2)
                    pool.tensor_tensor(xr[:, par, :, :], x0[:, :, :], over_rows(tA[:, 1, :]), ALU.add).then_inc(pool_a, 1)

                def a_ln():
                    pool.wait_ge(dve_a, at(DVE_A, "ag3", a))
                    rstd(mvA[:, :, 1], rsA, eps_ln, pool_a, POOL_A, "ve1", a)

                def low_part(lo, full, hi, sem_):
                    pool.tensor_tensor(lo[:, :, :], full[:, :, :], hi[:, :, :].bitcast(F32), ALU.subtract).then_inc(sem_, 1)

                def a_ht():
                    pool.wait_ge(act_a, at(ACT_A, "hi", a))
                    past(pool, pe_a, PE_A, "v", a, 1)
                    low_part(hA_lo, hA, hA_hi, pool_a)

                def c_ht():
                    pool.wait_ge(act_c, at(ACT_C, "hi", c))
                    past(pool, pe_c, PE_C, "f3", c, 1)
                    low_part(hC_lo, hC, hC_hi, pool_c)

                def c_proj():
                    pool.wait_ge(dve_c, at(DVE_C, "gate1", c))
                    pool.tensor_tensor(xc[:, :, :], xc[:, :, :], xr[:, par, :, :], ALU.add).then_inc(pool_c, 1)
                    pool.wait_ge(pool_c, at(POOL_C, "x2", c))
                    pool.wait_ge(tC_in, 16 * c + 16)
                    past(pool, pool_c, POOL_C, "x3", c, 1)
                    pool.tensor_tensor(xcr[:, :, :], xc[:, :, :], over_rows(tC[:, 2, :]), ALU.add).then_inc(pool_c, 1)

                def c_ln():
                    pool.wait_ge(dve_c, at(DVE_C, "ag1", c))
                    past(pool, dve_c, DVE_C, "n1", c, 1)
                    rstd(mvC[:, :, 1], rsC, eps_ln, pool_c, POOL_C, "ve", c)

                def c_g(n):
                    if n == 3:
                        pool.wait_ge(dve_c, at(DVE_C, "gate2", c))
                        pool.tensor_tensor(x3[:, par, :, :], x3[:, par, :, :], xcr[:, :, :], ALU.add).then_inc(pool_c, 1)

                def c_xt():
                    pool.wait_ge(act_d, at(ACT_D, "sq1", c))
                    past(pool, act_d, ACT_D, "gelu3", c, 1)
                    past(pool, dve_d, DVE_D, "h3", c, 1)
                    rstd(ssD[:, :], rsD, eps_rms, pool_d, POOL_D, "ve", c)
                    pool.wait_ge(act_d, at(ACT_D, "hi", c))
                    past(pool, pe_d, PE_D, "v3", c, 1)
                    low_part(hD_lo, hD, hD_hi, pool_d)

                for stage, what, n in slices:
                    if stage == "A":
                        if what == "down":
                            a_down()
                        elif what == "up":
                            a_up()
                        elif what == "lna":
                            a_n0()
                        elif what == "ln":
                            a_ln()
                        elif what == "ht":
                            a_ht()
                    elif stage == "C":
                        if what == "proj":
                            c_proj()
                        elif what == "ln":
                            c_ln()
                        elif what == "ht":
                            c_ht()
                        elif what == "g":
                            c_g(n)
                        elif what == "xt":
                            c_xt()

            turns(pool, turn, POOL_ORDER)


def kernel(x, cond_256, fside_BxS_0, L0_cond_Wd, L0_cond_bd, L0_cond_Wu, L0_cond_bu, L0_cond_Wdd, L0_cond_bdd, L0_cond_Wdu,
           L0_cond_bdu, L1_cond_weight, L1_cond_bias, L1_cond_lin_w, L1_cond_lin_b, L2_cond_W_t1, L2_cond_b_t1, L2_cond_W_t2,
           L2_cond_b_t2, L2_cond_W_c, L2_cond_b_c, L2_cond_W_qkv, L2_cond_b_qkv, L2_cond_W_o, L2_cond_b_o, L2_cond_W_f1,
           L2_cond_b_f1, L2_cond_W_f2, L2_cond_b_f2, L3_cond_norm_w, L3_cond_up_w, L3_cond_down_w):
    import numpy as np
    import concourse.bacc as bacc
    from concourse.bass_utils import run_bass_kernel_spmd

    c = np.ascontiguousarray
    arr = np.asarray
    x = arr(x)

    def tiles(w):
        return c(w.reshape(-1, P, w.shape[1]).transpose(1, 0, 2).reshape(P, -1))

    def col(v):
        return v.reshape(-1, P).T

    heads = np.arange(D).reshape(4, 2, 2, DH).transpose(1, 2, 0, 3).reshape(-1)
    wqkv = arr(L2_cond_W_qkv).T
    bqkv = arr(L2_cond_b_qkv)
    wqkv = np.concatenate([wqkv[:, 0:D][:, heads], wqkv[:, D:2 * D][:, heads], wqkv[:, 2 * D:]], 1)
    wd, bdd = arr(L0_cond_Wd), arr(L0_cond_bdd).reshape(BN, D)
    wu, bdu = arr(L0_cond_Wu), arr(L0_cond_bdu).reshape(D, BN)

    def by_part(w):
        return w.reshape(BN, KT, P).transpose(2, 0, 1).reshape(P, -1)

    arrays = {
        "xT": c(x.reshape(NB, L, KT, P).transpose(0, 3, 2, 1)),
        "x": c(x.reshape(NB, RT, P, D).transpose(0, 2, 1, 3)),
        "hyper": c(np.concatenate([arr(L0_cond_Wdd).T, arr(L0_cond_Wdu).T], 0)),
        "base": c(np.concatenate([by_part(wd), wu.T, by_part(bdd), bdu.T], 1)),
        "cols": c(np.concatenate([
            np.eye(P, dtype=np.float32), col(arr(L2_cond_b_t1)), col(arr(L2_cond_b_t2)), col(arr(L2_cond_b_c)),
            col(arr(L0_cond_bd)), col(bqkv[0:D][heads]), col(bqkv[D:2 * D][heads]), col(bqkv[2 * D:]), col(arr(L2_cond_b_f1)),
            np.zeros((P, 192 - 159), np.float32), tiles(arr(fside_BxS_0).T), tiles(arr(L2_cond_W_t2).T),
            tiles(arr(L2_cond_W_c).T)], 1)),
        "k64": c(np.concatenate([arr(cond_256).T, arr(L2_cond_W_t1).T, arr(L1_cond_lin_w).T, arr(L3_cond_norm_w).T], 1)),
        "rows": c(np.concatenate([arr(v).reshape(-1) for v in (
            L1_cond_lin_b, L1_cond_weight, L1_cond_bias, L2_cond_b_o, L2_cond_b_f2, arr(L2_cond_b_c)[4 * D:], L0_cond_bu)])[None, :]),
        "w_qkv": tiles(wqkv),
        "w_o": tiles(arr(L2_cond_W_o).T),
        "w_f1": tiles(arr(L2_cond_W_f1).T),
        "w_f2": tiles(arr(L2_cond_W_f2).T),
        "w_up": tiles(arr(L3_cond_up_w).T),
        "w_down": tiles(arr(L3_cond_down_w).T),
    }
    nc = bacc.Bacc("TRN2", target_bir_lowering=False, num_devices=1)
    ins = [nc.dram_tensor(f"in_{n}", a.shape, mybir.dt.from_np(a.dtype), kind="ExternalInput").ap() for n, a in arrays.items()]
    out = nc.dram_tensor("out_y", (NB, L, D), F32, kind="ExternalOutput").ap()
    rows_scratch = nc.dram_tensor("rows_scratch", (NB, 5, D), F32, kind="Internal").ap()
    cur_scratch = nc.dram_tensor("cur_scratch", (NB, P, 2 * D), F32, kind="Internal").ap()
    qk_scratch = nc.dram_tensor("qk_scratch", (4, P, 2 * L), F32, kind="Internal").ap()
    cond_seq_kernel(nc, *ins, out, rows_scratch, cur_scratch, qk_scratch)
    r = run_bass_kernel_spmd(nc, [{f"in_{n}": a for n, a in arrays.items()}], core_ids=[0])
    return r.results[0]["out_y"]
```

```python
from contextlib import ExitStack

import concourse.bass as bass
from concourse import mybir

F32 = mybir.dt.float32
F32R = mybir.dt.float32r
BF16 = mybir.dt.bfloat16
ALU = mybir.AluOpType
ACT = mybir.ActivationFunctionType
AX = mybir.AxisListType

P = 128
NB = 16
L = 256
D = 256
BN = 128
HC = 64
NH = 16
DH = D // NH
FF = 1024
RT = L // P
KT = D // P
FT = FF // P
NCH = 16
CHC = BN * D // NCH
QTS = 4
HALF = 512
DELTA = 0.1
EPS_LN = 1e-5
EPS_RMS = 1e-6
Q_MIN = 1e-5
ROUND = 1.5 * 2.0 ** 23
KQ = 3 * DH
KM = KQ + 2

PE_A = ["down", "up", "ht", "q", "k", "v"]
PE_S = [f"s{u}" for u in range(NH)]
PE_M = [f"m{g}" for g in range(4)]
PE_T = [f"t{h}" for h in range(NH)]
PE_O = [f"o{h}" for h in range(NH)]
PE_C = ["ot", "proj", "ht", "f0", "f1", "f2", "f3", "y"]
PE_D = ["xt", "g0", "v0", "g1", "v1", "g2", "v2", "g3", "v3", "qt0", "y0", "qt1", "y1"]
ACT_A = ["relu", "ev0", "ev1", "hi", "qhi0", "qhi1", "khi0", "khi1", "v"]
ACT_T = [f"exp{h}" for h in range(NH)]
ACT_C = ["ot", "ev0", "ev1", "hi"] + [f"gelu{m}" for m in range(FT)]
ACT_D = ["sq0", "sq1", "ev0", "ev1", "hi", "gelu0", "gelu1", "gelu2", "gelu3", "qt0", "qt1"]
DVE_A = ["x0", "st0", "st1", "ag0", "ag1", "n0", "n1", "st2", "st3", "ag2", "ag3", "n2", "n3",
         "qlo0", "qlo1", "klo0", "klo1"]
DVE_S = [f"max{u}" for u in range(NH)]
DVE_M = [f"{part}{g}" for g in range(4) for part in ("hi", "lo")]
DVE_O = ["rec0", "norm0", "rec1", "norm1"]
DVE_C = ["gate1", "st0", "st1", "ag0", "ag1", "n0", "n1", "gate2"]
DVE_D = ["h0", "h1", "amax0", "step0", "inv0", "back0", "ra0", "rb0",
         "h2", "h3", "amax1", "step1", "inv1", "back1", "ra1", "rb1", "y0", "y1"]
POOL_A = ["xbu", "ve0", "rs0", "w2", "x1", "xr", "ve1", "rs1", "lo"]
POOL_C = ["x2", "xr", "ve", "rs", "lo", "x3"]
POOL_D = ["ve", "rs", "lo"]


def at(steps, name, b):
    return b * len(steps) + (steps.index(name) + 1)


ORDERS = {
  "full": {
    "SP": """
        C.ot B.m0 A.load B.m1 B.m2 B.m3 A.k D.y0 D.y1""".split(),
    "PE": """
        A.down B.s0 C.ot B.s1 A.up C.proj D.u0 B.s2 B.s3 D.u1 B.m0 C.ht B.s4 B.s5 D.u2 B.s6 B.s7 C.f0 C.f1 C.f2 A.ht B.m1
        C.f3 B.t0 B.s8 B.t1 D.u3 B.s9 A.q B.s10 B.o0 B.t2 B.s11 B.t3 B.o1 A.k B.t4 B.o2 B.m2 B.t5 B.o3 B.t6 B.s12 A.v B.o4
        B.o5 B.s13 B.t7 C.g0 B.s14 B.o6 B.t8 B.s15 B.t9 B.o7 B.m3 C.g1 D.qt0 B.t10 C.g2 B.o8 D.y0 D.qt1 B.o9 B.o10 B.t11
        B.t12 C.g3 B.t13 B.t14 B.o11 B.t15 B.o12 D.y1 B.o13 C.xt B.o14 B.o15""".split(),
    "ACT": """
        A.down C.ot D.u0 D.u1 C.ht D.u2 C.f0 C.f1 C.f2 A.ht B.t0 B.t1 C.f3 B.t2 B.t3 A.q B.t4 A.k B.t5 B.t6 D.u3 B.t7 B.t8
        B.t9 B.t10 D.qt0 B.t11 B.t12 A.v B.t13 D.qt1 B.t14 B.t15 C.xt""".split(),
    "DVE": """
        B.s0 A.up C.proj B.s1 A.lna C.ln D.u0 B.s2 B.s3 C.lnb B.m0 D.u1 A.ln B.s4 B.s5 D.quant0 B.s6 A.lnb B.s7 B.m1 D.u2
        B.s8 B.s9 B.s10 B.s11 A.q B.m2 A.k B.s12 D.u3 B.s13 B.s14 B.s15 B.o7 B.m3 D.quant1 D.y0 C.g3 D.y1 A.cur B.o15""".split(),
    "POOL": """
        A.down A.up C.proj C.ln A.lna C.ht A.ln A.ht C.g3 C.xt""".split(),
  },
  "one": {
    "SP": """
        B.m0 A.load B.m1 B.m2 B.m3 A.k""".split(),
    "PE": """
        A.down A.up B.s0 B.s1 B.s2 B.s3 B.m0 B.s4 B.s5 B.s6 B.s7 A.ht B.m1 B.t0 B.s8 B.t1 B.s9 A.q B.t2 B.s10 B.o0 B.t3
        B.s11 B.o1 A.k B.t4 B.m2 B.t5 B.o2 B.s12 B.o3 A.v B.t6 B.o4 B.s13 B.t7 B.o5 B.s14 B.o6 B.o7 B.s15 B.t8 B.m3 B.t9
        B.t10 B.o8 B.t11 B.o9 B.t12 B.o10 B.t13 B.t14 B.o11 B.t15 B.o12 B.o13 B.o14 B.o15""".split(),
    "ACT": """
        A.down A.ht B.t0 B.t1 A.q B.t2 B.t3 B.t4 A.k B.t5 A.v B.t6 B.t7 B.t8 B.t9 B.t10 B.t11 B.t12 B.t13 B.t14 B.t15""".split(),
    "DVE": """
        A.up B.s0 B.s1 A.lna B.s2 B.s3 B.m0 A.ln B.s4 B.s5 A.lnb B.s6 B.s7 B.m1 B.s8 B.s9 B.s10 B.s11 B.m2 A.q B.s12 A.k
        B.s13 B.s14 A.cur B.s15 B.o7 B.m3 B.o15""".split(),
    "POOL": """
        A.down A.up A.lna A.ln A.ht""".split(),
  },
  "two": {
    "SP": """
        C.ot B.m0 A.load B.m1 B.m2 B.m3 A.k""".split(),
    "PE": """
        A.down C.ot A.up C.proj B.s0 B.s1 B.s2 B.s3 B.m0 C.ht B.s4 B.s5 C.f0 B.s6 B.s7 C.f1 C.f2 A.ht B.m1 B.s8 C.f3 B.t0
        B.s9 A.q B.t1 B.t2 B.s10 B.o0 B.t3 B.s11 A.k B.m2 B.t4 B.o1 B.o2 B.o3 B.t5 B.s12 A.v B.t6 B.s13 B.o4 C.g0 B.o5 B.t7
        B.o6 B.s14 B.o7 B.t8 B.s15 C.g1 B.t9 B.m3 B.t10 B.o8 B.o9 C.g2 B.t11 B.t12 B.o10 B.o11 B.t13 C.g3 B.o12 B.o13 B.t14
        B.t15 C.xt B.o14 B.o15""".split(),
    "ACT": """
        A.down C.ot C.ht C.f0 C.f1 A.ht C.f2 C.f3 B.t0 B.t1 B.t2 B.t3 A.q B.t4 A.k B.t5 B.t6 A.v B.t7 B.t8 B.t9 B.t10 B.t11
        B.t12 B.t13 B.t14 B.t15 C.xt""".split(),
    "DVE": """
        A.up C.proj B.s0 B.s1 B.s2 C.ln A.lna B.s3 C.lnb B.m0 A.ln B.s4 B.s5 A.lnb B.s6 B.s7 B.m1 B.s8 B.s9 B.s10 B.s11 B.m2
        A.q A.k B.s12 B.s13 B.s14 A.cur B.o7 B.s15 B.m3 C.g3 B.o15""".split(),
    "POOL": """
        A.down A.up C.proj C.ln A.lna A.ln C.ht A.ht C.g3 C.xt""".split(),
  },
  "drain": {
    "SP": """
        C.ot B.m0 B.m1 B.m2 B.m3 D.y0 D.y1""".split(),
    "PE": """
        C.ot B.s0 C.proj B.s1 B.s2 D.u0 B.s3 D.u1 B.m0 B.s4 C.ht B.s5 D.u2 B.s6 B.s7 C.f0 C.f1 C.f2 C.f3 B.m1 B.t0 B.s8 D.u3
        B.s9 B.t1 B.o0 B.t2 B.s10 B.t3 B.o1 B.s11 B.m2 B.o2 B.t4 B.o3 B.t5 B.t6 B.s12 B.o4 B.s13 B.o5 B.t7 C.g0 B.s14 B.o6
        B.o7 B.s15 D.qt0 C.g1 B.t8 B.t9 B.m3 B.o8 B.t10 C.g2 D.y0 B.o9 B.t11 D.qt1 B.t12 B.o10 B.t13 B.o11 C.g3 B.o12 B.t14
        B.t15 B.o13 D.y1 B.o14 B.o15 C.xt""".split(),
    "ACT": """
        C.ot D.u0 D.u1 C.ht D.u2 C.f0 C.f1 C.f2 C.f3 B.t0 B.t1 B.t2 B.t3 B.t4 B.t5 D.u3 B.t6 B.t7 D.qt0 B.t8 B.t9 B.t10
        B.t11 D.qt1 B.t12 B.t13 B.t14 B.t15 C.xt""".split(),
    "DVE": """
        B.s0 C.proj B.s1 C.ln D.u0 C.lnb B.s2 B.s3 B.m0 B.s4 D.u1 B.s5 B.s6 D.quant0 B.s7 B.m1 D.u2 B.s8 B.s9 B.s10 B.s11
        B.m2 B.s12 B.s13 B.s14 D.u3 B.s15 B.o7 B.m3 D.quant1 D.y0 C.g3 D.y1 B.o15""".split(),
    "POOL": """
        C.proj C.ln C.ht C.g3 C.xt""".split(),
  },
}
OWN_ORDER = {1: "one", 2: "two", NB: "drain"}


def order(slices, a, b, c, d):
    on = {"A": a, "B": b, "C": c, "D": d}
    out = []
    for name in slices:
        what = name[2:].rstrip("0123456789")
        if on[name[0]]:
            out.append((name[0], what, int(name[2 + len(what):] or 0)))
    return out


def cond_seq_kernel(nc, xT, x, hyper, base, cols, k64, rows, w_qkv, w_o, w_f1, w_f2, w_up, w_down, out,
                    rows_scratch, cur_scratch, qk_scratch):
    ctx = ExitStack()
    with ctx:
        def sb(name, shape, dt):
            return ctx.enter_context(nc.sbuf_tensor(name, shape, dt))

        def sem(name):
            return ctx.enter_context(nc.semaphore(name))

        wqkv_hi = sb("wqkv_hi", [P, KT, 3 * D], F32R)
        wqkv_lo_at = nc.sbuf_base
        wqkv_lo = sb("wqkv_lo", [P, KT, 3 * D], F32R)
        wf1_hi = sb("wf1_hi", [P, KT, FF], F32R)
        wf1_lo_at = nc.sbuf_base
        wf1_lo = sb("wf1_lo", [P, KT, FF], F32R)
        wup_hi = sb("wup_hi", [P, KT, 2 * FF], F32R)
        wup_lo_at = nc.sbuf_base
        wup_lo = sb("wup_lo", [P, KT, 2 * FF], F32R)
        wo = sb("wo", [P, KT, D], F32)
        wf2 = sb("wf2", [P, FT, D], F32)
        wq3 = sb("wq3", [P, FT, D], BF16)
        small = sb("small", [P, 192], F32)
        ident = small[:, 0:128]
        bt1, bt2, bc_t = small[:, 128:130], small[:, 130:132], small[:, 132:144]
        bd, bq, bk, bv, bf1 = small[:, 144:145], small[:, 145:147], small[:, 147:149], small[:, 149:151], small[:, 151:159]
        identb = sb("identb", [P, P], BF16)
        bu_t = sb("bu_t", [P, D], F32)
        w2_t = sb("w2_t", [P, D], F32)
        base_c = sb("base_c", [P, 2 * D], F32)
        mod = sb("mod", [P, 8, NB], F32)
        scale3 = sb("scale3", [P, KT, NB], F32)
        wmean = sb("wmean", [P, 4], F32)
        half_neg = sb("half_neg", [P, RT], F32)
        eps_ln = sb("eps_ln", [P, RT], F32)
        eps_rms = sb("eps_rms", [P, RT], F32)
        Kp = sb("Kp", [P, 2, NH // 2, L], F32R)
        Va = sb("Va", [P, 2, RT, NH, DH + 1], F32)
        xT_t = sb("xT_t", [P, KT, L], F32)
        x_t = sb("x_t", [P, RT, D], F32)
        cur = sb("cur", [P, 2 * D], F32)
        tA = sb("tA", [P, 2, D], F32)
        stage_at = nc.sbuf_base
        Qp = sb("Qp", [P, 2, NH // 2, L], F32R)
        tC = sb("tC", [P, 3, D], F32)
        dn = sb("dn", [P, L], F32)
        x0 = sb("x0", [P, RT, D], F32)
        xr = sb("xr", [P, 2, RT, D], F32)
        hA = sb("hA", [P, KT, L], F32)
        hA_hi = sb("hA_hi", [P, KT, L], F32R)
        hA_lo = sb("hA_lo", [P, KT, L], F32R)
        q_hi = sb("q_hi", [P, 2, L], F32R)
        q_lo = sb("q_lo", [P, 2, L], F32R)
        k_hi = sb("k_hi", [P, 2, L], F32R)
        k_lo = sb("k_lo", [P, 2, L], F32R)
        stA = sb("stA", [P, RT, 6], F32)
        mvA = sb("mvA", [P, RT, 2], F32)
        rsA = sb("rsA", [P, 2, RT], F32)
        nmax = sb("nmax", [P, 2, 8], F32)
        m_hi = sb("m_hi", [8, 2, P], F32R)
        m_lo = sb("m_lo", [8, 2, P], F32R)
        Pr = sb("Pr", [P, 3, 2 * L], F32)
        rec = sb("rec", [P, RT, 8], F32)
        o_t = sb("o_t", [P, RT, D], F32)
        oT = sb("oT", [P, KT, L], F32)
        xc = sb("xc", [P, RT, D], F32)
        xcr = sb("xcr", [P, RT, D], F32)
        stC = sb("stC", [P, RT, 6], F32)
        mvC = sb("mvC", [P, RT, 2], F32)
        rsC = sb("rsC", [P, 2, RT], F32)
        hC = sb("hC", [P, KT, L], F32)
        hC_hi = sb("hC_hi", [P, KT, L], F32R)
        hC_lo = sb("hC_lo", [P, KT, L], F32R)
        G = sb("G", [P, FT, L], F32)
        x3 = sb("x3", [P, 2, RT, D], F32)
        hD = sb("hD", [P, KT, L], F32)
        hD_hi = sb("hD_hi", [P, KT, L], F32R)
        hD_lo = sb("hD_lo", [P, KT, L], F32R)
        sq = sb("sq", [P, D], F32)
        gl_at = nc.sbuf_base
        gl = sb("gl", [P, 2, HALF], F32)
        hd = sb("hd", [P, FF], F32)
        ssD = sb("ssD", [P, RT], F32)
        rsD = sb("rsD", [P, 2, RT], F32)
        am = sb("am", [P, RT, 4], F32)
        qi = sb("qi", [P, RT, FF], BF16)
        qT = sb("qT", [P, FT, P], BF16)
        ys = sb("ys", [P, RT, D], F32)

        def staged(name, shape, dt, words):
            nonlocal stage_at
            t = nc.alloc_sbuf_tensor_at(name, shape, dt, offset=stage_at)
            stage_at += 4 * words
            return t

        hyp = staged("hyp", [P, 4, CHC], F32, 4 * CHC)
        gen = staged("gen", [2 * NB, 4, CHC], F32, 4 * CHC)
        wc = staged("wc", [P, KT, 6 * D], F32, KT * 6 * D)
        base_t = staged("base_t", [P, 2, 2, D], F32, 4 * D)
        condbd = staged("condbd", [P, 2 * NB], F32, 2 * NB)
        c64 = staged("c64", [HC, NB + 3 * D], F32, NB + 3 * D)
        wt2 = staged("wt2", [P, KT, D], F32, KT * D)
        side = staged("side", [P, KT, NB], F32, KT * NB)
        zb = staged("zb", [P, 4, KT, NB], F32, 4 * KT * NB)
        s1 = staged("s1", [P, KT, NB], F32, KT * NB)
        s2 = staged("s2", [P, KT, NB], F32, KT * NB)
        assert stage_at <= nc.sbuf_base, (stage_at, nc.sbuf_base)
        row_t = nc.alloc_sbuf_tensor_at("row_t", [NB, 8 * D], F32, offset=wup_lo_at)
        tb = nc.alloc_sbuf_tensor_at("tb", [NB, 8, D], F32, offset=wup_lo_at + 32 * D)
        wqkv_raw = nc.alloc_sbuf_tensor_at("wqkv_raw", [P, KT * 3 * D], F32, offset=wqkv_lo_at)
        wf1_raw = nc.alloc_sbuf_tensor_at("wf1_raw", [P, KT * FF], F32, offset=wf1_lo_at)
        wup_raw = nc.alloc_sbuf_tensor_at("wup_raw", [P, KT * 2 * FF], F32, offset=wup_lo_at)
        wdn_raw = nc.alloc_sbuf_tensor_at("wdn_raw", [P, FT * D], F32, offset=gl_at)

        bank = [ctx.enter_context(nc.psum_tensor(f"bank{i}", [P, HALF], F32)) for i in range(8)]
        F_BANK = [bank[5], bank[1], bank[2], bank[5]]
        S_BANK = [bank[3 * (u % 2)] if u < 8 else bank[0] for u in range(NH)]

        pe_a, pe_s, pe_m, pe_t, pe_o, pe_c, pe_d = (sem(f"pe_{s}") for s in "asmtocd")
        act_a, act_t, act_c, act_d = (sem(f"act_{s}") for s in "atcd")
        dve_a, dve_s, dve_m, dve_o, dve_c, dve_d = (sem(f"dve_{s}") for s in "asmocd")
        pool_a, pool_c, pool_d = (sem(f"pool_{s}") for s in "acd")
        xT_in, x_in, cur_in, tA_in, tC_in = (sem(f"{s}_in") for s in ("xT", "x", "cur", "tA", "tC"))
        qh_out, ql_out, kh_out, kl_out = (sem(f"{s}_out") for s in ("qh", "ql", "kh", "kl"))
        qp_in, kp_in = sem("qp_in"), sem("kp_in")
        mx_in = [sem(f"mx_in{g}") for g in range(4)]
        y_out = [sem(f"y_out{r}") for r in range(RT)]
        hyp_in = [sem(f"hyp_in{i}") for i in range(4)]
        gen_out = [sem(f"gen_out{i}") for i in range(4)]
        hyp_mm, gen_act, gen_dve = sem("hyp_mm"), sem("gen_act"), sem("gen_dve")
        small_in, k64_in, side_in, row_in, wt2_in, wc_in, cond_in, base_in = (
            sem(f"{s}_in") for s in ("small", "k64", "side", "row", "wt2", "wc", "cond", "base"))
        wqkv_in, wo_in, wf1_in, wup_in, wf2_in, wdn_in = (sem(f"{s}_in") for s in ("wqkv", "wo", "wf1", "wup", "wf2", "wdn"))
        act_w, dve_w, pe_w, prep, zero = sem("act_w"), sem("dve_w"), sem("pe_w"), sem("prep"), sem("zero")
        cur_ready = sem("cur_ready")
        pre_pe, pre_act, ones_set = sem("pre_pe"), sem("pre_act"), sem("ones_set")
        rows_out, cond_clear = sem("rows_out"), sem("cond_clear")

        block = ctx.enter_context(nc.Block())

        PREP = ["z1", "d1", "r1", "s1", "z2a", "z2", "d2", "r2", "s2", "mod", "scale3", "tbl", "a12", "co",
                "tb1", "tb2", "c", "a1co", "a2bf", "w2", "identb"]
        PRE_PE = ["t1", "t2", "mod", "s3", "tb", "a12", "co"]
        ACT_W = ["qkv", "f1", "up"]
        DVE_W = ["base", "qkv", "f1", "up", "wabs", "mean", "inv", "wround", "wclip", "wq"]

        def turns(eng, body, engine, before={}):
            full = ORDERS["full"][engine]

            def alone(t):
                slices = order(ORDERS[OWN_ORDER.get(t, "full")][engine], t < NB, 1 <= t <= NB, 2 <= t <= NB + 1, t >= 3)
                if (t, None) in before:
                    before[t, None]()
                first = 0
                for k, one in enumerate(slices):
                    if (t, one) in before:
                        body(t, t % 2, slices[first:k])
                        before[t, one]()
                        first = k
                body(t, t % 2, slices[first:])

            for t in range(4):
                alone(t)
            with eng.Fori(4, NB - 2, 2) as t:
                body(t, 0, order(full, True, True, True, True))
                body(t + 1, 1, order(full, True, True, True, True))
            for t in range(NB - 2, NB + 3):
                alone(t)

        def past(eng, sem_, steps, name, b, back):
            if not isinstance(b, int) or b >= back:
                eng.wait_ge(sem_, at(steps, name, b - back))

        @block.sync
        def _(sp):
            def load_chunk(s):
                sp.dma_start(hyp[:, s, :], hyper[:, s * CHC:(s + 1) * CHC]).then_inc(hyp_in[s], 16)

            sp.dma_start(c64[:, :], k64).then_inc(k64_in, 16)
            load_chunk(0)
            sp.wait_ge(cond_clear, 1)
            sp.dma_start(condbd[0:HC, 0:NB], k64[:, 0:NB]).then_inc(cond_in, 16)
            sp.dma_start(condbd[HC:P, NB:2 * NB], k64[:, 0:NB]).then_inc(cond_in, 16)
            sp.dma_start(small[:, 0:192], cols[:, 0:192]).then_inc(small_in, 16)
            sp.dma_start(side[:, :, :].rearrange("p a b -> p (a b)"), cols[:, 192:224]).then_inc(side_in, 16)
            sp.dma_start(wt2[:, :, :].rearrange("p a b -> p (a b)"), cols[:, 224:736]).then_inc(wt2_in, 16)
            load_chunk(1)
            sp.dma_start(wc[:, :, :].rearrange("p k n -> p (k n)"), cols[:, 736:736 + KT * 6 * D]).then_inc(wc_in, 16)
            load_chunk(2)
            sp.dma_start(row_t[:, :], rows.to_broadcast([NB, 8 * D])).then_inc(row_in, 16)
            sp.dma_start(bu_t[:, :], rows[:, 7 * D:8 * D].to_broadcast([P, D])).then_inc(row_in, 16)
            sp.dma_start(w2_t[:, :], rows[:, D:2 * D].to_broadcast([P, D])).then_inc(row_in, 16)
            sp.dma_start(wo[:, :, :].rearrange("p k n -> p (k n)"), w_o).then_inc(wo_in, 16)
            load_chunk(3)

            cur_flat = cur_scratch.rearrange("s b p n -> (s b) (p n)")

            def generated(i, s):
                sp.wait_ge(gen_act, i * 8 + (2 * s + 2))
                sp.wait_ge(gen_dve, i * 8 + (2 * s + 2))
                sp.dma_start(cur_flat[:, bass.ds(i * (4 * CHC) + s * CHC, CHC)], gen[:, s, :]).then_inc(gen_out[s], 16)

            with sp.Fori(0, NCH // 4 - 1) as i:
                for s in range(4):
                    sp.wait_ge(hyp_mm, i * (4 * QTS) + QTS * (s + 1))
                    sp.dma_start(hyp[:, s, :], hyper[:, bass.ds((i + 1) * (4 * CHC) + s * CHC, CHC)]).then_inc(hyp_in[s], 16)
                    generated(i, s)
            sp.dma_start(base_t[:, :, :, :].rearrange("p a b c -> p (a b c)"), base).then_inc(base_in, 16)
            sp.wait_ge(prep, PREP.index("a2bf") + 1)
            sp.dma_start(rows_scratch, tb[:, 0:5, :]).then_inc(rows_out, 16)

            def load_rows(b):
                sp.dma_start(xT_t[:, :, :], xT[bass.ds(b, 1)].rearrange("o p a b -> (o p) a b")).then_inc(xT_in, 16)
                sp.dma_start(x_t[:, :, :], x[bass.ds(b, 1)].rearrange("o p a b -> (o p) a b")).then_inc(x_in, 16)

            def load_weights(b):
                sp.dma_start(cur[:, :].rearrange("p (s n) -> p s n", s=2),
                             cur_scratch[:, bass.ds(b, 1)].rearrange("s o p n -> (o p) s n")).then_inc(cur_in, 16)
                sp.dma_start(tA[:, :, :].rearrange("p a b -> p (a b)"),
                             rows_scratch[bass.ds(b, 1), 0:2, :].rearrange("o a b -> o (a b)").to_broadcast([P, 2 * D])).then_inc(tA_in, 16)

            load_rows(0)
            for s in range(4):
                generated(NCH // 4 - 1, s)
            sp.wait_ge(rows_out, 16)
            for s in range(4):
                sp.wait_ge(gen_out[s], 16 * (NCH // 4))
            load_weights(0)
            sp.dma_start(wqkv_raw[:, :], w_qkv).then_inc(wqkv_in, 16)
            sp.wait_ge(prep, len(PREP))
            sp.dma_start(wf1_raw[:, :], w_f1).then_inc(wf1_in, 16)
            sp.dma_start(wup_raw[:, :], w_up).then_inc(wup_in, 16)

            def late_weights():
                sp.dma_start(wf2[:, :, :].rearrange("p k n -> p (k n)"), w_f2).then_inc(wf2_in, 16)
                sp.dma_start(wdn_raw[:, :], w_down).then_inc(wdn_in, 16)

            def turn(t, par, slices):
                a, b, c = t, t - 1, t - 2
                index = lambda v: v if isinstance(v, int) else sp.snap(v)
                upcoming, gated, stored = index(t + 1), index(t - 2), index(t - 3)
                value = lambda v: v if isinstance(v, int) else sp.to_reg(v)
                xT_used, x_read, x_used = value(at(PE_A, "up", a)), value(at(POOL_A, "xr", a)), value(at(DVE_A, "x0", a))
                for stage, what, n in slices:
                    if (stage, what) == ("A", "k"):
                        for parts, ready_hi, ready_lo, outs, w in (
                                ((q_hi, q_lo), "qhi1", "qlo1", (qh_out, ql_out), 0),
                                ((k_hi, k_lo), "khi1", "klo1", (kh_out, kl_out), 2)):
                            sp.wait_ge(act_a, at(ACT_A, ready_hi, a))
                            sp.dma_start(qk_scratch[w], parts[0][:, :, :].rearrange("p a b -> p (a b)").bitcast(F32)).then_inc(outs[0], 16)
                            sp.wait_ge(dve_a, at(DVE_A, ready_lo, a))
                            sp.dma_start(qk_scratch[w + 1], parts[1][:, :, :].rearrange("p a b -> p (a b)").bitcast(F32)).then_inc(outs[1], 16)
                        for outs, dst, srcs, arrived in (((qh_out, ql_out), Qp, (0, 0, 1), qp_in), ((kh_out, kl_out), Kp, (2, 3, 2), kp_in)):
                            sp.wait_ge(outs[0], 16 * a + 16)
                            sp.wait_ge(outs[1], 16 * a + 16)
                            if not isinstance(a, int) or a >= 2:
                                sp.wait_ge(pe_t, at(PE_T, "t15", a - 2))
                            for half in range(2):
                                for r, w in enumerate(srcs):
                                    sp.dma_start(
                                        dst[64 * half + DH * r:64 * half + DH * (r + 1), par, :, :].rearrange("d (j c) n -> d j (c n)", j=4).bitcast(F32),
                                        qk_scratch[w, 64 * half:64 * half + 64, :].rearrange("(j d) n -> d j n", j=4)).then_inc(arrived, 16)
                    elif (stage, what) == ("B", "m"):
                        sp.wait_ge(dve_m, at(DVE_M, f"lo{n}", b))
                        for half in range(2):
                            for row, part in ((KQ, m_hi), (KQ + 1, m_lo)):
                                src = part[4 * half:4 * half + 4, n % 2, :]
                                sp.dma_start(Qp[64 * half + row:64 * half + row + 1, 1 - par, 2 * n:2 * n + 2, :].bitcast(F32),
                                             src.bitcast(F32)).then_inc(mx_in[n], 16)
                    elif (stage, what) == ("A", "load"):
                        if not isinstance(t, int) or t + 1 < NB:
                            sp.wait_ge(pe_a, xT_used)
                            sp.wait_ge(pool_a, x_read)
                            sp.wait_ge(dve_a, x_used)
                            load_weights(upcoming)
                            load_rows(upcoming)
                    elif (stage, what) == ("C", "ot"):
                        past(sp, dve_c, DVE_C, "gate2", c, 1)
                        past(sp, pool_c, POOL_C, "xr", c, 1)
                        sp.dma_start(tC[:, :, :].rearrange("p a b -> p (a b)"),
                                     rows_scratch[bass.ds(gated, 1), 2:5, :].rearrange("o a b -> o (a b)").to_broadcast([P, 3 * D])).then_inc(tC_in, 16)
                    elif (stage, what) == ("D", "y"):
                        sp.wait_ge(dve_d, at(DVE_D, f"y{n}", t - 3))
                        sp.dma_start(out[bass.ds(stored, 1), n * P:(n + 1) * P, :].rearrange("o p n -> (o p) n"), ys[:, n, :]).then_inc(y_out[n], 16)

            turns(sp, turn, "SP", {(1, None): late_weights})
            for r in range(RT):
                sp.wait_ge(y_out[r], 16 * NB)

        @block.tensor
        def _(pe):
            def three(dst, lhs, rhs, first, last):
                for i, (l, r) in enumerate(((lhs[0], rhs[0]), (lhs[1], rhs[0]), (lhs[0], rhs[1]))):
                    mm = pe.matmul(dst, l, r, start=first and i == 0, stop=last and i == 2)
                return mm

            def generate(i, s):
                pe.wait_ge(hyp_in[s], i * 16 + 16)
                for q in range(QTS):
                    if not isinstance(i, int) or i or s:
                        pe.wait_ge(gen_act if q % 2 == 0 else gen_dve, i * 8 + (2 * s + q // 2 - 1))
                    pe.matmul(bank[q][0:2 * NB, :], condbd[:, :], hyp[:, s, q * HALF:(q + 1) * HALF], start=True, stop=True).then_inc(hyp_mm, 1)

            pe.wait_ge(k64_in, 16)
            for m in range(KT):
                mm = pe.matmul(bank[4][:, m * NB:(m + 1) * NB], c64[:, NB + m * P:NB + (m + 1) * P], c64[:, 0:NB], start=True, stop=True)
            mm.then_inc(pre_pe, 1)
            pe.wait_ge(cond_in, 32)
            generate(0, 0)
            pe.wait_ge(wt2_in, 16)
            pe.wait_ge(prep, PREP.index("s1") + 1)
            for m in range(KT):
                for k in range(KT):
                    mm = pe.matmul(bank[5][:, m * NB:(m + 1) * NB], wt2[:, k, m * P:(m + 1) * P], s1[:, k, :], start=k == 0, stop=k == KT - 1)
            mm.then_inc(pre_pe, 1)
            generate(0, 1)
            pe.wait_ge(wc_in, 16)
            pe.wait_ge(prep, PREP.index("s2") + 1)
            for m in range(8):
                for k in range(KT):
                    mm = pe.matmul(bank[6][:, m * NB:(m + 1) * NB], wc[:, k, m * P:(m + 1) * P], s2[:, k, :], start=k == 0, stop=k == KT - 1)
            mm.then_inc(pre_pe, 1)
            for m in range(KT):
                mm = pe.matmul(bank[7][:, m * NB:(m + 1) * NB], c64[:, NB + 2 * D + m * P:NB + 2 * D + (m + 1) * P], c64[:, 0:NB], start=True, stop=True)
            mm.then_inc(pre_pe, 1)
            pe.matmul(bank[4][0:NB, 0:D], c64[:, 0:NB], c64[:, NB + D:NB + 2 * D], start=True, stop=True).then_inc(pre_pe, 1)
            for k in range(KT):
                mm = pe.matmul(bank[5][0:NB, 0:2 * D], s2[:, k, :], wc[:, k, 4 * D:6 * D], start=k == 0, stop=k == KT - 1)
            mm.then_inc(pre_pe, 1)
            generate(0, 2)
            pe.wait_ge(wo_in, 16)
            pe.wait_ge(small_in, 16)
            pe.wait_ge(prep, PREP.index("mod") + 1)
            for k in range(KT):
                mm = pe.matmul(bank[6][0:NB, 0:D], bv[:, k:k + 1].to_broadcast([P, NB]), wo[:, k, :], start=k == 0, stop=k == KT - 1)
            mm.then_inc(pre_pe, 1)
            generate(0, 3)
            with pe.Fori(1, NCH // 4) as i:
                for s in range(4):
                    generate(i, s)
            pe.wait_ge(prep, len(PREP))

            def with_qkv():
                pe.wait_ge(dve_w, at(DVE_W, "qkv", 0))

            def with_f1():
                pe.wait_ge(dve_w, at(DVE_W, "f1", 0))
                pe.wait_ge(wf2_in, 16)
                pe.wait_ge(dve_w, at(DVE_W, "wabs", 0))
                pe.wait_ge(ones_set, 1)
                pe.matmul(bank[7][:, 0:1], wmean[:, 3:4].to_broadcast([P, P]), wmean[:, 2:3], start=True, stop=True).then_inc(pe_w, 1)

            def with_up():
                pe.wait_ge(dve_w, len(DVE_W))

            def turn(t, par, slices):
                a, b, c, d = t, t - 1, t - 2, t - 3
                with_c = any(s[0] == "C" for s in slices)

                def a_down():
                    pe.wait_ge(xT_in, 16 * a + 16)
                    pe.wait_ge(cur_ready, a + 1)
                    past(pe, act_a, ACT_A, "v", a, 1)
                    for k in range(KT):
                        mm = pe.matmul(bank[4][:, 0:L], cur[:, k * BN:(k + 1) * BN], xT_t[:, k, :], start=k == 0, stop=k == KT - 1)
                    mm.then_inc(pe_a, 1)

                def a_up():
                    pe.wait_ge(act_a, at(ACT_A, "relu", a))
                    for r in range(RT):
                        mm = pe.matmul(bank[4][:, r * D:(r + 1) * D], dn[:, r * P:(r + 1) * P], cur[:, D:2 * D], start=True, stop=True)
                    mm.then_inc(pe_a, 1)

                def a_ht():
                    pe.wait_ge(dve_a, at(DVE_A, "n3", a))
                    for k in range(KT):
                        for r in range(RT):
                            mm = pe.transpose(bank[4][:, k * L + r * P:k * L + (r + 1) * P], x0[:, r, k * P:(k + 1) * P], ident)
                    mm.then_inc(pe_a, 1)

                def a_q():
                    pe.wait_ge(pool_a, at(POOL_A, "lo", a))
                    for m in range(2):
                        for k in range(KT):
                            mm = three(bank[4][:, m * L:(m + 1) * L], (wqkv_hi[:, k, m * P:(m + 1) * P], wqkv_lo[:, k, m * P:(m + 1) * P]),
                                       (hA_hi[:, k, :], hA_lo[:, k, :]), k == 0, k == KT - 1)
                    mm.then_inc(pe_a, 1)

                def a_k():
                    if with_c:
                        pe.wait_ge(act_c, at(ACT_C, "gelu7", c))
                    else:
                        past(pe, dve_a, DVE_A, "klo1", a, 1)
                    for m in range(2):
                        for k in range(KT):
                            mm = three(bank[5][:, m * L:(m + 1) * L], (wqkv_hi[:, k, D + m * P:D + (m + 1) * P], wqkv_lo[:, k, D + m * P:D + (m + 1) * P]),
                                       (hA_hi[:, k, :], hA_lo[:, k, :]), k == 0, k == KT - 1)
                    mm.then_inc(pe_a, 1)

                def a_v():
                    pe.wait_ge(dve_a, at(DVE_A, "qlo1", a))
                    for r in range(RT):
                        for k in range(KT):
                            mm = three(bank[4][:, r * D:(r + 1) * D], (hA_hi[:, k, r * P:(r + 1) * P], hA_lo[:, k, r * P:(r + 1) * P]),
                                       (wqkv_hi[:, k, 2 * D:3 * D], wqkv_lo[:, k, 2 * D:3 * D]), k == 0, k == KT - 1)
                    mm.then_inc(pe_a, 1)

                def b_s(u):
                    lo, g = 64 * (u % 2), u // 2
                    if u == 0:
                        pe.wait_ge(qp_in, 96 * b + 96)
                        pe.wait_ge(kp_in, 96 * b + 96)
                        past(pe, dve_m, DVE_M, "lo3", b, 1)
                    elif u == 1:
                        past(pe, dve_o, DVE_O, "norm1", b, 1)
                    elif u % 4 == 0:
                        pe.wait_ge(dve_m, at(DVE_M, f"lo{u // 4 - 1}", b))
                    else:
                        pe.wait_ge(dve_s, at(DVE_S, f"max{u - 2 if u < 8 else u - 1}", b))
                    for r in range(RT):
                        mm = pe.matmul(S_BANK[u][:, r * L:(r + 1) * L], Qp[lo:lo + KQ, 1 - par, g, r * P:(r + 1) * P],
                                       Kp[lo:lo + KQ, 1 - par, g, :], start=True, stop=True)
                    mm.then_inc(pe_s, 1)

                def b_m(g):
                    pe.wait_ge(dve_s, at(DVE_S, f"max{4 * g + 3}", b))
                    pe.transpose(bank[0][0:8, 0:P], nmax[:, g % 2, :], ident).then_inc(pe_m, 1)

                def b_t(h):
                    lo, g = 64 * (h % 2), h // 2
                    dst = bank[1 + h % 2]
                    if h % 4 == 0:
                        pe.wait_ge(mx_in[h // 4], 64 * b + 64)
                    if h >= 2:
                        pe.wait_ge(act_t, at(ACT_T, f"exp{h - 2}", b))
                    elif with_c:
                        pe.wait_ge(act_c, at(ACT_C, f"gelu{3 + 2 * h}", c))
                    else:
                        past(pe, act_t, ACT_T, f"exp{h + 14}", b, 1)
                    for k in range(RT):
                        mm = pe.matmul(dst[:, k * L:(k + 1) * L], Kp[lo:lo + KM, 1 - par, g, k * P:(k + 1) * P],
                                       Qp[lo:lo + KM, 1 - par, g, :], start=True, stop=True)
                    mm.then_inc(pe_t, 1)

                def b_o(h):
                    if h == 0:
                        pe.wait_ge(act_a, at(ACT_A, "v", b))
                        pe.wait_ge(dve_s, at(DVE_S, "max7", b))
                    if h == 8:
                        pe.wait_ge(dve_o, at(DVE_O, "norm0", b))
                    pe.wait_ge(act_t, at(ACT_T, f"exp{h}", b))
                    for r in range(RT):
                        for k in range(RT):
                            col = (r * 8 + h % 8) * (DH + 1)
                            mm = pe.matmul(bank[3][:, col:col + DH + 1], Pr[:, h % 3, k * L + r * P:k * L + (r + 1) * P],
                                           Va[:, 1 - par, k, h, :], start=k == 0, stop=k == RT - 1)
                    mm.then_inc(pe_o, 1)

                def c_ot():
                    pe.wait_ge(dve_o, at(DVE_O, "norm1", c))
                    past(pe, dve_c, DVE_C, "gate2", c, 1)
                    if isinstance(c, int) and c == 0:
                        pe.wait_ge(dve_a, at(DVE_A, "klo1", a - 1))
                    for k in range(KT):
                        for r in range(RT):
                            mm = pe.transpose(bank[5][:, k * L + r * P:k * L + (r + 1) * P], o_t[:, r, k * P:(k + 1) * P], ident)
                    mm.then_inc(pe_c, 1)

                def c_proj():
                    pe.wait_ge(act_c, at(ACT_C, "ot", c))
                    for r in range(RT):
                        for k in range(KT):
                            mm = pe.matmul(bank[5][:, r * D:(r + 1) * D], oT[:, k, r * P:(r + 1) * P], wo[:, k, :], start=k == 0, stop=k == KT - 1)
                    mm.then_inc(pe_c, 1)

                def c_ht():
                    pe.wait_ge(dve_c, at(DVE_C, "n1", c))
                    for k in range(KT):
                        for r in range(RT):
                            mm = pe.transpose(bank[5][:, k * L + r * P:k * L + (r + 1) * P], xc[:, r, k * P:(k + 1) * P], ident)
                    mm.then_inc(pe_c, 1)

                def c_f(n):
                    if n == 0:
                        pe.wait_ge(pool_c, at(POOL_C, "lo", c))
                    if n == 3:
                        pe.wait_ge(act_c, at(ACT_C, "gelu1", c))
                    for m in (2 * n, 2 * n + 1):
                        for k in range(KT):
                            mm = three(F_BANK[n][:, (m % 2) * L:(m % 2 + 1) * L], (wf1_hi[:, k, m * P:(m + 1) * P], wf1_lo[:, k, m * P:(m + 1) * P]),
                                       (hC_hi[:, k, :], hC_lo[:, k, :]), k == 0, k == KT - 1)
                    mm.then_inc(pe_c, 1)

                def c_g(n):
                    r = n // 2
                    if n == 0:
                        pe.wait_ge(act_c, at(ACT_C, "gelu7", c))
                        if not isinstance(a, int) or a < NB:
                            pe.wait_ge(dve_a, at(DVE_A, "klo1", a))
                    for k in range(4 * (n % 2), 4 * (n % 2) + 4):
                        mm = pe.matmul(bank[5][:, r * D:(r + 1) * D], G[:, k, r * P:(r + 1) * P], wf2[:, k, :], start=k == 0, stop=k == FT - 1)
                    if n == 3:
                        mm.then_inc(pe_c, 1)

                def c_xt():
                    pe.wait_ge(pool_c, at(POOL_C, "x3", c))
                    past(pe, dve_d, DVE_D, "y1", c, 1)
                    for k in range(KT):
                        for r in range(RT):
                            mm = pe.transpose(bank[6][:, k * L + r * P:k * L + (r + 1) * P], x3[:, par, r, k * P:(k + 1) * P], ident)
                    mm.then_inc(pe_d, 1)

                def d_u(n):
                    r, col = n // 2, (n % 2) * HALF
                    if n == 0:
                        pe.wait_ge(pool_d, at(POOL_D, "lo", d))
                    else:
                        pe.wait_ge(act_d, at(ACT_D, f"gelu{n - 1}", d))
                    lhs = [(hD_hi[:, k, r * P:(r + 1) * P], hD_lo[:, k, r * P:(r + 1) * P]) for k in range(KT)]
                    for k in range(KT):
                        c0 = FF + col
                        mm = three(bank[6][:, :], lhs[k], (wup_hi[:, k, c0:c0 + HALF], wup_lo[:, k, c0:c0 + HALF]), k == 0, k == KT - 1)
                    mm.then_inc(pe_d, 1)
                    if n == 0:
                        past(pe, act_d, ACT_D, "qt1", d, 1)
                    else:
                        pe.wait_ge(dve_d, at(DVE_D, f"h{n - 1}", d))
                    for k in range(KT):
                        mm = three(bank[7][:, :], lhs[k], (wup_hi[:, k, col:col + HALF], wup_lo[:, k, col:col + HALF]), k == 0, k == KT - 1)
                    mm.then_inc(pe_d, 1)

                def d_qt(r):
                    pe.wait_ge(dve_d, at(DVE_D, "h3" if r == 0 else "rb1", d))
                    if r == 1:
                        pe.wait_ge(act_d, at(ACT_D, "qt0", d))
                    for k in range(FT):
                        mm = pe.transpose(bank[7][:, :].bitcast(BF16)[:, k * P:(k + 1) * P], qi[:, r, k * P:(k + 1) * P], identb[:, :])
                    mm.then_inc(pe_d, 1)

                def d_y(r):
                    pe.wait_ge(act_d, at(ACT_D, f"qt{r}", d))
                    if r == 1:
                        pe.wait_ge(dve_d, at(DVE_D, "y0", d))
                    for k in range(FT):
                        mm = pe.matmul(bank[6][:, 0:D], qT[:, k, :], wq3[:, k, :], start=k == 0, stop=k == FT - 1)
                    mm.then_inc(pe_d, 1)

                for stage, what, n in slices:
                    if stage == "A" and what in ("down", "up", "ht", "q", "k", "v"):
                        {"down": a_down, "up": a_up, "ht": a_ht, "q": a_q, "k": a_k, "v": a_v}[what]()
                    elif stage == "B":
                        {"s": b_s, "m": b_m, "t": b_t, "o": b_o}[what](n)
                    elif stage == "C" and what in ("ot", "proj", "ht", "xt"):
                        {"ot": c_ot, "proj": c_proj, "ht": c_ht, "xt": c_xt}[what]()
                    elif stage == "C" and what in ("f", "g"):
                        {"f": c_f, "g": c_g}[what](n)
                    elif stage == "D" and what in ("u", "qt", "y"):
                        {"u": d_u, "qt": d_qt, "y": d_y}[what](n)

            turns(pe, turn, "PE", {(0, ("A", "q", 0)): with_qkv, (2, None): with_f1, (3, None): with_up})

        @block.scalar
        def _(act):
            def generated(i, s):
                if not isinstance(i, int):
                    act.wait_ge(gen_out[s], i * 16)
                for q in (0, 2):
                    act.wait_ge(hyp_mm, i * (4 * QTS) + (QTS * s + q + 1))
                    act.activation(gen[:, s, q * HALF:(q + 1) * HALF], bank[q][0:2 * NB, :], ACT.Copy).then_inc(gen_act, 1)

            act.wait_ge(prep, PREP.index("z1") + 1)
            act.activation(zb[:, 1], zb[:, 0], ACT.Exp, scale=-1.0).then_inc(pre_act, 1)
            generated(0, 0)
            act.wait_ge(prep, PREP.index("z2") + 1)
            act.activation(zb[:, 3], zb[:, 2], ACT.Exp, scale=-1.0).then_inc(pre_act, 1)
            generated(0, 1)
            generated(0, 2)
            act.wait_ge(prep, PREP.index("tbl") + 1)
            act.activation(tb[:, 6, :], tb[:, 5, :], ACT.Tanh).then_inc(pre_act, 1)
            generated(0, 3)

            def high_part(hi, raw, arrived):
                act.wait_ge(arrived, 16)
                act.activation(hi[:, :, :].rearrange("p k n -> p (k n)"), raw[:, :], ACT.Copy).then_inc(act_w, 1)

            with act.Fori(1, NCH // 4) as i:
                for s in range(4):
                    generated(i, s)
            act.wait_ge(rows_out, 16)
            act.wait_ge(prep, len(PREP))
            for s in range(4):
                act.wait_ge(gen_out[s], 16 * (NCH // 4))

            def qkv_weights():
                high_part(wqkv_hi, wqkv_raw, wqkv_in)

            def late_weights():
                high_part(wf1_hi, wf1_raw, wf1_in)
                high_part(wup_hi, wup_raw, wup_in)

            def turn(t, par, slices):
                a, b, c, d = t, t - 1, t - 2, t - 3

                def a_down():
                    act.wait_ge(pe_a, at(PE_A, "down", a))
                    past(act, pe_a, PE_A, "up", a, 1)
                    act.activation(dn[:, :], bank[4][:, 0:L], ACT.Relu, bias=bd).then_inc(act_a, 1)

                def modulate(dst, src, first, batch, sem_):
                    for k in range(KT):
                        act.activation(dst[:, k, :], src[:, k * L:(k + 1) * L], ACT.Identity, scale=mod[:, first + k, bass.ds(batch, 1)],
                                       bias=mod[:, first + 2 + k, bass.ds(batch, 1)]).then_inc(sem_, 1)

                def a_ht():
                    act.wait_ge(pe_a, at(PE_A, "ht", a))
                    past(act, pool_a, POOL_A, "lo", a, 1)
                    modulate(hA, bank[4], 0, a, act_a)
                    act.wait_ge(act_a, at(ACT_A, "ev1", a))
                    past(act, pe_a, PE_A, "v", a, 1)
                    act.activation(hA_hi[:, :, :], hA[:, :, :], ACT.Copy).then_inc(act_a, 1)

                def a_parts(what, src, dst, bias, outs):
                    act.wait_ge(pe_a, at(PE_A, what, a))
                    if not isinstance(a, int) or a >= 1:
                        act.wait_ge(outs, 16 * a)
                    for m in range(2):
                        act.activation(dst[:, m, :], src[:, m * L:(m + 1) * L], ACT.Identity, bias=bias[:, m:m + 1]).then_inc(act_a, 1)

                def a_v():
                    act.wait_ge(pe_a, at(PE_A, "v", a))
                    past(act, pe_o, PE_O, "o15", a, 2)
                    act.activation(Va[:, par, :, :, 0:DH], bank[4][:, :].rearrange("p (r h e) -> p r h e", r=RT, h=NH),
                                   ACT.Copy).then_inc(act_a, 1)

                def b_t(h):
                    act.wait_ge(pe_t, at(PE_T, f"t{h}", b))
                    if h >= 3:
                        act.wait_ge(pe_o, at(PE_O, f"o{h - 3}", b))
                    else:
                        past(act, pe_o, PE_O, "o15", b, 1)
                    act.activation(Pr[:, h % 3, :], bank[1 + h % 2][:, :], ACT.Exp, scale=DH ** -0.5).then_inc(act_t, 1)

                def c_ot():
                    act.wait_ge(pe_c, at(PE_C, "ot", c))
                    past(act, pe_c, PE_C, "proj", c, 1)
                    act.activation(oT[:, :, :].rearrange("p k n -> p (k n)"), bank[5][:, :], ACT.Copy).then_inc(act_c, 1)

                def c_ht():
                    act.wait_ge(pe_c, at(PE_C, "ht", c))
                    past(act, pool_c, POOL_C, "lo", c, 1)
                    modulate(hC, bank[5], 4, c, act_c)
                    act.wait_ge(act_c, at(ACT_C, "ev1", c))
                    past(act, pe_c, PE_C, "f3", c, 1)
                    act.activation(hC_hi[:, :, :], hC[:, :, :], ACT.Copy).then_inc(act_c, 1)

                def c_f(n):
                    act.wait_ge(pe_c, at(PE_C, f"f{n}", c))
                    past(act, pe_c, PE_C, "y", c, 1)
                    for m in (2 * n, 2 * n + 1):
                        act.activation(G[:, m, :], F_BANK[n][:, (m % 2) * L:(m % 2 + 1) * L], ACT.Gelu_apprx_tanh,
                                       bias=bf1[:, m:m + 1]).then_inc(act_c, 1)

                def c_xt():
                    act.wait_ge(pool_c, at(POOL_C, "x3", c))
                    for r in range(RT):
                        if r:
                            act.wait_ge(act_d, at(ACT_D, "sq0", c))
                        else:
                            past(act, pool_d, POOL_D, "ve", c, 1)
                            past(act, act_d, ACT_D, "sq1", c, 1)
                        act.activation(sq[:, :], x3[:, par, r, :], ACT.Square, scale=D ** -0.5, accum_out=ssD[:, r:r + 1]).then_inc(act_d, 1)
                    act.wait_ge(pe_d, at(PE_D, "xt", c))
                    past(act, pool_d, POOL_D, "lo", c, 1)
                    for k in range(KT):
                        act.activation(hD[:, k, :], bank[6][:, k * L:(k + 1) * L], ACT.Copy, scale=scale3[:, k, bass.ds(c, 1)]).then_inc(act_d, 1)
                    act.wait_ge(act_d, at(ACT_D, "ev1", c))
                    past(act, pe_d, PE_D, "v3", c, 1)
                    act.activation(hD_hi[:, :, :], hD[:, :, :], ACT.Copy).then_inc(act_d, 1)

                def d_u(n):
                    act.wait_ge(pe_d, at(PE_D, f"g{n}", d))
                    if n == 0:
                        act.wait_ge(pool_d, at(POOL_D, "rs", d))
                    if n >= 2:
                        act.wait_ge(dve_d, at(DVE_D, f"h{n - 2}", d))
                    else:
                        past(act, dve_d, DVE_D, f"h{n + 2}", d, 1)
                    act.activation(gl[:, n % 2, :], bank[6][:, :], ACT.Gelu, scale=rsD[:, 1, n // 2:n // 2 + 1]).then_inc(act_d, 1)

                def d_qt(r):
                    act.wait_ge(pe_d, at(PE_D, f"qt{r}", d))
                    if r:
                        act.wait_ge(pe_d, at(PE_D, "y0", d))
                    else:
                        past(act, pe_d, PE_D, "y1", d, 1)
                    act.activation(qT[:, :, :].rearrange("p k n -> p (k n)"), bank[7][:, :].bitcast(BF16), ACT.Copy).then_inc(act_d, 1)

                for stage, what, n in slices:
                    if stage == "A":
                        if what == "down":
                            a_down()
                        elif what == "ht":
                            a_ht()
                        elif what == "q":
                            a_parts("q", bank[4], q_hi, bq, qh_out)
                        elif what == "k":
                            a_parts("k", bank[5], k_hi, bk, kh_out)
                        elif what == "v":
                            a_v()
                    elif stage == "B" and what == "t":
                        b_t(n)
                    elif stage == "C":
                        if what == "ot":
                            c_ot()
                        elif what == "ht":
                            c_ht()
                        elif what == "f":
                            c_f(n)
                        elif what == "xt":
                            c_xt()
                    elif stage == "D":
                        if what == "u":
                            d_u(n)
                        elif what == "qt":
                            d_qt(n)

            turns(act, turn, "ACT", {(0, ("A", "ht", 0)): qkv_weights, (1, None): late_weights})

        @block.vector
        def _(dve):
            def bcast(col, n):
                return col.unsqueeze(2).to_broadcast([P, col.shape[1], n])

            def z(i):
                return zb[:, i]

            done = [0]

            def step(ins):
                ins.then_inc(prep, 1)
                done[0] += 1

            def after_last():
                dve.wait_ge(prep, done[0])

            def generated(i, s):
                if not isinstance(i, int):
                    dve.wait_ge(gen_out[s], i * 16)
                for q in (1, 3):
                    dve.wait_ge(hyp_mm, i * (4 * QTS) + (QTS * s + q + 1))
                    dve.tensor_copy(gen[:, s, q * HALF:(q + 1) * HALF], bank[q][0:2 * NB, :]).then_inc(gen_dve, 1)

            mm4 = bank[4][:, 0:KT * NB].rearrange("p (k n) -> p k n", k=KT)
            mm5 = bank[5][:, 0:KT * NB].rearrange("p (k n) -> p k n", k=KT)
            dve.wait_ge(small_in, 16)
            dve.wait_ge(pre_pe, 1)
            step(dve.tensor_tensor(z(0), mm4, bcast(bt1, NB), ALU.add))
            dve.wait_ge(pre_act, 1)
            step(dve.tensor_scalar(z(1), z(1), 1.0, None, ALU.add))
            after_last()
            step(dve.reciprocal(z(1), z(1)))
            after_last()
            step(dve.tensor_tensor(s1[:, :, :], z(0), z(1), ALU.mult))
            generated(0, 0)
            dve.wait_ge(pre_pe, 2)
            step(dve.tensor_tensor(z(2), mm5, bcast(bt2, NB), ALU.add))
            dve.wait_ge(side_in, 16)
            after_last()
            step(dve.tensor_tensor(z(2), z(2), side[:, :, :], ALU.add))
            dve.wait_ge(pre_act, 2)
            step(dve.tensor_scalar(z(3), z(3), 1.0, None, ALU.add))
            after_last()
            step(dve.reciprocal(z(3), z(3)))
            after_last()
            step(dve.tensor_tensor(s2[:, :, :], z(2), z(3), ALU.mult))
            generated(0, 1)
            dve.wait_ge(pre_pe, 3)
            step(dve.tensor_tensor(mod[:, :, :], bank[6][:, 0:8 * NB].rearrange("p (k n) -> p k n", k=8), bcast(bc_t[:, 0:8], NB), ALU.add))
            dve.wait_ge(pre_pe, 4)
            step(dve.tensor_scalar(scale3[:, :, :].rearrange("p k n -> p (k n)"), bank[7][:, 0:KT * NB], 1.0, None, ALU.add))
            lin_b, w, bias, b_o, b_f2 = (row_t[0:NB, i * D:(i + 1) * D] for i in range(5))
            dve.wait_ge(row_in, 48)
            dve.wait_ge(pre_pe, 5)
            step(dve.tensor_tensor(tb[:, 5, :], bank[4][0:NB, 0:D], lin_b, ALU.add))
            dve.wait_ge(pre_pe, 6)
            step(dve.tensor_tensor(tb[:, 2:4, :].rearrange("p a b -> p (a b)"), bank[5][0:NB, :], row_t[0:NB, 5 * D:7 * D], ALU.add))
            generated(0, 2)
            dve.wait_ge(pre_pe, 7)
            step(dve.tensor_tensor(tb[:, 7, :], bank[6][0:NB, 0:D], b_o, ALU.add))
            generated(0, 3)
            dve.wait_ge(pre_act, 3)
            step(dve.tensor_tensor(tb[:, 5, :], tb[:, 6, :], bias, ALU.add))
            after_last()
            step(dve.tensor_tensor(tb[:, 5, :], tb[:, 5, :], w, ALU.mult))
            after_last()
            step(dve.tensor_tensor(tb[:, 0, :], tb[:, 5, :], bias, ALU.add))
            step(dve.tensor_tensor(tb[:, 1, :], tb[:, 7, :], tb[:, 2, :], ALU.mult))
            step(dve.tensor_tensor(tb[:, 4, :], tb[:, 3, :], b_f2, ALU.mult))
            step(dve.tensor_tensor(w2_t[:, :], w2_t[:, :], w2_t[:, :], ALU.mult))
            step(dve.tensor_copy(identb[:, :], ident))
            assert done[0] == len(PREP)

            with dve.Fori(1, NCH // 4) as i:
                for s in range(4):
                    generated(i, s)

            def low_part(hi, lo, raw, step_):
                dve.wait_ge(act_w, at(ACT_W, step_, 0))
                dve.tensor_tensor(lo[:, :, :].rearrange("p k n -> p (k n)"), raw[:, :],
                                  hi[:, :, :].rearrange("p k n -> p (k n)").bitcast(F32), ALU.subtract).then_inc(dve_w, 1)

            dve.wait_ge(base_in, 16)
            dve.scalar_tensor_tensor(base_c[:, :], base_t[:, 1].rearrange("p a b -> p (a b)"), DELTA,
                                     base_t[:, 0].rearrange("p a b -> p (a b)"), ALU.mult, ALU.add).then_inc(dve_w, 1)
            dve.wait_ge(prep, len(PREP))
            dve.wait_ge(rows_out, 16)
            for s in range(4):
                dve.wait_ge(gen_out[s], 16 * (NCH // 4))

            def combine(b):
                dve.wait_ge(cur_in, 16 * b + 16)
                dve.wait_ge(dve_w, at(DVE_W, "base", 0))
                dve.scalar_tensor_tensor(cur[:, :], cur[:, :], DELTA, base_c[:, :], ALU.mult, ALU.add).then_inc(cur_ready, 1)

            combine(0)
            dwn = wdn_raw[:, :]

            def qkv_weights():
                low_part(wqkv_hi, wqkv_lo, wqkv_raw, "qkv")

            def late_weights():
                low_part(wf1_hi, wf1_lo, wf1_raw, "f1")
                low_part(wup_hi, wup_lo, wup_raw, "up")
                dve.wait_ge(wdn_in, 16)
                dve.tensor_reduce(wmean[:, 2:3], dwn, AX.X, ALU.add, apply_absolute_value=True).then_inc(dve_w, 1)

            def ternary():
                dve.wait_ge(pe_w, 1)
                dve.tensor_scalar(wmean[:, 0:1], bank[7][:, 0:1], 1.0 / (D * FF), Q_MIN, ALU.mult, ALU.max).then_inc(dve_w, 1)
                dve.wait_ge(dve_w, at(DVE_W, "mean", 0))
                dve.reciprocal(wmean[:, 1:2], wmean[:, 0:1]).then_inc(dve_w, 1)
                dve.wait_ge(dve_w, at(DVE_W, "inv", 0))
                dve.tensor_scalar(dwn, dwn, wmean[:, 1:2], ROUND, ALU.mult, ALU.add).then_inc(dve_w, 1)
                dve.wait_ge(dve_w, at(DVE_W, "wround", 0))
                dve.tensor_scalar(dwn, dwn, -ROUND, 1.0, ALU.add, ALU.min).then_inc(dve_w, 1)
                dve.wait_ge(dve_w, at(DVE_W, "wclip", 0))
                dve.tensor_scalar(wq3[:, :, :].rearrange("p k n -> p (k n)"), dwn, -1.0, None, ALU.max).then_inc(dve_w, 1)

            def turn(t, par, slices):
                a, b, c, d = t, t - 1, t - 2, t - 3

                def stats(src, st, mv, sem_, steps, names, batch):
                    values = [at(steps, names[r], batch) for r in range(RT)]
                    values = [v if isinstance(v, int) else dve.to_reg(v) for v in values]
                    for r in range(RT):
                        dve.bn_stats(st[:, r, :], src[:, r, :]).then_inc(sem_, 1)
                    for r in range(RT):
                        dve.wait_ge(prep, len(PREP))
                        dve.wait_ge(sem_, values[r])
                        dve.bn_aggr(mv[:, r, :], st[:, r, :]).then_inc(sem_, 1)

                def normalise(buf, mv, rs, sem_):
                    for r in range(RT):
                        dve.tensor_scalar(buf[:, r, :], buf[:, r, :], mv[:, r, 0:1], rs[:, 1, r:r + 1],
                                          ALU.subtract, ALU.mult).then_inc(sem_, 1)

                def a_up():
                    dve.wait_ge(pe_a, at(PE_A, "up", a))
                    dve.wait_ge(pool_a, at(POOL_A, "xbu", a))
                    past(dve, pe_a, PE_A, "ht", a, 1)
                    past(dve, pool_a, POOL_A, "rs1", a, 1)
                    dve.tensor_tensor(x0[:, :, :].rearrange("p r n -> p (r n)"), bank[4][:, :],
                                      x_t[:, :, :].rearrange("p r n -> p (r n)"), ALU.add).then_inc(dve_a, 1)
                    dve.wait_ge(dve_a, at(DVE_A, "x0", a))
                    stats(x0, stA, mvA, dve_a, DVE_A, ("st0", "st1"), a)

                def a_n0():
                    dve.wait_ge(pool_a, at(POOL_A, "rs0", a))
                    normalise(x0, mvA, rsA, dve_a)

                def a_ln():
                    dve.wait_ge(pool_a, at(POOL_A, "x1", a))
                    stats(x0, stA, mvA, dve_a, DVE_A, ("st2", "st3"), a)

                def a_n1():
                    dve.wait_ge(pool_a, at(POOL_A, "rs1", a))
                    normalise(x0, mvA, rsA, dve_a)

                def a_parts(what, src, hi, lo, bias, outs):
                    dve.wait_ge(act_a, at(ACT_A, f"{what}hi1", a))
                    if not isinstance(a, int) or a >= 1:
                        dve.wait_ge(outs, 16 * a)
                    for m in range(2):
                        dve.scalar_tensor_tensor(lo[:, m, :], src[:, m * L:(m + 1) * L], bias[:, m:m + 1], hi[:, m, :].bitcast(F32),
                                                 ALU.add, ALU.subtract).then_inc(dve_a, 1)

                def b_s(u):
                    col = 4 * (u % 2) + 2 * ((u % 4) // 2)
                    dve.wait_ge(pe_s, at(PE_S, f"s{u}", b))
                    if u % 4 == 0:
                        if u >= 8:
                            dve.wait_ge(pe_m, at(PE_M, f"m{u // 4 - 2}", b))
                        else:
                            past(dve, pe_m, PE_M, f"m{u // 4 + 2}", b, 1)
                    dve.tensor_reduce(nmax[:, (u // 4) % 2, col:col + 2], S_BANK[u][:, :].rearrange("p (r n) -> p r n", r=RT),
                                      AX.X, ALU.max, negate=True).then_inc(dve_s, 1)

                def b_m(g):
                    dve.wait_ge(pe_m, at(PE_M, f"m{g}", b))
                    if g >= 2:
                        dve.wait_ge(mx_in[g - 2], 64 * b + 64)
                    elif not isinstance(b, int) or b >= 1:
                        dve.wait_ge(mx_in[g + 2], 64 * b)
                    dve.tensor_copy(m_hi[:, g % 2, :], bank[0][0:8, 0:P]).then_inc(dve_m, 1)
                    dve.wait_ge(dve_m, at(DVE_M, f"hi{g}", b))
                    dve.tensor_tensor(m_lo[:, g % 2, :], bank[0][0:8, 0:P], m_hi[:, g % 2, :].bitcast(F32), ALU.subtract).then_inc(dve_m, 1)

                def b_o(h):
                    if h % 8 != 7:
                        return
                    n = h // 8
                    dve.wait_ge(pe_o, at(PE_O, f"o{h}", b))
                    if n:
                        dve.wait_ge(dve_o, at(DVE_O, "norm0", b))
                    else:
                        past(dve, dve_o, DVE_O, "norm1", b, 1)
                        past(dve, pe_c, PE_C, "ot", b, 1)
                    acc = bank[3][:, 0:RT * 8 * (DH + 1)].rearrange("p (h e) -> p h e", e=DH + 1)
                    dve.reciprocal(rec[:, :, :].rearrange("p r h -> p (r h)").unsqueeze(2), acc[:, :, DH:DH + 1]).then_inc(dve_o, 1)
                    dve.wait_ge(dve_o, at(DVE_O, f"rec{n}", b))
                    dve.tensor_tensor(o_t[:, :, n * P:(n + 1) * P].rearrange("p r (h e) -> p r h e", e=DH),
                                      acc[:, :, 0:DH].rearrange("p (r h) e -> p r h e", r=RT),
                                      rec[:, :, :].unsqueeze(3).to_broadcast([P, RT, 8, DH]), ALU.mult).then_inc(dve_o, 1)

                def over_rows(row):
                    return row.unsqueeze(1).to_broadcast([P, RT, D])

                def c_proj():
                    dve.wait_ge(pe_c, at(PE_C, "proj", c))
                    dve.wait_ge(tC_in, 16 * c + 16)
                    past(dve, pe_c, PE_C, "ht", c, 1)
                    past(dve, pool_c, POOL_C, "rs", c, 1)
                    dve.tensor_tensor(xc[:, :, :], bank[5][:, :].rearrange("p (r n) -> p r n", r=RT), over_rows(tC[:, 0, :]),
                                      ALU.mult).then_inc(dve_c, 1)

                def c_ln():
                    dve.wait_ge(pool_c, at(POOL_C, "x2", c))
                    stats(xc, stC, mvC, dve_c, DVE_C, ("st0", "st1"), c)

                def c_n1():
                    dve.wait_ge(pool_c, at(POOL_C, "rs", c))
                    dve.wait_ge(pool_c, at(POOL_C, "xr", c))
                    normalise(xc, mvC, rsC, dve_c)

                def c_g(n):
                    if n != 3:
                        return
                    dve.wait_ge(pe_c, at(PE_C, "y", c))
                    past(dve, dve_d, DVE_D, "y1", c, 2)
                    dve.tensor_tensor(x3[:, par, :, :], bank[5][:, :].rearrange("p (r n) -> p r n", r=RT), over_rows(tC[:, 1, :]),
                                      ALU.mult).then_inc(dve_c, 1)

                def d_u(n):
                    dve.wait_ge(pe_d, at(PE_D, f"v{n}", d))
                    dve.wait_ge(act_d, at(ACT_D, f"gelu{n}", d))
                    if n == 2:
                        dve.wait_ge(dve_d, at(DVE_D, "rb0", d))
                    elif n == 0:
                        past(dve, dve_d, DVE_D, "rb1", d, 1)
                    dve.scalar_tensor_tensor(hd[:, (n % 2) * HALF:(n % 2 + 1) * HALF], bank[7][:, :], rsD[:, 1, n // 2:n // 2 + 1],
                                             gl[:, n % 2, :], ALU.mult, ALU.mult).then_inc(dve_d, 1)

                def d_quant(r):
                    top, size, inv, back = (am[:, r, i:i + 1] for i in range(4))
                    dve.wait_ge(dve_d, at(DVE_D, f"h{2 * r + 1}", d))
                    dve.tensor_reduce(top, hd[:, :], AX.X, ALU.max, apply_absolute_value=True).then_inc(dve_d, 1)
                    dve.wait_ge(dve_d, at(DVE_D, f"amax{r}", d))
                    dve.tensor_scalar(size, top, Q_MIN, 1.0 / 127.0, ALU.max, ALU.mult).then_inc(dve_d, 1)
                    dve.wait_ge(dve_d, at(DVE_D, f"step{r}", d))
                    dve.reciprocal(inv, size).then_inc(dve_d, 1)
                    dve.tensor_tensor(back, size, wmean[:, 0:1], ALU.mult).then_inc(dve_d, 1)
                    dve.wait_ge(dve_d, at(DVE_D, f"inv{r}", d))
                    dve.tensor_scalar(hd[:, :], hd[:, :], inv, ROUND, ALU.mult, ALU.add).then_inc(dve_d, 1)
                    dve.wait_ge(dve_d, at(DVE_D, f"ra{r}", d))
                    past(dve, pe_d, PE_D, f"qt{r}", d, 1)
                    dve.tensor_scalar(qi[:, r, :], hd[:, :], -ROUND, 127.0, ALU.add, ALU.min).then_inc(dve_d, 1)

                def d_y(r):
                    dve.wait_ge(pe_d, at(PE_D, f"y{r}", d))
                    dve.wait_ge(dve_d, at(DVE_D, f"back{r}", d))
                    if not isinstance(d, int) or d >= 1:
                        dve.wait_ge(y_out[r], 16 * d)
                    dve.scalar_tensor_tensor(ys[:, r, :], bank[6][:, 0:D], am[:, r, 3:4], x3[:, 1 - par, r, :], ALU.mult, ALU.add).then_inc(dve_d, 1)

                for stage, what, n in slices:
                    if stage == "A":
                        if what == "up":
                            a_up()
                        elif what == "lna":
                            a_n0()
                        elif what == "ln":
                            a_ln()
                        elif what == "lnb":
                            a_n1()
                        elif what == "cur":
                            if not isinstance(t, int) or t + 1 < NB:
                                combine(t + 1)
                        elif what == "q":
                            a_parts("q", bank[4], q_hi, q_lo, bq, ql_out)
                        elif what == "k":
                            a_parts("k", bank[5], k_hi, k_lo, bk, kl_out)
                    elif stage == "B":
                        if what == "s":
                            b_s(n)
                        elif what == "m":
                            b_m(n)
                        elif what == "o":
                            b_o(n)
                    elif stage == "C":
                        if what == "proj":
                            c_proj()
                        elif what == "ln":
                            c_ln()
                        elif what == "lnb":
                            c_n1()
                        elif what == "g":
                            c_g(n)
                    else:
                        if what == "u":
                            d_u(n)
                        elif what == "quant":
                            d_quant(n)
                        elif what == "y":
                            d_y(n)

            turns(dve, turn, "DVE", {(0, ("A", "ln", 0)): qkv_weights, (1, ("B", "o", 15)): late_weights, (2, ("B", "o", 15)): ternary})

        @block.gpsimd
        def _(pool):
            pool.memset(condbd[:, :], 0.0).then_inc(cond_clear, 1)
            pool.memset(wmean[:, 3:4], 1.0).then_inc(ones_set, 1)
            pool.memset(half_neg[:, :], -0.5).then_inc(zero, 1)
            pool.memset(eps_ln[:, :], EPS_LN).then_inc(zero, 1)
            pool.memset(eps_rms[:, :], EPS_RMS).then_inc(zero, 1)
            for n, lo in enumerate((32, 96)):
                pool.wait_ge(zero, 3 + n)
                pool.memset(Kp[lo:lo + 32, :, :, :].bitcast(F32), 1.0).then_inc(zero, 1)
            pool.wait_ge(zero, 5)
            pool.memset(Va[:, :, :, :, DH:DH + 1], 1.0).then_inc(zero, 1)
            pool.wait_ge(prep, len(PREP))
            pool.wait_ge(rows_out, 16)
            for s in range(4):
                pool.wait_ge(gen_out[s], 16 * (NCH // 4))
            pool.wait_ge(zero, 6)

            def turn(t, par, slices):
                a, b, c, d = t, t - 1, t - 2, t - 3

                def rstd(src, rs, eps, sem_, steps, names, batch):
                    pool.tensor_tensor(rs[:, 0, :], src, eps[:, :], ALU.add).then_inc(sem_, 1)
                    pool.wait_ge(sem_, at(steps, names, batch))
                    pool.tensor_tensor(rs[:, 1, :], rs[:, 0, :], half_neg[:, :], ALU.pow).then_inc(sem_, 1)

                def over_rows(row):
                    return row.unsqueeze(1).to_broadcast([P, RT, D])

                def a_down():
                    pool.wait_ge(x_in, 16 * a + 16)
                    pool.tensor_tensor(x_t[:, :, :], x_t[:, :, :], over_rows(bu_t[:, :]), ALU.add).then_inc(pool_a, 1)

                def a_up():
                    pool.wait_ge(dve_a, at(DVE_A, "ag1", a))
                    past(pool, dve_a, DVE_A, "n3", a, 1)
                    rstd(mvA[:, :, 1], rsA, eps_ln, pool_a, POOL_A, "ve0", a)

                def a_n0():
                    pool.wait_ge(dve_a, at(DVE_A, "n1", a))
                    pool.tensor_tensor(x0[:, :, :], x0[:, :, :], over_rows(w2_t[:, :]), ALU.mult).then_inc(pool_a, 1)
                    pool.wait_ge(pool_a, at(POOL_A, "w2", a))
                    pool.wait_ge(tA_in, 16 * a + 16)
                    pool.tensor_tensor(x0[:, :, :], x0[:, :, :], over_rows(tA[:, 0, :]), ALU.add).then_inc(pool_a, 1)
                    pool.wait_ge(pool_a, at(POOL_A, "x1", a))
                    past(pool, pool_c, POOL_C, "x2", a, 2)
                    pool.tensor_tensor(xr[:, par, :, :], x0[:, :, :], over_rows(tA[:, 1, :]), ALU.add).then_inc(pool_a, 1)

                def a_ln():
                    pool.wait_ge(dve_a, at(DVE_A, "ag3", a))
                    rstd(mvA[:, :, 1], rsA, eps_ln, pool_a, POOL_A, "ve1", a)

                def low_part(lo, full, hi, sem_):
                    pool.tensor_tensor(lo[:, :, :], full[:, :, :], hi[:, :, :].bitcast(F32), ALU.subtract).then_inc(sem_, 1)

                def a_ht():
                    pool.wait_ge(act_a, at(ACT_A, "hi", a))
                    past(pool, pe_a, PE_A, "v", a, 1)
                    low_part(hA_lo, hA, hA_hi, pool_a)

                def c_ht():
                    pool.wait_ge(act_c, at(ACT_C, "hi", c))
                    past(pool, pe_c, PE_C, "f3", c, 1)
                    low_part(hC_lo, hC, hC_hi, pool_c)

                def c_proj():
                    pool.wait_ge(dve_c, at(DVE_C, "gate1", c))
                    pool.tensor_tensor(xc[:, :, :], xc[:, :, :], xr[:, par, :, :], ALU.add).then_inc(pool_c, 1)
                    pool.wait_ge(pool_c, at(POOL_C, "x2", c))
                    pool.wait_ge(tC_in, 16 * c + 16)
                    past(pool, pool_c, POOL_C, "x3", c, 1)
                    pool.tensor_tensor(xcr[:, :, :], xc[:, :, :], over_rows(tC[:, 2, :]), ALU.add).then_inc(pool_c, 1)

                def c_ln():
                    pool.wait_ge(dve_c, at(DVE_C, "ag1", c))
                    past(pool, dve_c, DVE_C, "n1", c, 1)
                    rstd(mvC[:, :, 1], rsC, eps_ln, pool_c, POOL_C, "ve", c)

                def c_g(n):
                    if n == 3:
                        pool.wait_ge(dve_c, at(DVE_C, "gate2", c))
                        pool.tensor_tensor(x3[:, par, :, :], x3[:, par, :, :], xcr[:, :, :], ALU.add).then_inc(pool_c, 1)

                def c_xt():
                    pool.wait_ge(act_d, at(ACT_D, "sq1", c))
                    past(pool, act_d, ACT_D, "gelu3", c, 1)
                    past(pool, dve_d, DVE_D, "h3", c, 1)
                    rstd(ssD[:, :], rsD, eps_rms, pool_d, POOL_D, "ve", c)
                    pool.wait_ge(act_d, at(ACT_D, "hi", c))
                    past(pool, pe_d, PE_D, "v3", c, 1)
                    low_part(hD_lo, hD, hD_hi, pool_d)

                for stage, what, n in slices:
                    if stage == "A":
                        if what == "down":
                            a_down()
                        elif what == "up":
                            a_up()
                        elif what == "lna":
                            a_n0()
                        elif what == "ln":
                            a_ln()
                        elif what == "ht":
                            a_ht()
                    elif stage == "C":
                        if what == "proj":
                            c_proj()
                        elif what == "ln":
                            c_ln()
                        elif what == "ht":
                            c_ht()
                        elif what == "g":
                            c_g(n)
                        elif what == "xt":
                            c_xt()

            turns(pool, turn, "POOL")


def kernel(x, cond_256, fside_BxS_0, L0_cond_Wd, L0_cond_bd, L0_cond_Wu, L0_cond_bu, L0_cond_Wdd, L0_cond_bdd, L0_cond_Wdu,
           L0_cond_bdu, L1_cond_weight, L1_cond_bias, L1_cond_lin_w, L1_cond_lin_b, L2_cond_W_t1, L2_cond_b_t1, L2_cond_W_t2,
           L2_cond_b_t2, L2_cond_W_c, L2_cond_b_c, L2_cond_W_qkv, L2_cond_b_qkv, L2_cond_W_o, L2_cond_b_o, L2_cond_W_f1,
           L2_cond_b_f1, L2_cond_W_f2, L2_cond_b_f2, L3_cond_norm_w, L3_cond_up_w, L3_cond_down_w):
    import numpy as np
    import concourse.bacc as bacc
    from concourse.bass_utils import run_bass_kernel_spmd

    c = np.ascontiguousarray
    arr = np.asarray
    x = arr(x)

    def tiles(w):
        return c(w.reshape(-1, P, w.shape[1]).transpose(1, 0, 2).reshape(P, -1))

    def col(v):
        return v.reshape(-1, P).T

    heads = np.arange(D).reshape(4, 2, 2, DH).transpose(1, 2, 0, 3).reshape(-1)
    wqkv = arr(L2_cond_W_qkv).T
    bqkv = arr(L2_cond_b_qkv)
    wqkv = np.concatenate([wqkv[:, 0:D][:, heads], wqkv[:, D:2 * D][:, heads], wqkv[:, 2 * D:]], 1)
    wd, bdd = arr(L0_cond_Wd), arr(L0_cond_bdd).reshape(BN, D)
    wu, bdu = arr(L0_cond_Wu), arr(L0_cond_bdu).reshape(D, BN)

    def by_part(w):
        return np.moveaxis(w.reshape(-1, BN, KT, P), (1, 2, 3), (3, 2, 1)).reshape(-1, P, KT * BN)

    arrays = {
        "xT": c(x.reshape(NB, L, KT, P).transpose(0, 3, 2, 1)),
        "x": c(x.reshape(NB, RT, P, D).transpose(0, 2, 1, 3)),
        "hyper": c(np.concatenate([by_part(arr(L0_cond_Wdd).T).reshape(HC, -1),
                                   arr(L0_cond_Wdu).T.reshape(HC, D, BN).transpose(0, 2, 1).reshape(HC, -1)], 0)),
        "base": c(np.concatenate([by_part(wd)[0], wu.T, by_part(bdd)[0], bdu.T], 1)),
        "cols": c(np.concatenate([
            np.eye(P, dtype=np.float32), col(arr(L2_cond_b_t1)), col(arr(L2_cond_b_t2)), col(arr(L2_cond_b_c)),
            col(arr(L0_cond_bd)), col(bqkv[0:D][heads]), col(bqkv[D:2 * D][heads]), col(bqkv[2 * D:]), col(arr(L2_cond_b_f1)),
            np.zeros((P, 192 - 159), np.float32), tiles(arr(fside_BxS_0).T), tiles(arr(L2_cond_W_t2).T),
            tiles(arr(L2_cond_W_c).T)], 1)),
        "k64": c(np.concatenate([arr(cond_256).T, arr(L2_cond_W_t1).T, arr(L1_cond_lin_w).T, arr(L3_cond_norm_w).T], 1)),
        "rows": c(np.concatenate([arr(v).reshape(-1) for v in (
            L1_cond_lin_b, L1_cond_weight, L1_cond_bias, L2_cond_b_o, L2_cond_b_f2, arr(L2_cond_b_c)[4 * D:], L0_cond_bu)])[None, :]),
        "w_qkv": tiles(wqkv),
        "w_o": tiles(arr(L2_cond_W_o).T),
        "w_f1": tiles(arr(L2_cond_W_f1).T),
        "w_f2": tiles(arr(L2_cond_W_f2).T),
        "w_up": tiles(arr(L3_cond_up_w).T),
        "w_down": tiles(arr(L3_cond_down_w).T),
    }
    nc = bacc.Bacc("TRN2", target_bir_lowering=False, num_devices=1)
    ins = [nc.dram_tensor(f"in_{n}", a.shape, mybir.dt.from_np(a.dtype), kind="ExternalInput").ap() for n, a in arrays.items()]
    out = nc.dram_tensor("out_y", (NB, L, D), F32, kind="ExternalOutput").ap()
    rows_scratch = nc.dram_tensor("rows_scratch", (NB, 5, D), F32, kind="Internal").ap()
    cur_scratch = nc.dram_tensor("cur_scratch", (2, NB, P, D), F32, kind="Internal").ap()
    qk_scratch = nc.dram_tensor("qk_scratch", (4, P, 2 * L), F32, kind="Internal").ap()
    cond_seq_kernel(nc, *ins, out, rows_scratch, cur_scratch, qk_scratch)
    r = run_bass_kernel_spmd(nc, [{f"in_{n}": a for n, a in arrays.items()}], core_ids=[0])
    return r.results[0]["out_y"]
```
